# Optimizing a Trainium2 kernel written in Bass

```python
import numpy as np
import jax
import jax.numpy as jnp

def _softmax(x, axis=-1):
    return jax.nn.softmax(x, axis=axis)

def _gelu(x):
    return jax.nn.gelu(x, approximate=True)

def _silu(x):
    return jax.nn.silu(x)

def _sigmoid(x):
    return jax.nn.sigmoid(x)

def _layernorm(x, axis=-1, eps=1e-05):
    m = jnp.mean(x, axis=axis, keepdims=True)
    v = jnp.var(x, axis=axis, keepdims=True)
    return (x - m) / jnp.sqrt(v + eps)

def _scatter_add(tgt, idx, src, axis=0):
    return tgt.at[idx].add(src)

def _segment_sum(src, seg, n):
    return jax.ops.segment_sum(src, seg, n)
kernel_name = 'mk_prb_d1_jaxref_r2_1eebad'

def setup_inputs(seed: int=0):
    np.random.seed(seed)
    _w = jnp.asarray

    def _L0_attn_setup():
        import jax, jax.numpy as jnp
        import numpy as np
        N_HEADS = 16
        SEG = 64
        EPS = 1e-06

        def _sigma(x):
            return jax.nn.elu(x) + 1.0

        def _infini_attention(x, W_q, W_k, W_v, W_o, beta_param):
            B, T, D = x.shape
            H = N_HEADS
            dk = D // H
            assert T % SEG == 0
            S = T // SEG

            def proj(W):
                y = (x @ W.T).reshape(B, T, H, dk).transpose(0, 2, 1, 3)
                return y.reshape(B, H, S, SEG, dk).transpose(2, 0, 1, 3, 4)
            Qs, Ks, Vs = (proj(W_q), proj(W_k), proj(W_v))
            beta = jax.nn.sigmoid(beta_param).reshape(1, H, 1, 1)
            causal = jnp.triu(jnp.ones((SEG, SEG), dtype=bool), k=1)
            inv_sqrt_dk = 1.0 / jnp.sqrt(jnp.asarray(dk, x.dtype))
            M0 = jnp.zeros((B, H, dk, dk), dtype=x.dtype)
            z0 = jnp.zeros((B, H, dk), dtype=x.dtype)

            def step(carry, qkv):
                M, z = carry
                q, k, v = qkv
                sq = _sigma(q)
                denom_q = jnp.sum(sq * z[:, :, None, :], axis=-1, keepdims=True) + EPS
                A_mem = jnp.matmul(sq, M) / denom_q
                scores = jnp.matmul(q, jnp.swapaxes(k, -2, -1)) * inv_sqrt_dk
                scores = jnp.where(causal, -jnp.inf, scores)
                A_dot = jnp.matmul(jax.nn.softmax(scores, axis=-1), v)
                A_s = beta * A_mem + (1.0 - beta) * A_dot
                sk = _sigma(k)
                denom_k = jnp.sum(sk * z[:, :, None, :], axis=-1, keepdims=True) + EPS
                V_prev = jnp.matmul(sk, M) / denom_k
                M_new = M + jnp.einsum('bhtk,bhtv->bhkv', sk, v - V_prev)
                z_new = z + jnp.sum(sk, axis=-2)
                return ((M_new, z_new), A_s)
            (M, z), outs = jax.lax.scan(step, (M0, z0), (Qs, Ks, Vs))
            out = outs.transpose(1, 3, 0, 2, 4).reshape(B, S * SEG, H, dk)
            out = outs.transpose(1, 2, 0, 3, 4).reshape(B, H, T, dk)
            out = out.transpose(0, 2, 1, 3).reshape(B, T, D)
            out = out @ W_o.T
            return (out, M.mean(0), z.mean(0))

        def _reference_tuple_inner(x, W_q, W_k, W_v, W_o, beta_param):
            return _infini_attention(x, W_q, W_k, W_v, W_o, beta_param)
        key = jax.random.key(seed)
        kx, kq, kk, kv, ko = jax.random.split(key, 5)
        B, T, D = (4, 2048, 512)
        scale = D ** (-0.5)
        return {'x': jax.random.normal(kx, (B, T, D), dtype=jnp.float32), 'W_q': jax.random.normal(kq, (D, D), dtype=jnp.float32) * scale, 'W_k': jax.random.normal(kk, (D, D), dtype=jnp.float32) * scale, 'W_v': jax.random.normal(kv, (D, D), dtype=jnp.float32) * scale, 'W_o': jax.random.normal(ko, (D, D), dtype=jnp.float32) * scale, 'beta_param': jnp.zeros((N_HEADS,), dtype=jnp.float32)}
    _L0_attn_in = _L0_attn_setup()

    def _L0_ffn_setup():
        import jax, jax.numpy as jnp
        import numpy as np
        B, S, D, H, F = (4, 2048, 512, 16, 2048)
        CAP = 0.125
        ROPE_BASE = 10000.0

        def rmsnorm(x, g):
            return x * jax.lax.rsqrt(jnp.mean(x * x, -1, keepdims=True) + 1e-06) * g

        def rope(t, pos):
            hd = t.shape[-1]
            inv = 1.0 / ROPE_BASE ** (jnp.arange(0, hd, 2, dtype=jnp.float32) / hd)
            f = pos[:, None, :, None].astype(jnp.float32) * inv
            emb = jnp.concatenate([f, f], axis=-1)
            cos, sin = (jnp.cos(emb), jnp.sin(emb))
            rot = jnp.concatenate([-t[..., hd // 2:], t[..., :hd // 2]], axis=-1)
            return t * cos + rot * sin
        key = jax.random.key(seed)
        ks = jax.random.split(key, 9)
        scale = 0.02
        x = jax.random.normal(ks[0], (B, S, D), jnp.float32)
        causal = jnp.where(jnp.tril(jnp.ones((S, S), bool)), 0.0, -1000000000.0).astype(jnp.float32)
        attention_mask = jnp.broadcast_to(causal[None, None], (B, 1, S, S))
        position_ids = jnp.broadcast_to(jnp.arange(S, dtype=jnp.int32), (B, S))
        return {'x': x, 'attention_mask': attention_mask, 'position_ids': position_ids, 'router_w': jax.random.normal(ks[1], (D, 1), jnp.float32) * scale, 'router_b': jnp.zeros((1,), jnp.float32), 'wq': jax.random.normal(ks[2], (D, D), jnp.float32) * scale, 'wk': jax.random.normal(ks[3], (D, D), jnp.float32) * scale, 'wv': jax.random.normal(ks[4], (D, D), jnp.float32) * scale, 'wo': jax.random.normal(ks[5], (D, D), jnp.float32) * scale, 'w1': jax.random.normal(ks[6], (D, F), jnp.float32) * scale, 'w2': jax.random.normal(ks[7], (F, D), jnp.float32) * scale, 'ln1': jnp.ones((D,), jnp.float32), 'ln2': jnp.ones((D,), jnp.float32)}
    _L0_ffn_in = _L0_ffn_setup()
    _d = {'L0_attn_x': _L0_attn_in['x'], 'L0_attn_W_q': _L0_attn_in['W_q'], 'L0_attn_W_k': _L0_attn_in['W_k'], 'L0_attn_W_v': _L0_attn_in['W_v'], 'L0_attn_W_o': _L0_attn_in['W_o'], 'L0_attn_beta_param': _L0_attn_in['beta_param'], 'L0_ffn_attention_mask': _L0_ffn_in['attention_mask'], 'L0_ffn_position_ids': _L0_ffn_in['position_ids'], 'L0_ffn_router_w': _L0_ffn_in['router_w'], 'L0_ffn_router_b': _L0_ffn_in['router_b'], 'L0_ffn_wq': _L0_ffn_in['wq'], 'L0_ffn_wk': _L0_ffn_in['wk'], 'L0_ffn_wv': _L0_ffn_in['wv'], 'L0_ffn_wo': _L0_ffn_in['wo'], 'L0_ffn_w1': _L0_ffn_in['w1'], 'L0_ffn_w2': _L0_ffn_in['w2'], 'L0_ffn_ln1': _L0_ffn_in['ln1'], 'L0_ffn_ln2': _L0_ffn_in['ln2']}
    _x0 = _d['L0_attn_x']
    _d['L0_attn_x'] = jax.random.normal(jax.random.fold_in(jax.random.key(seed), 1), (1, 8192, 512), dtype=_x0.dtype)
    del _x0
    return _d

def reference(L0_attn_x, L0_attn_W_q, L0_attn_W_k, L0_attn_W_v, L0_attn_W_o, L0_attn_beta_param, L0_ffn_attention_mask, L0_ffn_position_ids, L0_ffn_router_w, L0_ffn_router_b, L0_ffn_wq, L0_ffn_wk, L0_ffn_wv, L0_ffn_wo, L0_ffn_w1, L0_ffn_w2, L0_ffn_ln1, L0_ffn_ln2):

    def _L0_attn_ref(x, W_q, W_k, W_v, W_o, beta_param):
        import jax, jax.numpy as jnp
        import numpy as np
        N_HEADS = 16
        SEG = 64
        EPS = 1e-06

        def _sigma(x):
            return jax.nn.elu(x) + 1.0

        def _infini_attention(x, W_q, W_k, W_v, W_o, beta_param):
            B, T, D = x.shape
            H = N_HEADS
            dk = D // H
            assert T % SEG == 0
            S = T // SEG

            def proj(W):
                y = (x @ W.T).reshape(B, T, H, dk).transpose(0, 2, 1, 3)
                return y.reshape(B, H, S, SEG, dk).transpose(2, 0, 1, 3, 4)
            Qs, Ks, Vs = (proj(W_q), proj(W_k), proj(W_v))
            beta = jax.nn.sigmoid(beta_param).reshape(1, H, 1, 1)
            causal = jnp.triu(jnp.ones((SEG, SEG), dtype=bool), k=1)
            inv_sqrt_dk = 1.0 / jnp.sqrt(jnp.asarray(dk, x.dtype))
            M0 = jnp.zeros((B, H, dk, dk), dtype=x.dtype)
            z0 = jnp.zeros((B, H, dk), dtype=x.dtype)

            def step(carry, qkv):
                M, z = carry
                q, k, v = qkv
                sq = _sigma(q)
                denom_q = jnp.sum(sq * z[:, :, None, :], axis=-1, keepdims=True) + EPS
                A_mem = jnp.matmul(sq, M) / denom_q
                scores = jnp.matmul(q, jnp.swapaxes(k, -2, -1)) * inv_sqrt_dk
                scores = jnp.where(causal, -jnp.inf, scores)
                A_dot = jnp.matmul(jax.nn.softmax(scores, axis=-1), v)
                A_s = beta * A_mem + (1.0 - beta) * A_dot
                sk = _sigma(k)
                denom_k = jnp.sum(sk * z[:, :, None, :], axis=-1, keepdims=True) + EPS
                V_prev = jnp.matmul(sk, M) / denom_k
                M_new = M + jnp.einsum('bhtk,bhtv->bhkv', sk, v - V_prev)
                z_new = z + jnp.sum(sk, axis=-2)
                return ((M_new, z_new), A_s)
            (M, z), outs = jax.lax.scan(step, (M0, z0), (Qs, Ks, Vs))
            out = outs.transpose(1, 3, 0, 2, 4).reshape(B, S * SEG, H, dk)
            out = outs.transpose(1, 2, 0, 3, 4).reshape(B, H, T, dk)
            out = out.transpose(0, 2, 1, 3).reshape(B, T, D)
            out = out @ W_o.T
            return (out, M.mean(0), z.mean(0))

        def _reference_tuple_inner(x, W_q, W_k, W_v, W_o, beta_param):
            return _infini_attention(x, W_q, W_k, W_v, W_o, beta_param)
        return _reference_tuple_inner(x, W_q, W_k, W_v, W_o, beta_param)[0]

    def _L0_ffn_ref(x, attention_mask, position_ids, router_w, router_b, wq, wk, wv, wo, w1, w2, ln1, ln2):
        import jax, jax.numpy as jnp
        import numpy as np
        B, S, D, H, F = (4, 2048, 512, 16, 2048)
        CAP = 0.125
        ROPE_BASE = 10000.0

        def rmsnorm(x, g):
            return x * jax.lax.rsqrt(jnp.mean(x * x, -1, keepdims=True) + 1e-06) * g

        def rope(t, pos):
            hd = t.shape[-1]
            inv = 1.0 / ROPE_BASE ** (jnp.arange(0, hd, 2, dtype=jnp.float32) / hd)
            f = pos[:, None, :, None].astype(jnp.float32) * inv
            emb = jnp.concatenate([f, f], axis=-1)
            cos, sin = (jnp.cos(emb), jnp.sin(emb))
            rot = jnp.concatenate([-t[..., hd // 2:], t[..., :hd // 2]], axis=-1)
            return t * cos + rot * sin
        b, s, d = x.shape
        hd = d // H
        weights = (x @ router_w)[..., 0] + router_b[0]
        k = int(CAP * s)
        topv, topi = jax.lax.top_k(weights, k)
        thr = topv[:, -1]
        sel_mask = (weights > thr[:, None]).astype(x.dtype)
        kc = k - 1
        sel_idx = jnp.sort(topi[:, :kc], axis=1)
        bidx = jnp.arange(b)[:, None]
        x_sel = x[bidx, sel_idx]
        pos_sel = position_ids[bidx, sel_idx]
        w_sel = weights[bidx, sel_idx]
        m = attention_mask[:, 0]
        m_sel = m[bidx[:, :, None], sel_idx[:, :, None], sel_idx[:, None, :]]
        hn = rmsnorm(x_sel, ln1)

        def heads(t):
            return t.reshape(b, kc, H, hd).transpose(0, 2, 1, 3)
        q = rope(heads(hn @ wq), pos_sel)
        kk = rope(heads(hn @ wk), pos_sel)
        v = heads(hn @ wv)
        sc = jnp.einsum('bhqd,bhkd->bhqk', q, kk) / np.sqrt(hd).astype(np.float32)
        sc = sc + m_sel[:, None]
        a = jax.nn.softmax(sc, axis=-1)
        o = jnp.einsum('bhqk,bhkd->bhqd', a, v).transpose(0, 2, 1, 3).reshape(b, kc, d) @ wo
        x1 = x_sel + o
        x2 = x1 + jax.nn.gelu(rmsnorm(x1, ln2) @ w1) @ w2
        proc = x2 * w_sel[..., None]
        out = jnp.zeros_like(x).at[bidx, sel_idx].set(proc)
        return out + x * (1.0 - sel_mask)[..., None]
    x = L0_attn_x
    xn = _layernorm(x, axis=-1)
    x = x + _L0_attn_ref(xn, L0_attn_W_q, L0_attn_W_k, L0_attn_W_v, L0_attn_W_o, L0_attn_beta_param) + _L0_ffn_ref(xn, L0_ffn_attention_mask, L0_ffn_position_ids, L0_ffn_router_w, L0_ffn_router_b, L0_ffn_wq, L0_ffn_wk, L0_ffn_wv, L0_ffn_wo, L0_ffn_w1, L0_ffn_w2, L0_ffn_ln1, L0_ffn_ln2)
    return x

_drawn_inputs = setup_inputs


def setup_inputs(seed=0):
    import zlib

    import numpy as np

    out = dict(_drawn_inputs(seed))
    spreads = {'L0_attn_beta_param': (0.0, 2.0), 'L0_ffn_ln1': (1.0, 0.6), 'L0_ffn_ln2': (1.0, 0.6)}
    factors = {'L0_ffn_wq': 8.0, 'L0_ffn_wk': 8.0, 'L0_ffn_wv': 4.283, 'L0_ffn_wo': 4.417}
    for name, (base, spread) in spreads.items():
        noise = np.random.default_rng([zlib.crc32(name.encode()), seed]).standard_normal(out[name].shape)
        drawn = base * np.exp(spread * noise) if base else spread * noise
        out[name] = jnp.asarray(drawn.astype(out[name].dtype))
    for name, factor in factors.items():
        out[name] = (out[name] * factor).astype(out[name].dtype)
    return out
```

```python
from contextlib import ExitStack

import numpy as np

import concourse.bass as bass
from concourse import mybir

F32 = mybir.dt.float32
BF16 = mybir.dt.bfloat16
I32 = mybir.dt.int32
U32 = mybir.dt.uint32
ALU = mybir.AluOpType
ACT = mybir.ActivationFunctionType
AX = mybir.AxisListType



def alone(eng, sem):
    eng.sem_inc(sem, 1)


P = 128
NEG = -1.0e30
MAGIC = 1597463007.0


def bc(t, n):
    return t.rearrange("p (m o) -> p m o", o=1).broadcast_to([t.shape[0], t.shape[1], n])


def bm(t, m):
    return t.rearrange("p (o n) -> p o n", o=1).broadcast_to([t.shape[0], m, t.shape[1]])


def infini_attention(nc, x, wqT, wkT, wvT, woT, beta, router_w, router_b, out, wcol):
    T, D = x.shape
    H = beta.shape[1]
    DK = D // H
    SEG = 64
    G = D // P
    J = P // DK
    TILES = 2
    SEGS = 4
    BT = TILES * P
    NB = T // BT
    VW = DK + 1
    SCALE = float(DK) ** -0.5

    with ExitStack() as ctx:
        def sb(name, shape, dt=F32):
            return ctx.enter_context(nc.sbuf_tensor(name, shape, dt))

        def sem(name):
            return ctx.enter_context(nc.semaphore(name))

        wq = sb("wq", [P, G, D])
        wk = sb("wk", [P, G, D])
        wv = sb("wv", [P, G, D])
        wo = sb("wo", [P, G, D])
        rw = sb("rw", [P, D])
        rb = sb("rb", [P, 1])
        ident = sb("ident", [P, P])
        identb = sb("identb", [P, P], BF16)
        causal = sb("causal", [P, SEG], BF16)
        headmask = sb("headmask", [P, J])
        bt = sb("bt", [P, H])
        be = sb("be", [P, H])
        bs = sb("bs", [P, H])
        betas = sb("betas", [P, H])
        omb = sb("omb", [P, J, G])
        xin = sb("xin", [P, 2, TILES, D])
        xn = sb("xn", [P, 2, TILES, D])
        xu = sb("xu", [P, 2, TILES, D])
        junk = sb("junk", [P, D])
        stats = sb("stats", [P, TILES, 6])
        mv = sb("mv", [P, TILES, 2])
        var = sb("var", [P, TILES])
        rstd = sb("rstd", [P, TILES])
        nwt = sb("nwt", [P, TILES])
        rs1 = sb("rs1", [P, TILES])
        nmr = sb("nmr", [P, TILES])
        wt = sb("wt", [P, TILES])
        xnT = sb("xnT", [P, G, BT])
        QT = sb("QT", [P, 2, G, BT])
        KT = sb("KT", [P, 2, G, BT])
        SQT = sb("SQT", [P, 2, G, BT])
        SKT = sb("SKT", [P, G, BT])
        ET = sb("ET", [P, 2, 2, BT])
        RT = sb("RT", [P, 2, 2, BT])
        SK = sb("SK", [P, 2, TILES, D])
        DV = sb("DV", [P, 2, TILES, 2, H, VW])
        VS = sb("VS", [P, 2, TILES, H, VW])
        ksum = sb("ksum", [P, G, SEGS])
        Z = sb("Z", [P, 2, SEGS + 1, G])
        Zbd = sb("Zbd", [P, 2, SEGS, G, J])
        den = sb("den", [P, 2, 2 * TILES * H])
        rden = sb("rden", [P, 2, 2 * TILES * H])
        w2 = sb("w2", [P, 2, TILES, H])
        mx = sb("mx", [P, J, G])
        Pq = sb("Pq", [P, J, G, SEG])
        PT = sb("PT", [P, J, G, SEG])
        rl = sb("rl", [P, J, G])
        w1 = sb("w1", [P, J, G])
        T1 = sb("T1", [P, D])
        T2 = sb("T2", [P, D])
        As = sb("As", [P, D])
        AT = sb("AT", [P, G, P])
        outt = sb("outt", [P, 2, D])
        NA = sb("NA", [P, 2, G, DK])
        M = sb("M", [P, 2, G, DK])
        Mbd = sb("Mbd", [P, 2, G, P])

        proj = [ctx.enter_context(nc.psum_tensor(f"proj{i}", [P, 512], F32)) for i in range(2)]
        S = ctx.enter_context(nc.psum_tensor("S", [P, J, 512], F32))
        AB = ctx.enter_context(nc.psum_tensor("AB", [P, 2, G, 2, DK], F32))
        AM = ctx.enter_context(nc.psum_tensor("AM", [P, 512], F32))

        s_w = sem("s_w")
        s_rows = sem("s_rows")
        s_x = [sem("s_x0"), sem("s_x1")]
        s_alone_pe = sem("s_alone_pe")
        s_alone_dve = sem("s_alone_dve")
        s_c0 = sem("s_c0")
        s_const = sem("s_const")
        s_beta = sem("s_beta")
        s_be = sem("s_be")
        s_dve = sem("s_dve")
        s_ln = sem("s_ln")
        s_full = [sem("s_full0"), sem("s_full1")]
        s_free = [sem("s_free0"), sem("s_free1")]
        s_sq = sem("s_sq")
        s_sk = sem("s_sk")
        s_zbd = sem("s_zbd")
        s_dsk = sem("s_dsk")
        s_vs = [sem("s_vs0"), sem("s_vs1")]
        s_S = sem("s_S")
        s_sub = sem("s_sub")
        s_exp = sem("s_exp")
        s_pt = sem("s_pt")
        s_pv = sem("s_pv")
        s_ab = sem("s_ab")
        s_na = sem("s_na")
        s_tm = sem("s_tm")
        s_m = sem("s_m")
        s_mbd = sem("s_mbd")
        s_am = sem("s_am")
        s_t2 = sem("s_t2")
        s_t1 = sem("s_t1")
        s_as = sem("s_as")
        s_od = sem("s_od")
        s_of = sem("s_of")

        ORDER = (["XT0", "QT0", "KT0", "KT1", "OUT0", "SK0", "DEN", "OUT1"],
                 ["XT1", "QT1", "AST0", "V0", "V1", "SK1", "AST1"])
        STAGE2 = ("AST0", "OUT0", "AST1", "OUT1")
        FIRST = [[u for u in o if u not in STAGE2] for o in ORDER]
        LAST = [[u for u in o if u in STAGE2] for o in ORDER]

        def use(name, m, last):
            b = 0 if name in ORDER[0] else 1
            if m is None:
                return b, FIRST[b].index(name)
            order = (LAST if last else ORDER)[b]
            return b, m * len(ORDER[b]) + (len(FIRST[b]) + order.index(name))

        def take(eng, name, m, last=False):
            b, k = use(name, m, last)
            if not (isinstance(k, int) and k == 0):
                eng.wait_ge(s_free[b], k)
            return proj[b], s_full[b]

        def got(eng, name, m, last=False):
            b, k = use(name, m, last)
            eng.wait_ge(s_full[b], k + 1)
            return proj[b], s_free[b]

        def moved(eng, name, m, last=False):
            b, k = use(name, m, last)
            eng.wait_ge(s_free[b], k + 1)

        x_t = x.rearrange("(n a p) d -> n p a d", a=TILES, p=P)
        out_t = out.rearrange("(n a p) d -> n a p d", a=TILES, p=P)
        halves = [(32 * 0, 32 * 1), (32 * 2, 32 * 3)]
        PAIRS = (NB - 2) // 2
        assert NB == 2 * PAIRS + 2

        block = ctx.enter_context(nc.Block())

        @block.sync
        def _(sp):
            sp.sem_inc(s_of, 2)
            sp.dma_start(wq[:, :, :], wqT.rearrange("(c p) n -> p c n", p=P)).then_inc(s_w, 16)
            for n in range(2):
                sp.dma_start(xin[:, n, :, :], x_t[n]).then_inc(s_x[n], 16)
            for w, d in ((wk, wkT), (wv, wvT), (wo, woT)):
                sp.dma_start(w[:, :, :], d.rearrange("(c p) n -> p c n", p=P)).then_inc(s_w, 16)

            def shift_v(m, p):
                moved(sp, "V1", m)
                for src, dst in halves:
                    sp.dma_start(VS[dst:dst + 32, p, :, :, :], DV[src:src + 32, p, :, 1, :, :]).then_inc(s_vs[p], 16)

            def half(m, i, p, ln=True, stage1=True):
                if ln:
                    sp.wait_ge(s_ln, m + 1)
                    sp.dma_start(xin[:, p, :, :], x_t[m + 2]).then_inc(s_x[p], 16)
                moved(sp, "OUT0", m, not stage1)
                sp.dma_start(out_t[m, 0], outt[:, 0, :]).then_inc(s_od, 16)
                sp.wait_ge(s_od, m * 32 + 16)
                sp.sem_inc(s_of, 1)
                if stage1:
                    shift_v(m, 1 - p)
                moved(sp, "OUT1", m, not stage1)
                sp.dma_start(out_t[m, 1], outt[:, 1, :]).then_inc(s_od, 16)
                sp.wait_ge(s_od, m * 32 + 32)
                sp.sem_inc(s_of, 1)

            shift_v(None, 0)
            with sp.Fori(0, PAIRS) as i:
                half(i * 2, i, 0)
                half(i * 2 + 1, i, 1)
            half(NB - 2, PAIRS, 0, ln=False)
            half(NB - 1, PAIRS, 1, ln=False, stage1=False)
            sp.wait_ge(s_od, 32 * NB)

        @block.gpsimd
        def _(pool):
            pool.dma_start(rw[:, :], router_w.rearrange("d a -> a d").broadcast_to([P, D])).then_inc(s_rows, 16)
            pool.dma_start(rb[:, :], router_b.broadcast_to([P, 1])).then_inc(s_rows, 16)
            pool.dma_start(bt[:, :], beta.broadcast_to([P, H])).then_inc(s_rows, 16)
            pool.sem_inc(s_as, 1)
            pool.sem_inc(s_mbd, 1)
            pool.memset(ident[:, :], 0.0)
            pool.memset(identb[:, :], 0.0)
            pool.memset(causal[:, :], 0.0)
            pool.memset(headmask[:, :], 0.0)
            pool.memset(Z[:, :, :, :], 0.0)
            pool.memset(M[:, :, :, :], 0.0)
            pool.memset(Mbd[:, :, :, :], 0.0)
            for p in range(2):
                for a in range(TILES):
                    pool.memset(DV[:, p, a, 1, :, DK:VW], 1.0)
            pool.memset(junk[:, :], 0.0).then_inc(s_c0, 1)
            pool.wait_ge(s_c0, 1)
            for t in (ident, identb):
                pool.affine_select(out=t[:, :], in_=t[:, :], compare_op=ALU.not_equal, fill=1.0,
                                   base=0, pattern=[[-1, P]], channel_multiplier=1)
            step = 1
            for q in (0, SEG):
                pool.memset(junk[:, 0:1], 0.0).then_inc(s_c0, 1)
                step += 1
                pool.wait_ge(s_c0, step)
                pool.affine_select(out=causal[q:q + SEG, :], in_=causal[q:q + SEG, :], compare_op=ALU.is_ge,
                                   fill=NEG, base=0, pattern=[[-1, SEG]], channel_multiplier=1).then_inc(s_c0, 1)
                step += 1
                pool.wait_ge(s_c0, step)
            for j in range(J):
                pool.memset(headmask[DK * j:DK * j + DK, j:j + 1], 1.0).then_inc(s_c0, 1)
                step += 1
                pool.wait_ge(s_c0, step)
            pool.memset(junk[:, :], 0.0).then_inc(s_const, 1)
            pool.wait_ge(s_const, 1)

            def diagonal(s_no, b):
                pool.wait_ge(s_m, s_no + 2)
                for g in range(G):
                    ins = pool.tensor_tensor(Mbd[:, 1 - b, g, :].rearrange("p (j d) -> p j d", j=J),
                                             bm(M[:, 1 - b, g, :], J), bc(headmask[:, :], DK), ALU.mult)
                ins.then_inc(s_mbd, 1)

            def rows(n2, m, a):
                pool.wait_ge(s_t2, n2 + 2)
                pool.wait_ge(s_t1, n2 + 2)
                pool.tensor_tensor(As[:, :], T1[:, :], T2[:, :], ALU.add).then_inc(s_as, 1)
                pool.wait_ge(s_as, n2 + 2)

            def half(m):
                for a in range(TILES):
                    for b in range(2):
                        diagonal(m * SEGS + (2 * a + b), b)
                    rows(m * 2 + a, m, a)

            with pool.Fori(0, PAIRS) as i:
                half(i * 2)
                half(i * 2 + 1)
            half(NB - 2)
            half(NB - 1)

        @block.scalar
        def _(act):
            act.wait_ge(s_rows, 16 * 3)
            act.activation(be[:, :], bt[:, :], ACT.Exp, scale=-1.0).then_inc(s_be, 1)

            def copy(dst, src):
                return act.activation(dst, src, ACT.Copy)

            def xT(m, k):
                bank, free = got(act, f"XT{k}", m)
                copy(xnT[:, 2 * k:2 * k + 2, :], bank[:, :].rearrange("p (c t) -> p c t", c=2)).then_inc(free, 1)

            def feature(m, k, name, raw, pn, scale, s_used):
                bank, free = got(act, f"{name}{k}", m)
                v = bank[:, :].rearrange("p (c t) -> p c t", c=2)
                act.activation(raw[:, pn, 2 * k:2 * k + 2, :], v, ACT.Copy, scale=scale)
                if s_used is not None:
                    act.wait_ge(*s_used)
                act.activation(ET[:, k, :, :], v, ACT.Exp)
                act.activation(RT[:, k, :, :], v, ACT.Relu).then_inc(free, 1)

            def v_tile(m, pn, a):
                bank, free = got(act, f"V{a}", m)
                copy(DV[:, pn, a, 1, :, 0:DK], bank[:, :].rearrange("p (h d) -> p h d", h=H)).then_inc(free, 1)

            def sk_tile(m, pn, a):
                bank, free = got(act, f"SK{a}", m)
                copy(SK[:, pn, a, :], bank[:, :]).then_inc(free, 1)

            def prob(m, a):
                act.wait_ge(s_sub, m * 2 + (a + 1))
                act.activation(Pq[:, :, :, :], Pq[:, :, :, :], ACT.Exp).then_inc(s_exp, 1)

            def neg_a(m, sg):
                act.wait_ge(s_ab, m * SEGS + (sg + 1))
                copy(NA[:, sg % 2, :, :], AB[:, sg % 2, :, 0, :]).then_inc(s_na, 1)

            def a_t(m, a, last):
                bank, free = got(act, f"AST{a}", m, last)
                copy(AT[:, :, :], bank[:, :].rearrange("p (g t) -> p g t", g=G)).then_inc(free, 1)

            def half(m, p, stage1=True):
                last = not stage1
                n2 = (m + 1) * 2 if stage1 else None
                pn = 1 - p
                prob(m, 0)
                if stage1:
                    xT(m, 0)
                    xT(m, 1)
                neg_a(m, 0)
                if stage1:
                    for k in range(2):
                        feature(m, k, "QT", QT, pn, SCALE, (s_sk, m * 2 + (k + 1)))
                neg_a(m, 1)
                if stage1:
                    feature(m, 0, "KT", KT, pn, 1.0, (s_sq, n2 + 1))
                a_t(m, 0, last)
                neg_a(m, 2)
                prob(m, 1)
                if stage1:
                    feature(m, 1, "KT", KT, pn, 1.0, (s_sq, n2 + 2))
                    v_tile(m, pn, 0)
                    v_tile(m, pn, 1)
                neg_a(m, 3)
                if stage1:
                    sk_tile(m, pn, 0)
                    sk_tile(m, pn, 1)
                a_t(m, 1, last)

            xT(None, 0)
            xT(None, 1)
            for k in range(2):
                feature(None, k, "QT", QT, 0, SCALE, None)
            for k in range(2):
                feature(None, k, "KT", KT, 0, 1.0, (s_sq, k + 1))
            v_tile(None, 0, 0)
            v_tile(None, 0, 1)
            sk_tile(None, 0, 0)
            sk_tile(None, 0, 1)
            with act.Fori(0, PAIRS) as i:
                half(i * 2, 0)
                half(i * 2 + 1, 1)
            half(NB - 2, 0)
            half(NB - 1, 1, stage1=False)

        @block.vector
        def _(dve):
            done = [0]
            base = [0]

            def link(ins):
                done[0] += 1
                ins.then_inc(s_dve, 1)
                dve.wait_ge(s_dve, base[0] + done[0])

            def layer_norm(n, nh, p):
                dve.wait_ge(s_x[p], (nh + 1) * 16)
                for a in range(TILES):
                    ins = dve.bn_stats(stats[:, a, :], xin[:, p, a, :])
                    if a == TILES - 1:
                        link(ins)
                    else:
                        ins.then_inc(s_dve, 1)
                        done[0] += 1
                alone(dve, s_alone_dve)
                for a in range(TILES):
                    ins = dve.bn_aggr(mv[:, a, :], stats[:, a, :])
                    if a == TILES - 1:
                        link(ins)
                    else:
                        ins.then_inc(s_dve, 1)
                        done[0] += 1
                link(dve.tensor_scalar(var[:, :], mv[:, :, 1], 1e-5, None, ALU.add))
                rsqrt(dve, link, rstd[:, :], var[:, :], nwt[:, :])
                dve.scalar_tensor_tensor(out=nmr[:, :], in0=mv[:, :, 0], scalar=-1.0, in1=rstd[:, :],
                                         op0=ALU.mult, op1=ALU.mult)
                link(dve.tensor_scalar(rs1[:, :], rstd[:, :], 1.0, None, ALU.add))
                for a in range(TILES):
                    dve.tensor_scalar(xn[:, p, a, :], xin[:, p, a, :], mv[:, a, 0:1], rstd[:, a:a + 1],
                                      ALU.subtract, ALU.mult)
                    link(dve.tensor_scalar(xu[:, p, a, :], xin[:, p, a, :], rs1[:, a:a + 1], nmr[:, a:a + 1],
                                           ALU.mult, ALU.add))

            def sigma(m, name, k, dst, s_done):
                moved(dve, f"{name}{k}", m)
                dve.scalar_tensor_tensor(out=dst, in0=ET[:, k, :, :], scalar=1.0, in1=RT[:, k, :, :],
                                         op0=ALU.min, op1=ALU.add).then_inc(s_done, 1)

            def z_chain(n, n2, pn):
                dve.wait_ge(s_sk, n2 + 2)
                link(dve.tensor_reduce(ksum[:, :, :], SKT[:, :, :].rearrange("p g (s t) -> p g s t", s=SEGS),
                                       AX.X, ALU.add))
                link(dve.tensor_copy(Z[:, pn, 0, :], Z[:, 1 - pn, SEGS, :]))
                for s in range(SEGS):
                    link(dve.tensor_tensor(Z[:, pn, s + 1, :], Z[:, pn, s, :], ksum[:, :, s], ALU.add))
                sg = SEGS * G
                dve.tensor_tensor(Zbd[:, pn, :, :, :].rearrange("p s g j -> p (s g) j"),
                                  Z[:, pn, 0:SEGS, :].rearrange("p s (g o) -> p (s g) o", o=1).broadcast_to([P, sg, J]),
                                  headmask[:, :].rearrange("p (o j) -> p o j", o=1).broadcast_to([P, sg, J]),
                                  ALU.mult).then_inc(s_zbd, 1)

            def denominators(m, n2, pn):
                bank, free = got(dve, "DEN", m)
                N = 2 * TILES * H
                dve.tensor_scalar(den[:, pn, :], bank[:, 0:N], 1e-6, None, ALU.add).then_inc(free, 1)
                moved(dve, "DEN", m)
                link(dve.reciprocal(rden[:, pn, :], den[:, pn, :]))
                link(dve.tensor_tensor(w2[:, pn, :, :], rden[:, pn, TILES * H:N].rearrange("p (a h) -> p a h", a=TILES),
                                  betas[:, :].rearrange("p (o h) -> p o h", o=1).broadcast_to([P, TILES, H]), ALU.mult))
                for a in range(TILES):
                    moved(dve, f"SK{a}", m)
                    dve.scalar_tensor_tensor(
                        out=DV[:, pn, a, 0, :, 0:DK], in0=SK[:, pn, a, :].rearrange("p (h d) -> p h d", h=H),
                        scalar=-1.0,
                        in1=rden[:, pn, a * H:a * H + H].rearrange("p (h o) -> p h o", o=1).broadcast_to([P, H, DK]),
                        op0=ALU.mult, op1=ALU.mult).then_inc(s_dsk, 1)

            def s_half(a):
                return S[:, :, a * 256:a * 256 + 256].rearrange("p j (g k) -> p j g k", g=G)

            def softmax_in(m, a):
                dve.wait_ge(s_S, m * 2 + (a + 1))
                link(dve.tensor_reduce(mx[:, :, :], s_half(a), AX.X, ALU.max))
                dve.tensor_tensor(Pq[:, :, :, :], s_half(a),
                                  mx[:, :, :].rearrange("p j (g o) -> p j g o", o=1).broadcast_to([P, J, G, SEG]),
                                  ALU.subtract).then_inc(s_sub, 1)

            def p_transpose(m, a):
                dve.wait_ge(s_exp, m * 2 + (a + 1))
                dve.transpose(PT[:, :, :, :].rearrange("p j g k -> p (j g k)"),
                              Pq[:, :, :, :].rearrange("p j g k -> p (j g k)")).then_inc(s_pt, 1)

            def m_next(m, sg):
                b = sg % 2
                dve.wait_ge(s_tm, m * SEGS + (sg + 1))
                dve.tensor_tensor(M[:, 1 - b, :, :], AB[:, b, :, 1, :], M[:, b, :, :], ALU.add).then_inc(s_m, 1)

            def softmax_part(m, a):
                dve.wait_ge(s_pv, m * 2 + (a + 1))
                dve.wait_ge(s_as, m * 2 + a + 1)
                O = S[:, :, a * 256:a * 256 + G * VW].rearrange("p j (g d) -> p j g d", g=G)
                link(dve.reciprocal(rl[:, :, :].rearrange("p j (g o) -> p j g o", o=1), O[:, :, :, DK:VW]))
                link(dve.tensor_tensor(w1[:, :, :], rl[:, :, :], omb[:, :, :], ALU.mult))
                dve.tensor_tensor(T1[:, :].rearrange("p (g j d) -> p j g d", g=G, j=J), O[:, :, :, 0:DK],
                                  w1[:, :, :].rearrange("p j (g o) -> p j g o", o=1).broadcast_to([P, J, G, DK]),
                                  ALU.mult).then_inc(s_t1, 1)

            def memory_part(m, p, a):
                dve.wait_ge(s_am, m * SEGS + (2 * a + 2))
                dve.tensor_tensor(T2[:, :].rearrange("p (h d) -> p h d", h=H),
                                  AM[:, :].rearrange("p (h d) -> p h d", h=H),
                                  w2[:, p, a, :].rearrange("p (h o) -> p h o", o=1).broadcast_to([P, H, DK]),
                                  ALU.mult).then_inc(s_t2, 1)

            def out_rows(m, p, a, last):
                bank, free = got(dve, f"OUT{a}", m, last)
                dve.wait_ge(s_of, m * 2 + (a + 1))
                dve.tensor_tensor(outt[:, a, :], bank[:, :], xu[:, p, a, :], ALU.add).then_inc(free, 1)

            def ln_block(n, nh, p, col):
                layer_norm(n, nh, p)
                for a in range(TILES):
                    link(dve.tensor_tensor_reduce(junk[:, :], xn[:, p, a, :], rw[:, :], 1.0, 0.0, ALU.mult, ALU.add,
                                                  wt[:, a:a + 1]))
                dve.tensor_copy(col, wt[:, :]).then_inc(s_ln, 1)

            def half(m, i, p, ln=True, stage1=True):
                pn = 1 - p
                last = not stage1
                n2 = (m + 1) * 2 if stage1 else None
                softmax_in(m, 0)
                p_transpose(m, 0)
                if stage1:
                    sigma(m, "QT", 0, SQT[:, pn, 0:2, :], s_sq)
                m_next(m, 0)
                if stage1:
                    sigma(m, "QT", 1, SQT[:, pn, 2:4, :], s_sq)
                softmax_part(m, 0)
                if stage1:
                    sigma(m, "KT", 0, SKT[:, 0:2, :], s_sk)
                m_next(m, 1)
                memory_part(m, p, 0)
                softmax_in(m, 1)
                p_transpose(m, 1)
                if stage1:
                    sigma(m, "KT", 1, SKT[:, 2:4, :], s_sk)
                    z_chain(m + 1, n2, pn)
                m_next(m, 2)
                out_rows(m, p, 0, last)
                softmax_part(m, 1)
                m_next(m, 3)
                memory_part(m, p, 1)
                if stage1:
                    denominators(m, n2, pn)
                out_rows(m, p, 1, last)
                if ln:
                    ln_block(m + 2, i + 1, p, wcol[:, bass.ds((m + 2) * 2, 2)])

            LINKS = 74
            for s in (s_m, s_t1, s_t2):
                dve.sem_inc(s, 1)
            dve.wait_ge(s_const, 1)
            dve.wait_ge(s_rows, 16 * 3)
            dve.wait_ge(s_be, 1)
            link(dve.tensor_scalar(bs[:, :], be[:, :], 1.0, None, ALU.add))
            link(dve.reciprocal(betas[:, :], bs[:, :]))
            link(dve.tensor_scalar(omb[:, :, :].rearrange("p j g -> p g j"),
                                   betas[:, :].rearrange("p (g j) -> p g j", g=G), -1.0, 1.0, ALU.mult, ALU.add))
            for n in range(2):
                ln_block(n, 0, n, wcol[:, 2 * n:2 * n + 2])
            for k in range(2):
                sigma(None, "QT", k, SQT[:, 0, 2 * k:2 * k + 2, :], s_sq)
            for k in range(2):
                sigma(None, "KT", k, SKT[:, 2 * k:2 * k + 2, :], s_sk)
            z_chain(0, 0, 0)
            denominators(None, 0, 0)
            start = done[0]
            with dve.Fori(0, PAIRS) as i:
                done[0] = 0
                base[0] = i * LINKS + start
                half(i * 2, i, 0)
                half(i * 2 + 1, i, 1)
                assert done[0] == LINKS, done[0]
            base[0] = start + PAIRS * LINKS
            done[0] = 0
            half(NB - 2, PAIRS, 0, ln=False)
            half(NB - 1, PAIRS, 1, ln=False, stage1=False)
            dve.tensor_scalar(wcol[:, :], wcol[:, :], rb[:, 0:1], None, ALU.add)

        @block.tensor
        def _(pe):
            def x_transposes(m, n, pn, k):
                if k == 0:
                    pe.wait_ge(s_ln, n + 1)
                bank, full = take(pe, f"XT{k}", m)
                for c in range(2):
                    for a in range(TILES):
                        o = c * BT + a * P
                        ch = 2 * k + c
                        ins = pe.transpose(bank[:, o:o + P], xn[:, pn, a, ch * P:ch * P + P], ident[:, :])
                ins.then_inc(full, 1)

            def feature(m, n2, name, w, k):
                if k == 0 and name == "QT":
                    moved(pe, "XT0", m)
                    moved(pe, "XT1", m)
                bank, full = take(pe, f"{name}{k}", m)
                for g in range(2):
                    for c in range(G):
                        o = (2 * k + g) * P
                        ins = pe.matmul(bank[:, g * BT:g * BT + BT], w[:, c, o:o + P], xnT[:, c, :],
                                        start=c == 0, stop=c == G - 1)
                ins.then_inc(full, 1)

            def values(m, a):
                bank, full = take(pe, f"V{a}", m)
                for c in range(G):
                    ins = pe.matmul(bank[:, :], xnT[:, c, a * P:a * P + P], wv[:, c, :], start=c == 0, stop=c == G - 1)
                ins.then_inc(full, 1)

            def sk_rows(m, n2, a):
                if a == 0:
                    pe.wait_ge(s_sk, n2 + 2)
                bank, full = take(pe, f"SK{a}", m)
                for g in range(G):
                    ins = pe.transpose(bank[:, g * P:g * P + P], SKT[:, g, a * P:a * P + P], ident[:, :])
                ins.then_inc(full, 1)

            def denominators(m, n, pn):
                pe.wait_ge(s_zbd, n + 1)
                pe.wait_ge(s_sq, n * 2 + 2)
                bank, full = take(pe, "DEN", m)
                for q in range(2):
                    for a in range(TILES):
                        for b in range(2):
                            t = a * P + b * SEG
                            for g in range(G):
                                lhsT = SKT[:, g, t:t + SEG] if q == 0 else SQT[:, pn, g, t:t + SEG]
                                o = (q * TILES + a) * H + g * J
                                ins = pe.matmul(bank[b * SEG:b * SEG + SEG, o:o + J], lhsT,
                                                Zbd[:, pn, 2 * a + b, g, :], start=True, stop=True)
                ins.then_inc(full, 1)

            def scores(m, p, a):
                pe.wait_ge(s_t1, m * 2 + a + 1)
                for j in range(J):
                    pe.matmul(S[:, j, a * 256:a * 256 + 256].rearrange("p (g k) -> p g k", g=G), identb[:, :],
                              causal[:, :].rearrange("p (o k) -> p o k", o=1).broadcast_to([P, G, SEG]),
                              start=True, stop=False, skip_group_check=True)
                for b in range(2):
                    t = a * P + b * SEG
                    for g in range(G):
                        for j in range(J):
                            q = slice(DK * j, DK * j + DK)
                            o = a * 256 + g * SEG
                            ins = pe.matmul(S[b * SEG:b * SEG + SEG, j, o:o + SEG], QT[q, p, g, t:t + SEG],
                                            KT[q, p, g, t:t + SEG], start=False, stop=(g == G - 1),
                                            skip_group_check=True)
                ins.then_inc(s_S, 1)

            def a_and_b(m, p, sg):
                a, b = sg // 2, sg % 2
                if sg == 0:
                    pe.wait_ge(s_dsk, m * 2 + 2)
                pe.wait_ge(s_m, m * SEGS + sg + 1)
                alone(pe, s_alone_pe)
                t = slice(b * SEG, b * SEG + SEG)
                for g in range(G):
                    for j in range(J):
                        h = g * J + j
                        ins = pe.matmul(AB[DK * j:DK * j + DK, b, g, :, :], SK[t, p, a, h * DK:h * DK + DK],
                                        DV[t, p, a, :, h, 0:DK], start=g == 0, stop=g == G - 1,
                                        skip_group_check=True)
                ins.then_inc(s_ab, 1)

            def t_times_m(m, sg):
                b = sg % 2
                pe.wait_ge(s_na, m * SEGS + (sg + 1))
                alone(pe, s_alone_pe)
                for g in range(G):
                    for j in range(J):
                        q = slice(DK * j, DK * j + DK)
                        ins = pe.matmul(AB[q, b, g, 1, :], NA[q, b, g, :], M[q, b, g, :], start=False,
                                        stop=g == G - 1, skip_group_check=True)
                ins.then_inc(s_tm, 1)

            def memory(m, p, sg):
                a, b = sg // 2, sg % 2
                t = a * P + b * SEG
                pe.wait_ge(s_mbd, m * SEGS + sg + 1)
                if b == 0:
                    pe.wait_ge(s_t2, m * 2 + a + 1)
                for g in range(G):
                    ins = pe.matmul(AM[b * SEG:b * SEG + SEG, g * P:g * P + P], SQT[:, p, g, t:t + SEG],
                                    Mbd[:, b, g, :], start=True, stop=True)
                ins.then_inc(s_am, 1)

            def pv(m, mh, p, a):
                pe.wait_ge(s_pt, m * 2 + (a + 1))
                if a == 0:
                    pe.wait_ge(s_vs[p], (mh + 1) * 32)
                alone(pe, s_alone_pe)
                for g in range(G):
                    for j in range(J):
                        h = g * J + j
                        o = a * 256 + g * VW
                        for q in range(4):
                            r = slice(32 * q, 32 * q + 32)
                            dst = S[r, j, o:o + VW]
                            own = (q % 2) * 32
                            ins = pe.matmul(dst, PT[r, j, g, own:own + 32], DV[r, p, a, 1, h, :],
                                            start=True, stop=q % 2 == 0)
                            if q % 2:
                                ins = pe.matmul(dst, PT[r, j, g, 0:32], VS[r, p, a, h, :], start=False, stop=True)
                ins.then_inc(s_pv, 1)

            def as_transposes(m, a, last):
                pe.wait_ge(s_as, m * 2 + (a + 2))
                bank, full = take(pe, f"AST{a}", m, last)
                for g in range(G):
                    ins = pe.transpose(bank[:, g * P:g * P + P], As[:, g * P:g * P + P], ident[:, :])
                ins.then_inc(full, 1)

            def out_proj(m, a, last):
                moved(pe, f"AST{a}", m, last)
                bank, full = take(pe, f"OUT{a}", m, last)
                for g in range(G):
                    ins = pe.matmul(bank[:, :], AT[:, g, :], wo[:, g, :], start=g == 0, stop=g == G - 1)
                ins.then_inc(full, 1)

            def half(m, mh, p, stage1=True):
                pn = 1 - p
                last = not stage1
                n = m + 1 if stage1 else None
                n2 = (m + 1) * 2 if stage1 else None
                scores(m, p, 0)
                if stage1:
                    x_transposes(m, n, pn, 0)
                    x_transposes(m, n, pn, 1)
                a_and_b(m, p, 0)
                if stage1:
                    feature(m, n2, "QT", wq, 0)
                t_times_m(m, 0)
                memory(m, p, 0)
                if stage1:
                    feature(m, n2, "QT", wq, 1)
                a_and_b(m, p, 1)
                pv(m, mh, p, 0)
                if stage1:
                    feature(m, n2, "KT", wk, 0)
                t_times_m(m, 1)
                memory(m, p, 1)
                scores(m, p, 1)
                as_transposes(m, 0, last)
                a_and_b(m, p, 2)
                if stage1:
                    feature(m, n2, "KT", wk, 1)
                    values(m, 0)
                t_times_m(m, 2)
                memory(m, p, 2)
                out_proj(m, 0, last)
                pv(m, mh, p, 1)
                if stage1:
                    values(m, 1)
                a_and_b(m, p, 3)
                if stage1:
                    sk_rows(m, n2, 0)
                    sk_rows(m, n2, 1)
                t_times_m(m, 3)
                memory(m, p, 3)
                if stage1:
                    denominators(m, n, pn)
                as_transposes(m, 1, last)
                out_proj(m, 1, last)

            pe.wait_ge(s_const, 1)
            pe.wait_ge(s_w, 16 * 4)
            x_transposes(None, 0, 0, 0)
            x_transposes(None, 0, 0, 1)
            for name, w in (("QT", wq), ("KT", wk)):
                feature(None, 0, name, w, 0)
                feature(None, 0, name, w, 1)
            values(None, 0)
            values(None, 1)
            sk_rows(None, 0, 0)
            sk_rows(None, 0, 1)
            denominators(None, 0, 0)
            with pe.Fori(0, PAIRS) as i:
                half(i * 2, i, 0)
                half(i * 2 + 1, i, 1)
            half(NB - 2, PAIRS, 0)
            half(NB - 1, PAIRS, 1, stage1=False)


def select_tokens(nc, w, thr, idx, K, list_dram):
    NT = w.shape[1]
    N = P * NT
    Q = K // P
    BIG = 65536.0
    KNEG = float(N - K + 1)

    with ExitStack() as ctx:
        def sb(name, shape, dt=F32):
            return ctx.enter_context(nc.sbuf_tensor(name, shape, dt))

        def sem(name):
            return ctx.enter_context(nc.semaphore(name))

        onesP = sb("onesP", [P, P])
        before = sb("before", [P, P])
        oneT = sb("oneT", [P, NT])
        hit = sb("hit", [P, NT])
        y = sb("y", [P, NT])
        cnt = sb("cnt", [P, 2])
        flag = sb("flag", [P, 1])
        sign = sb("sign", [P, 1])
        kk = sb("kk", [P, 1])
        bitf = sb("bitf", [P, 1])
        biti = sb("biti", [P, 1], I32)
        cur = sb("cur", [P, 1], I32)
        cand = sb("cand", [P, 1], I32)
        keep = sb("keep", [P, 1], I32)
        lim = sb("lim", [P, 1])
        gt = sb("gt", [P, NT])
        eq = sb("eq", [P, NT])
        chosen = sb("chosen", [P, NT])
        tot = sb("tot", [P, NT])
        run = sb("run", [P, NT])
        place = sb("place", [P, NT])
        away = sb("away", [P, NT])
        dest = sb("dest", [P, NT], U32)
        token = sb("token", [P, NT], U32)
        zero = sb("zero", [P, 1], U32)
        pc = ctx.enter_context(nc.psum_tensor("pc", [P, 512], F32))
        pp = ctx.enter_context(nc.psum_tensor("pp", [P, 512], F32))
        pt = ctx.enter_context(nc.psum_tensor("pt", [P, 512], F32))

        s_k0 = sem("s_k0")
        s_k = sem("s_k")
        s_cnt = sem("s_cnt")
        s_tot = sem("s_tot")
        s_step = sem("s_step")
        s_x = sem("s_mark")
        s_pre = sem("s_pre")
        s_dest = sem("s_dest")
        s_pad = sem("s_pad")
        s_sc = sem("s_scat")
        s_idx = sem("s_idx")

        block = ctx.enter_context(nc.Block())

        @block.gpsimd
        def _(pool):
            pool.memset(onesP[:, :], 1.0)
            pool.memset(oneT[:, :], 1.0)
            pool.memset(zero[:, :], 0)
            pool.iota(token[:, :], pattern=[[P, NT]], base=0, channel_multiplier=1)
            pool.memset(before[:, :], 1.0).then_inc(s_k0, 1)
            pool.wait_ge(s_k0, 1)
            pool.affine_select(out=before[:, :], in_=before[:, :], compare_op=ALU.is_gt, fill=0.0,
                               base=0, pattern=[[1, P]], channel_multiplier=-1).then_inc(s_k, 1)
            pool.wait_ge(s_k, 1)
            pool.dma_start(list_dram[K - 1:K, :], zero[0:1, :]).then_inc(s_pad, 16)
            pool.wait_ge(s_pad, 16)
            pool.wait_ge(s_dest, 1)
            for j in range(NT):
                pool.indirect_dma_start(list_dram, bass.IndirectOffsetOnAxis(ap=dest[:, j:j + 1], axis=0),
                                        token[:, j:j + 1], None, bounds_check=K - 2,
                                        oob_is_err=False).then_inc(s_sc, 16)
            pool.wait_ge(s_sc, 16 * NT)
            pool.dma_start(idx[:, :], list_dram.rearrange("(p q) a -> p (q a)", q=Q)).then_inc(s_idx, 16)
            pool.wait_ge(s_idx, 16)

        @block.tensor
        def _(pe):
            pe.wait_ge(s_k, 1)

            def total(n):
                pe.wait_ge(s_cnt, n + 1)
                pe.matmul(pc[:, 0:2], onesP[:, :], cnt[:, :], start=True, stop=True).then_inc(s_tot, 1)

            total(0)
            with pe.Fori(0, 31) as i:
                total(i + 1)
            total(32)
            for n, x in enumerate((eq, chosen)):
                pe.wait_ge(s_x, n + 1)
                pe.matmul(pp[:, 0:NT], before[:, :], x[:, :], start=True, stop=True)
                pe.matmul(pt[:, 0:NT], onesP[:, :], x[:, :], start=True, stop=True).then_inc(s_pre, 1)

        @block.vector
        def _(dve):
            done = [0]
            base = [0]

            def link(ins):
                done[0] += 1
                ins.then_inc(s_step, 1)
                dve.wait_ge(s_step, base[0] + done[0])

            def count(src, level, op, n, out):
                dve.scalar_tensor_tensor(out=out, in0=src, scalar=level, in1=oneT[:, :], op0=op, op1=ALU.mult,
                                         accum_out=cnt[:, 0:1]).then_inc(s_cnt, 1)
                dve.wait_ge(s_tot, n + 1)

            dve.wait_ge(s_k, 1)
            link(dve.memset(cnt[:, :], 0.0))
            link(dve.memset(cur[:, :], 0))
            link(dve.memset(bitf[:, :], float(2 ** 30)))
            link(dve.memset(biti[:, :], 2 ** 30))
            count(w[:, :], 0.0, ALU.is_ge, 0, hit[:, :])
            link(dve.tensor_scalar(flag[:, :], pc[:, 0:1], float(K), None, ALU.is_ge))
            link(dve.tensor_scalar(sign[:, :], flag[:, :], 2.0, -1.0, ALU.mult, ALU.add))
            link(dve.tensor_scalar(kk[:, :], flag[:, :], float(K) - KNEG, KNEG, ALU.mult, ALU.add))
            link(dve.tensor_scalar(y[:, :], w[:, :], sign[:, 0:1], None, ALU.mult))
            start = done[0]
            LINKS = 5
            with dve.Fori(0, 31) as i:
                done[0] = 0
                base[0] = i * LINKS + start
                link(dve.tensor_tensor(cand[:, :], cur[:, :], biti[:, :], ALU.bitwise_or))
                count(y[:, :], cand[:, 0:1].bitcast(F32), ALU.is_ge, i + 1, hit[:, :])
                link(dve.tensor_scalar(keep[:, :], pc[:, 0:1], kk[:, 0:1], bitf[:, 0:1], ALU.is_ge, ALU.mult))
                link(dve.tensor_tensor(cur[:, :], cur[:, :], keep[:, :], ALU.bitwise_or))
                link(dve.tensor_scalar(bitf[:, :], bitf[:, :], 0.5, None, ALU.mult))
                link(dve.tensor_copy(biti[:, :], bitf[:, :]))
                assert done[0] == LINKS, done[0]
            base[0] = start + 31 * LINKS
            done[0] = 0
            link(dve.tensor_tensor(thr[:, :], cur[:, :].bitcast(F32), sign[:, :], ALU.mult))
            count(w[:, :], thr[:, 0:1], ALU.is_gt, 32, gt[:, :])
            link(dve.tensor_scalar(lim[:, :], pc[:, 0:1], -1.0, float(K - 1), ALU.mult, ALU.add))
            dve.tensor_scalar(eq[:, :], w[:, :], thr[:, 0:1], None, ALU.is_equal).then_inc(s_x, 1)

            def before_each(n):
                dve.wait_ge(s_pre, n + 1)
                link(dve.tensor_copy(tot[:, :], pt[:, 0:NT]))
                link(dve.tensor_tensor_scan(run[:, :], oneT[:, :], tot[:, :], 0.0, ALU.mult, ALU.add))
                link(dve.tensor_tensor(run[:, :], run[:, :], tot[:, :], ALU.subtract))
                link(dve.tensor_tensor(place[:, :], pp[:, 0:NT], run[:, :], ALU.add))

            before_each(0)
            link(dve.scalar_tensor_tensor(out=hit[:, :], in0=place[:, :], scalar=lim[:, 0:1], in1=eq[:, :],
                                          op0=ALU.is_lt, op1=ALU.mult))
            dve.tensor_tensor(chosen[:, :], gt[:, :], hit[:, :], ALU.add).then_inc(s_x, 1)
            dve.wait_ge(s_x, 2)
            before_each(1)
            link(dve.tensor_scalar(away[:, :], chosen[:, :], -BIG, BIG, ALU.mult, ALU.add))
            link(dve.tensor_tensor(place[:, :], place[:, :], chosen[:, :], ALU.mult))
            dve.tensor_tensor(dest[:, :], place[:, :], away[:, :], ALU.add).then_inc(s_dest, 1)


def rsqrt(dve, link, y, v, t):
    link(dve.tensor_scalar(y.bitcast(I32), v.bitcast(I32), -0.5, MAGIC, ALU.mult, ALU.add))
    for _ in range(4):
        link(dve.scalar_tensor_tensor(out=t, in0=y, scalar=-0.5, in1=y, op0=ALU.mult, op1=ALU.mult))
        link(dve.tensor_tensor(t, t, v, ALU.mult))
        link(dve.scalar_tensor_tensor(out=y, in0=t, scalar=1.5, in1=y, op0=ALU.add, op1=ALU.mult))


def feed_forward(nc, x, maskT, positions, router_w, router_b, wq_d, wk_d, wv_d, wo_d, w1_d, w2_d, ln1, ln2,
                 thr, idx, out, cols_dram):
    D = x.shape[1]
    F = w1_d.shape[1]
    C = maskT.shape[0]
    H, DK = 16, 32
    Q = idx.shape[1]
    K = Q * P
    G = D // P
    J = P // DK
    CC = C // P
    FC = F // P
    HF = DK // 2
    INV = 1.0 / np.sqrt(np.float32(DK))
    freq = (np.float32(1.0) / np.float32(10000.0) ** (np.arange(0, DK, 2, dtype=np.float32) / np.float32(DK)))
    TWO_PI = 2.0 * np.pi
    C1 = 6.28125
    C2 = float(np.float32(np.floor((TWO_PI - C1) * 2 ** 20) / 2 ** 20))
    C3 = float(np.float32(TWO_PI - C1 - C2))
    ROUND = 12582912.0
    PI = float(np.nextafter(np.float32(np.pi), np.float32(0)))

    with ExitStack() as ctx:
        def sb(name, shape, dt=F32, c=ctx):
            return c.enter_context(nc.sbuf_tensor(name, shape, dt))

        def sem(name, c=ctx):
            return c.enter_context(nc.semaphore(name))

        ident = sb("ident2", [P, P])
        xs = sb("xs", [P, Q, D])
        wsel = sb("wsel", [P, Q])
        above = sb("above", [P, Q])
        l1 = sb("l1", [P, D])
        l2 = sb("l2", [P, D])
        xs2 = sb("xs2", [P, Q, D])
        x1T = sb("x1T", [P, G, K])
        ms = sb("ms", [P, Q])
        rr = sb("rr", [P, Q])
        rt = sb("rt", [P, Q])

        mid = ctx.enter_context(ExitStack())
        QT = sb("QT2", [P, G, K], c=mid)
        KT = sb("KT2", [P, G, K], c=mid)
        V = sb("V2", [P, Q, D], c=mid)
        msel = sb("msel", [P, Q, K], c=mid)
        with ExitStack() as c1:
            wq = xs2[:, 0:4, :]
            wk = xs2[:, 4:8, :]
            wv = x1T[:, 0:2, :].rearrange("p g (a n) -> p (g a) n", n=D)
            mrow = x1T[:, 2:4, :]
            rw = sb("rw2", [P, D], c=c1)
            rb = sb("rb2", [P, 1], c=c1)
            pos = sb("pos", [P, Q], I32, c=c1)
            posf = sb("posf", [P, Q], c=c1)
            cidx = sb("cidx", [P, Q], U32, c=c1)
            c2 = sb("c2", [P, 2, Q], U32, c=c1)
            inv = sb("inv", [P, HF], c=c1)
            ang = sb("ang", [P, Q * HF], c=c1)
            turn = sb("turn", [P, Q * HF], c=c1)
            angc = sb("angc", [P, Q * HF], c=c1)
            sin = sb("sin", [P, Q, HF], c=c1)
            cos = sb("cos", [P, Q, HF], c=c1)
            nsin = sb("nsin", [P, Q, HF], c=c1)
            stats = sb("stats2", [P, Q, 6], c=c1)
            mv = sb("mv2", [P, Q, 2], c=c1)
            var = sb("var2", [P, Q], c=c1)
            rstd = sb("rstd2", [P, Q], c=c1)
            rt0 = sb("rt0", [P, Q], c=c1)
            hn = sb("hn", [P, D], c=c1)
            hnT = sb("hnT", [P, G, P], c=c1)
            qa = sb("qa", [P, D], c=c1)
            junk = qa
            qb = sb("qb", [P, D], c=c1)
            junk2 = sb("junk2", [P, 1], c=c1)
            qr = sb("qr", [P, 2, D], c=c1)
            mcol = sb("mcol", [P, 2, P * 8], c=c1)
            bank = [c1.enter_context(nc.psum_tensor(f"fb{i}", [P, 512], F32)) for i in range(6)]
            tb = [c1.enter_context(nc.psum_tensor(f"ft{i}", [P, 512], F32)) for i in range(2)]

            s_w = sem("s_w2", c1)
            s_xg = sem("s_xg", c1)
            s_rows = sem("s_rows2", c1)
            s_pos = sem("s_pos", c1)
            s_ci = sem("s_ci", c1)
            s_mr = [sem("s_mr0", c1), sem("s_mr1", c1)]
            s_mt = sem("s_mt", c1)
            s_mc = sem("s_mc", c1)
            s_mw = [sem("s_mw0", c1), sem("s_mw1", c1)]
            s_ms = sem("s_ms", c1)
            s_k0 = sem("s_l0", c1)
            s_k = sem("s_l", c1)
            s_st = sem("s_st", c1)
            s_pool = sem("s_pool", c1)
            s_ang = sem("s_ang", c1)
            s_sin = sem("s_sin", c1)
            s_hn = sem("s_hn", c1)
            s_ht = sem("s_ht", c1)
            s_hc = sem("s_hc", c1)
            s_q = sem("s_q2", c1)
            s_vc = sem("s_vc", c1)
            s_r = sem("s_r", c1)
            s_rt = sem("s_rt", c1)
            s_qt = sem("s_qt", c1)

            block = c1.enter_context(nc.Block())

            @block.sync
            def _(sp):
                for w_, d_ in ((wq, wq_d), (wk, wk_d), (wv, wv_d)):
                    sp.dma_start(w_[:, :, :], d_.rearrange("(c p) n -> p c n", p=P)).then_inc(s_w, 16)
                for r_, d_ in ((l1, ln1), (l2, ln2)):
                    sp.dma_start(r_[:, :], d_.broadcast_to([P, D])).then_inc(s_w, 16)
                sp.dma_start(rw[:, :], router_w.rearrange("d a -> a d").broadcast_to([P, D])).then_inc(s_w, 16)
                sp.dma_start(rb[:, :], router_b.broadcast_to([P, 1])).then_inc(s_w, 16)
                for t in range(Q):
                    for hh in range(2):
                        n = 2 * t + hh
                        sp.wait_ge(s_mc, 2 * n + 2)
                        dst = cols_dram.rearrange("(u c p) k -> u p c k", u=2, p=P)[hh, :, :, t * P:t * P + P]
                        sp.dma_start(dst, mcol[:, hh, :].rearrange("p (c k) -> p c k", k=P)).then_inc(s_mw[hh], 16)

            @block.gpsimd
            def _(pool):
                for q in range(Q):
                    pool.indirect_dma_start(xs[:, q, :], None, x,
                                            bass.IndirectOffsetOnAxis(ap=idx[:, q:q + 1], axis=0)).then_inc(s_xg, 16)
                pool.wait_ge(s_ci, 1)
                for q in range(Q):
                    pool.indirect_dma_start(pos[:, q:q + 1], None, positions,
                                            bass.IndirectOffsetOnAxis(ap=cidx[:, q:q + 1], axis=0)).then_inc(s_pos, 16)
                pool.memset(ident[:, :], 0.0)
                for c in range(HF):
                    pool.memset(inv[:, c:c + 1], float(freq[c]))
                pool.memset(junk2[:, :], 0.0).then_inc(s_k0, 1)
                pool.wait_ge(s_k0, 1)
                pool.affine_select(out=ident[:, :], in_=ident[:, :], compare_op=ALU.not_equal, fill=1.0,
                                   base=0, pattern=[[-1, P]], channel_multiplier=1).then_inc(s_k, 1)
                for t in range(Q):
                    for hh in range(2):
                        n = 2 * t + hh
                        if t > 0:
                            pool.wait_ge(s_mt, 2 * (n - 2) + 2)
                        pool.indirect_dma_start(mrow[:, hh, :], None, maskT.rearrange("c (u e) -> (c u) e", u=2),
                                                bass.IndirectOffsetOnAxis(ap=c2[:, hh, t:t + 1], axis=0)).then_inc(s_mr[hh], 16)
                for hh in range(2):
                    pool.wait_ge(s_mw[hh], 16 * Q)
                for q in range(Q):
                    pool.indirect_dma_start(msel[:, q, :], None, cols_dram,
                                            bass.IndirectOffsetOnAxis(ap=cidx[:, q:q + 1], axis=0)).then_inc(s_ms, 16)
                pool.wait_ge(s_ms, 16 * Q)

            @block.scalar
            def _(act):
                def masks(t):
                    for hh in range(2):
                        for e in range(2):
                            n = 4 * t + 2 * hh + e
                            act.wait_ge(s_mt, n + 1)
                            if t > 0 and e == 0:
                                act.wait_ge(s_mw[hh], 16 * t)
                            act.activation(mcol[:, hh, e * 512:e * 512 + 512], tb[n % 2][:, :], ACT.Copy).then_inc(s_mc, 1)

                act.wait_ge(s_ang, 1)
                act.activation(sin[:, :, :].rearrange("p q f -> p (q f)"), ang[:, :], ACT.Sin)
                act.activation(cos[:, :, :].rearrange("p q f -> p (q f)"), angc[:, :], ACT.Sin).then_inc(s_sin, 1)
                for t in range(Q):
                    act.wait_ge(s_ht, t + 1)
                    act.activation(hnT[:, :, :], bank[0][:, :].rearrange("p (g k) -> p g k", g=G), ACT.Copy).then_inc(s_hc, 1)
                    act.wait_ge(s_q, 3 * t + 3)
                    act.activation(V[:, t, :], bank[3][:, :], ACT.Copy).then_inc(s_vc, 1)
                    masks(t)
                    cols = slice(t * P, t * P + P)
                    act.wait_ge(s_rt, 2 * t + 1)
                    act.activation(QT[:, :, cols], bank[4][:, :].rearrange("p (g k) -> p g k", g=G), ACT.Copy,
                                   scale=float(INV)).then_inc(s_qt, 1)
                    act.wait_ge(s_rt, 2 * t + 2)
                    act.activation(KT[:, :, cols], bank[5][:, :].rearrange("p (g k) -> p g k", g=G), ACT.Copy)\
                       .then_inc(s_qt, 1)

            @block.vector
            def _(dve):
                done = [0]

                def link(ins):
                    done[0] += 1
                    ins.then_inc(s_st, 1)
                    dve.wait_ge(s_st, done[0])

                link(dve.tensor_scalar(cidx[:, :], idx[:, :], float(C - 1), None, ALU.min))
                link(dve.tensor_scalar(c2[:, 0, :], cidx[:, :], 2.0, None, ALU.mult))
                dve.tensor_scalar(c2[:, 1, :], cidx[:, :], 2.0, 1.0, ALU.mult, ALU.add).then_inc(s_ci, 1)
                dve.wait_ge(s_xg, 16 * Q)
                for q in range(Q):
                    link(dve.bn_stats(stats[:, q, :], xs[:, q, :]))
                    link(dve.bn_aggr(mv[:, q, :], stats[:, q, :]))
                link(dve.tensor_scalar(var[:, :], mv[:, :, 1], 1e-5, None, ALU.add))
                rsqrt(dve, link, rstd[:, :], var[:, :], rt0[:, :])
                dve.wait_ge(s_w, 16 * 7)
                for q in range(Q):
                    link(dve.tensor_scalar(xs[:, q, :], xs[:, q, :], mv[:, q, 0:1], rstd[:, q:q + 1],
                                           ALU.subtract, ALU.mult))
                    link(dve.tensor_tensor_reduce(junk[:, :], xs[:, q, :], rw[:, :], 1.0, 0.0, ALU.mult, ALU.add,
                                                  wsel[:, q:q + 1]))
                    link(dve.tensor_tensor_reduce(junk[:, :], xs[:, q, :], xs[:, q, :], 1.0, 0.0, ALU.mult, ALU.add,
                                                  ms[:, q:q + 1]))
                link(dve.tensor_scalar(wsel[:, :], wsel[:, :], rb[:, 0:1], None, ALU.add))
                link(dve.tensor_scalar(above[:, :], wsel[:, :], thr[:, 0:1], None, ALU.is_gt))
                link(dve.tensor_scalar(ms[:, :], ms[:, :], 1.0 / D, 1e-6, ALU.mult, ALU.add))
                rsqrt(dve, link, rr[:, :], ms[:, :], rt[:, :])
                dve.wait_ge(s_pos, 16 * Q)
                dve.wait_ge(s_k, 1)
                link(dve.tensor_copy(posf[:, :], pos[:, :]))
                a3 = ang[:, :].rearrange("p (q f) -> p q f", q=Q)
                link(dve.tensor_tensor(a3, bc(posf[:, :], HF), bm(inv[:, :], Q), ALU.mult))
                link(dve.tensor_scalar(turn[:, :], ang[:, :], 1.0 / TWO_PI, None, ALU.mult))
                link(dve.tensor_scalar(turn[:, :], turn[:, :], ROUND, -ROUND, ALU.add, ALU.add))
                for c in (C1, C2, C3):
                    link(dve.scalar_tensor_tensor(out=ang[:, :], in0=turn[:, :], scalar=-c, in1=ang[:, :],
                                                  op0=ALU.mult, op1=ALU.add))
                link(dve.tensor_scalar(ang[:, :], ang[:, :], PI, -PI, ALU.min, ALU.max))
                link(dve.tensor_scalar(angc[:, :], ang[:, :], TWO_PI / 4, None, ALU.add))
                link(dve.tensor_scalar(turn[:, :], angc[:, :], PI, -TWO_PI, ALU.is_gt, ALU.mult))
                link(dve.tensor_tensor(angc[:, :], angc[:, :], turn[:, :], ALU.add))
                dve.tensor_scalar(angc[:, :], angc[:, :], PI, -PI, ALU.min, ALU.max).then_inc(s_ang, 1)
                dve.wait_ge(s_sin, 1)
                link(dve.tensor_scalar(nsin[:, :, :], sin[:, :, :], -1.0, None, ALU.mult))
                for t in range(Q):
                    if t > 0:
                        dve.wait_ge(s_ht, t)
                    dve.scalar_tensor_tensor(out=hn[:, :], in0=xs[:, t, :], scalar=rr[:, t:t + 1], in1=l1[:, :],
                                             op0=ALU.mult, op1=ALU.mult).then_inc(s_hn, 1)
                    for n in range(2):
                        dve.wait_ge(s_q, 3 * t + n + 1)
                        if t > 0:
                            dve.wait_ge(s_rt, 2 * t + n - 1)
                        dve.wait_ge(s_r, 2 * t + n)
                        b3 = bank[1 + n][:, :].rearrange("p (h f) -> p h f", f=HF)
                        b4 = bank[1 + n][:, :].rearrange("p (h u f) -> p h u f", u=2, f=HF)
                        q4 = qb[:, :].rearrange("p (h u f) -> p h u f", u=2, f=HF)
                        link(dve.tensor_tensor(qa[:, :].rearrange("p (h f) -> p h f", f=HF), b3,
                                               bm(cos[:, t, :], 2 * H), ALU.mult))
                        link(dve.tensor_tensor(q4[:, :, 0, :], b4[:, :, 1, :], bm(nsin[:, t, :], H), ALU.mult))
                        link(dve.tensor_tensor(q4[:, :, 1, :], b4[:, :, 0, :], bm(sin[:, t, :], H), ALU.mult))
                        dve.tensor_tensor(qr[:, n, :], qa[:, :], qb[:, :], ALU.add).then_inc(s_r, 1)

            @block.tensor
            def _(pe):
                pe.wait_ge(s_k, 1)
                pe.wait_ge(s_w, 16 * 7)

                def masks(t):
                    for hh in range(2):
                        pe.wait_ge(s_mr[hh], 16 * (t + 1))
                        for e in range(2):
                            n = 4 * t + 2 * hh + e
                            if n >= 2:
                                pe.wait_ge(s_mc, n - 1)
                            for c in range(4):
                                o = (4 * e + c) * P
                                ins = pe.transpose(tb[n % 2][:, c * P:c * P + P], mrow[:, hh, o:o + P], ident[:, :])
                            ins.then_inc(s_mt, 1)

                for t in range(Q):
                    pe.wait_ge(s_hn, t + 1)
                    if t > 0:
                        pe.wait_ge(s_hc, t)
                    for g in range(G):
                        ins = pe.transpose(bank[0][:, g * P:g * P + P], hn[:, g * P:g * P + P], ident[:, :])
                    ins.then_inc(s_ht, 1)
                    pe.wait_ge(s_hc, t + 1)
                    if t > 0:
                        pe.wait_ge(s_r, 2 * t)
                        pe.wait_ge(s_vc, t)
                    for n, w_ in enumerate((wq, wk, wv)):
                        for c in range(G):
                            ins = pe.matmul(bank[1 + n][:, :], hnT[:, c, :], w_[:, c, :], start=c == 0, stop=c == G - 1)
                        ins.then_inc(s_q, 1)
                    masks(t)
                    for n in range(2):
                        pe.wait_ge(s_r, 2 * t + n + 1)
                        if t > 0:
                            pe.wait_ge(s_qt, 2 * t + n - 1)
                        for g in range(G):
                            ins = pe.transpose(bank[4 + n][:, g * P:g * P + P], qr[:, n, g * P:g * P + P], ident[:, :])
                        ins.then_inc(s_rt, 1)

        with ExitStack() as c2_:
            junk = sb("junk3", [P, D], c=c2_)
            wo = sb("wo2", [P, G, D], c=c2_)
            qc = sb("qc", [P, G, J, P], c=c2_)
            mc = sb("mc", [P, K], c=c2_)
            Sm = sb("Sm", [P, 2, K], c=c2_)
            mxs = sb("mxs", [P, 2, 2], c=c2_)
            rsum = sb("rsum", [P, H], c=c2_)
            rinv = sb("rinv", [P, H], c=c2_)
            PTs = sb("PTs", [P, 4, Q, P], c=c2_)
            OTs = sb("OTs", [P, G, P], c=c2_)
            On = sb("On", [P, D], c=c2_)
            OnT = sb("OnT", [P, G, P], c=c2_)
            x1c = sb("x1c", [P, D], c=c2_)
            h2 = sb("h2", [P, D], c=c2_)
            m1 = sb("m1", [P, 1], c=c2_)
            v1 = sb("v1", [P, 1], c=c2_)
            r1 = sb("r1", [P, 1], c=c2_)
            t1 = sb("t1", [P, 1], c=c2_)
            Sp = [c2_.enter_context(nc.psum_tensor(f"Sp{i}", [P, 1024], F32)) for i in range(2)]
            Tp = [c2_.enter_context(nc.psum_tensor(f"Tp{i}", [P, 512], F32)) for i in range(2)]
            Op = c2_.enter_context(nc.psum_tensor("Op", [P, 512], F32))
            Wp = c2_.enter_context(nc.psum_tensor("Wp", [P, 512], F32))

            s_w = sem("s_w3", c2_)
            s_alone = sem("s_alone", c2_)
            s_alone_pool = sem("s_alone_pool", c2_)
            s_q0 = sem("s_q0", c2_)
            s_qc = sem("s_qc", c2_)
            s_s = sem("s_s", c2_)
            s_sm = sem("s_sm", c2_)
            s_e = sem("s_e", c2_)
            s_t = sem("s_t", c2_)
            s_ta = sem("s_ta", c2_)
            s_td = sem("s_td", c2_)
            s_pv = sem("s_pv2", c2_)
            s_oc = sem("s_oc", c2_)
            s_on = sem("s_on", c2_)
            s_or = sem("s_or", c2_)
            s_ot = sem("s_ot", c2_)
            s_otc = sem("s_otc", c2_)
            s_wo = sem("s_wo", c2_)
            s_h2 = sem("s_h2", c2_)
            s_h2t = sem("s_h2t", c2_)
            s_x1 = sem("s_x1", c2_)
            s_dv = sem("s_dv", c2_)
            KC = K - 1

            block = c2_.enter_context(nc.Block())

            @block.sync
            def _(sp):
                sp.dma_start(wo[:, :, :], wo_d.rearrange("(c p) n -> p c n", p=P)).then_inc(s_w, 16)

            @block.gpsimd
            def _(pool):
                pool.memset(qc[:, :, :, :], 0.0).then_inc(s_q0, 1)
                pool.wait_ge(s_q0, 1)
                with pool.Fori(0, Q) as t:
                    pool.wait_ge(s_sm, t * H + 1)
                    alone(pool, s_alone_pool)
                    for j in range(J):
                        r = slice(DK * j, DK * j + DK)
                        pool.tensor_copy(qc[r, :, j, :], QT[r, :, bass.ds(t * P, P)]).then_inc(s_q0, 1)
                        pool.wait_ge(s_q0, t * J + (j + 2))
                        alone(pool, s_alone_pool)
                    pool.tensor_copy(mc[:, :], msel[:, bass.ds(t, 1), :].rearrange("p o k -> p (o k)")).then_inc(s_qc, 1)

            @block.scalar
            def _(act):
                act.sem_inc(s_ta, 1)
                act.sem_inc(s_oc, 1)
                with act.Fori(0, Q) as t:
                    def take_t(h):
                        act.wait_ge(s_t, t * (2 * H) + (2 * h + 1))
                        act.wait_ge(s_pv, t * G + h // 4 + 1)
                        act.activation(PTs[:, h % 4, 0:4, :], Tp[0][:, :].rearrange("p (k q) -> p k q", k=4),
                                       ACT.Copy).then_inc(s_ta, 1)

                    def take_o(g):
                        act.wait_ge(s_pv, t * G + (g + 2))
                        act.activation(OTs[:, g, :], Op[:, 0:P], ACT.Copy).then_inc(s_oc, 1)

                    for h in range(H):
                        act.wait_ge(s_sm, t * H + (h + 2))
                        act.activation(Sm[:, h % 2, 0:KC], Sm[:, h % 2, 0:KC], ACT.Exp, bias=mxs[:, h % 2, 1:2],
                                       accum_out=rsum[:, h:h + 1]).then_inc(s_e, 1)
                        if h > 0:
                            if h > 4 and (h - 1) % 4 == 0:
                                take_o((h - 1) // 4 - 1)
                            take_t(h - 1)
                    take_t(H - 1)
                    take_o(G - 1)
                    act.wait_ge(s_ot, t + 1)
                    act.activation(OnT[:, :, :], Wp[:, :].rearrange("p (g k) -> p g k", g=G), ACT.Copy).then_inc(s_otc, 1)
                    act.wait_ge(s_h2t, t + 1)
                    act.activation(x1T[:, :, bass.ds(t * P, P)], Wp[:, :].rearrange("p (g k) -> p g k", g=G),
                                   ACT.Copy).then_inc(s_x1, 1)

            @block.vector
            def _(dve):
                done = [0]
                LINKS = 33
                dve.sem_inc(s_sm, 1)
                dve.sem_inc(s_td, 1)
                dve.memset(Sm[:, :, KC:K], 0.0)
                with dve.Fori(0, Q) as t:
                    done[0] = 0

                    def link(ins):
                        done[0] += 1
                        ins.then_inc(s_dv, 1)
                        dve.wait_ge(s_dv, t * LINKS + done[0])

                    def take_t(h):
                        dve.wait_ge(s_t, t * (2 * H) + (2 * h + 2))
                        dve.wait_ge(s_pv, t * G + h // 4 + 1)
                        dve.tensor_copy(PTs[:, h % 4, 4:8, :], Tp[1][:, :].rearrange("p (k q) -> p k q", k=4))\
                           .then_inc(s_td, 1)

                    dve.wait_ge(s_qc, t + 1)
                    for h in range(H):
                        dve.wait_ge(s_s, t * H + (h + 1))
                        if h >= 2:
                            dve.wait_ge(s_t, t * (2 * H) + 2 * (h - 1))
                        alone(dve, s_alone)
                        link(dve.tensor_tensor_reduce(Sm[:, h % 2, 0:KC], Sp[h % 2][:, 0:KC], mc[:, 0:KC], 1.0,
                                                      -3.0e38, ALU.add, ALU.max, mxs[:, h % 2, 0:1]))
                        dve.tensor_scalar(mxs[:, h % 2, 1:2], mxs[:, h % 2, 0:1], -1.0, None, ALU.mult)\
                           .then_inc(s_sm, 1)
                        if h > 0:
                            take_t(h - 1)
                    take_t(H - 1)
                    dve.wait_ge(s_e, t * H + H)
                    link(dve.reciprocal(rinv[:, :], rsum[:, :]))
                    dve.wait_ge(s_on, t + 1)
                    dve.tensor_tensor(On[:, :].rearrange("p (h d) -> p h d", h=H),
                                      Wp[:, :].rearrange("p (h d) -> p h d", h=H), bc(rinv[:, :], DK),
                                      ALU.mult).then_inc(s_or, 1)
                    dve.wait_ge(s_wo, t + 1)
                    xt = xs[:, bass.ds(t, 1), :].rearrange("p o d -> p (o d)")
                    link(dve.tensor_tensor(x1c[:, :], Wp[:, :], xt, ALU.add))
                    dve.tensor_copy(xs2[:, bass.ds(t, 1), :].rearrange("p o d -> p (o d)"), x1c[:, :])
                    link(dve.tensor_tensor_reduce(junk[:, :], x1c[:, :], x1c[:, :], 1.0, 0.0, ALU.mult, ALU.add,
                                                  m1[:, :]))
                    link(dve.tensor_scalar(v1[:, :], m1[:, :], 1.0 / D, 1e-6, ALU.mult, ALU.add))
                    rsqrt(dve, link, r1[:, :], v1[:, :], t1[:, :])
                    dve.scalar_tensor_tensor(out=h2[:, :], in0=x1c[:, :], scalar=r1[:, 0:1], in1=l2[:, :],
                                             op0=ALU.mult, op1=ALU.mult).then_inc(s_h2, 1)
                    assert done[0] == LINKS, done[0]

            @block.tensor
            def _(pe):
                pe.sem_inc(s_pv, 1)
                pe.wait_ge(s_w, 16)
                with pe.Fori(0, Q) as t:
                    def score(h):
                        g, j = h // J, h % J
                        if h >= 2:
                            pe.wait_ge(s_sm, t * H + (h - 1) + 1)
                        for u in range(2):
                            n = 512 if u == 0 else KC - 512
                            ins = pe.matmul(Sp[h % 2][:, u * 512:u * 512 + n], qc[:, g, j, :],
                                            KT[:, g, u * 512:u * 512 + n], start=True, stop=True)
                        ins.then_inc(s_s, 1)

                    def turn_p(h):
                        pe.wait_ge(s_e, t * H + (h + 1))
                        pe.wait_ge(s_ta, t * H + h + 1)
                        for k in range(4):
                            ins = pe.transpose(Tp[0][:, k * P:k * P + P], Sm[:, h % 2, k * P:k * P + P], ident[:, :])
                        ins.then_inc(s_t, 1)
                        pe.wait_ge(s_td, t * H + h + 1)
                        for k in range(4, 8):
                            ins = pe.transpose(Tp[1][:, (k - 4) * P:(k - 4) * P + P],
                                               Sm[:, h % 2, k * P:k * P + P], ident[:, :])
                        ins.then_inc(s_t, 1)

                    def values(g):
                        pe.wait_ge(s_ta, t * H + (4 * g + 4) + 1)
                        pe.wait_ge(s_td, t * H + (4 * g + 4) + 1)
                        pe.wait_ge(s_oc, t * G + g + 1)
                        for k in range(Q):
                            n = P if k < Q - 1 else P - 1
                            for j in range(J):
                                r = slice(DK * j, DK * j + DK)
                                h = g * J + j
                                ins = pe.matmul(Op[r, 0:P], V[0:n, k, h * DK:h * DK + DK], PTs[0:n, j, k, :],
                                                start=k == 0, stop=k == Q - 1)
                        ins.then_inc(s_pv, 1)

                    pe.wait_ge(s_qc, t + 1)
                    score(0)
                    score(1)
                    for h in range(H):
                        turn_p(h)
                        if h + 2 < H:
                            score(h + 2)
                        if h % 4 == 3:
                            values(h // 4)
                    pe.wait_ge(s_oc, t * G + G + 1)
                    for g in range(G):
                        ins = pe.transpose(Wp[:, g * P:g * P + P], OTs[:, g, :], ident[:, :])
                    ins.then_inc(s_on, 1)
                    pe.wait_ge(s_or, t + 1)
                    for g in range(G):
                        ins = pe.transpose(Wp[:, g * P:g * P + P], On[:, g * P:g * P + P], ident[:, :])
                    ins.then_inc(s_ot, 1)
                    pe.wait_ge(s_otc, t + 1)
                    for g in range(G):
                        ins = pe.matmul(Wp[:, :], OnT[:, g, :], wo[:, g, :], start=g == 0, stop=g == G - 1)
                    ins.then_inc(s_wo, 1)
                    pe.wait_ge(s_h2, t + 1)
                    for g in range(G):
                        ins = pe.transpose(Wp[:, g * P:g * P + P], h2[:, g * P:g * P + P], ident[:, :])
                    ins.then_inc(s_h2t, 1)
                    pe.wait_ge(s_x1, t + 1)
        mid.close()
        mlp(nc, xs, xs2, x1T, wsel, above, w1_d, w2_d, idx, out)


def mlp(nc, xs, x1, x1T, wsel, above, w1_d, w2_d, idx, out):
    Q = xs.shape[1]
    D = xs.shape[2]
    F = w1_d.shape[1]
    K = Q * P
    G = D // P
    FC = F // P
    HT = K // 2
    QH = Q // 2

    with ExitStack() as ctx:
        def sb(name, shape, dt=F32):
            return ctx.enter_context(nc.sbuf_tensor(name, shape, dt))

        def sem(name):
            return ctx.enter_context(nc.semaphore(name))

        w1 = sb("w1m", [P, G, F])
        w2 = sb("w2m", [P, FC, D])
        GT = sb("GT", [P, FC, HT])
        nab = sb("nab", [P, Q])
        fin = sb("fin", [P, Q, D])
        hb = [ctx.enter_context(nc.psum_tensor(f"hb{i}", [P, 512], F32)) for i in range(4)]
        yb = [ctx.enter_context(nc.psum_tensor(f"yb{i}", [P, 512], F32)) for i in range(2)]

        s_w1 = sem("s_w1m")
        s_w2 = sem("s_w2m")
        s_h = sem("s_hm")
        s_g = sem("s_gm")
        s_y = sem("s_ym")
        s_v = sem("s_vm")
        s_f = sem("s_fm")
        s_t = sem("s_tm2")
        s_o = sem("s_om")

        block = ctx.enter_context(nc.Block())

        @block.sync
        def _(sp):
            sp.dma_start(w1[:, :, :], w1_d.rearrange("(c p) n -> p c n", p=P)).then_inc(s_w1, 16)
            sp.dma_start(w2[:, :, :], w2_d.rearrange("(c p) n -> p c n", p=P)).then_inc(s_w2, 16)

        @block.tensor
        def _(pe):
            pe.wait_ge(s_w1, 16)
            for u in range(2):
                for f in range(FC):
                    n = u * FC + f
                    if n >= 4:
                        pe.wait_ge(s_g, n - 3)
                    for c in range(G):
                        ins = pe.matmul(hb[n % 4][:, :], w1[:, c, f * P:f * P + P], x1T[:, c, u * HT:u * HT + HT],
                                        start=c == 0, stop=c == G - 1)
                    ins.then_inc(s_h, 1)
                if u == 0:
                    pe.wait_ge(s_w2, 16)
                pe.wait_ge(s_g, (u + 1) * FC)
                for q in range(QH):
                    n = u * QH + q
                    if n >= 2:
                        pe.wait_ge(s_t, n - 1)
                    for f in range(FC):
                        ins = pe.matmul(yb[n % 2][:, :], GT[:, f, q * P:q * P + P], w2[:, f, :],
                                        start=f == 0, stop=f == FC - 1)
                    ins.then_inc(s_y, 1)

        @block.scalar
        def _(act):
            for n in range(2 * FC):
                act.wait_ge(s_h, n + 1)
                act.activation(GT[:, n % FC, :], hb[n % 4][:, :], ACT.Gelu_apprx_tanh).then_inc(s_g, 1)

        @block.vector
        def _(dve):
            done = [0]

            def link(ins):
                done[0] += 1
                ins.then_inc(s_v, 1)
                dve.wait_ge(s_v, done[0])

            link(dve.tensor_scalar(nab[:, :], above[:, :], -1.0, None, ALU.mult))
            for q in range(Q):
                dve.wait_ge(s_y, q + 1)
                dve.tensor_tensor(fin[:, q, :], yb[q % 2][:, :], x1[:, q, :], ALU.add).then_inc(s_t, 1)
                dve.wait_ge(s_t, q + 1)
                link(dve.tensor_scalar(fin[:, q, :], fin[:, q, :], wsel[:, q:q + 1], None, ALU.mult))
                dve.scalar_tensor_tensor(out=fin[:, q, :], in0=xs[:, q, :], scalar=nab[:, q:q + 1],
                                         in1=fin[:, q, :], op0=ALU.mult, op1=ALU.add).then_inc(s_f, 1)

        @block.gpsimd
        def _(pool):
            for q in range(Q):
                pool.wait_ge(s_f, q + 1)
                n = P if q < Q - 1 else P - 1
                pool.indirect_dma_start(out, bass.IndirectOffsetOnAxis(ap=idx[0:n, q:q + 1], axis=0),
                                        fin[0:n, q, :], None, compute_op=ALU.add).then_inc(s_o, 16)
            pool.wait_ge(s_o, 16 * Q)


def build(nc, x, wqT, wkT, wvT, woT, beta, maskT, positions, router_w, router_b, wq, wk, wv, wo, w1, w2, ln1, ln2,
          out):
    T = x.shape[0]
    K = T // 8
    list_dram = nc.dram_tensor("chosen_list", [K, 1], U32, kind="Internal").ap()
    cols_dram = nc.dram_tensor("mask_columns", [maskT.shape[0], K], F32, kind="Internal").ap()
    with ExitStack() as ctx:
        w = ctx.enter_context(nc.sbuf_tensor("w", [P, T // P], F32))
        thr = ctx.enter_context(nc.sbuf_tensor("thr", [P, 1], F32))
        idx = ctx.enter_context(nc.sbuf_tensor("idx", [P, K // P], U32))
        infini_attention(nc, x, wqT, wkT, wvT, woT, beta, router_w, router_b, out, w)
        select_tokens(nc, w, thr, idx, K, list_dram)
        feed_forward(nc, x, maskT, positions, router_w, router_b, wq, wk, wv, wo, w1, w2, ln1, ln2, thr, idx, out,
                     cols_dram)


def kernel(**inputs):
    import numpy as _np
    import concourse.bacc as _bacc
    from concourse import mybir as _mybir
    from concourse.bass_utils import run_bass_kernel_spmd as _run

    def attn(name):
        return _np.asarray(inputs["L0_attn_" + name])

    def ffn(name):
        return _np.asarray(inputs["L0_ffn_" + name])

    arrays = {
        "x": attn("x")[0],
        "wqT": attn("W_q").T, "wkT": attn("W_k").T, "wvT": attn("W_v").T, "woT": attn("W_o").T,
        "beta": attn("beta_param")[None],
        "maskT": ffn("attention_mask")[0, 0].T, "positions": ffn("position_ids")[0][:, None],
        "router_w": ffn("router_w"), "router_b": ffn("router_b")[None],
        "wq": ffn("wq"), "wk": ffn("wk"), "wv": ffn("wv"), "wo": ffn("wo"), "w1": ffn("w1"), "w2": ffn("w2"),
        "ln1": ffn("ln1")[None], "ln2": ffn("ln2")[None],
    }
    arrays = {"in_" + k: _np.ascontiguousarray(v) for k, v in arrays.items()}
    nc = _bacc.Bacc("TRN2", target_bir_lowering=False, num_devices=1)
    args = [nc.dram_tensor(k, v.shape, _mybir.dt.from_np(v.dtype), kind="ExternalInput").ap()
            for k, v in arrays.items()]
    rows = arrays["in_x"].shape
    args.append(nc.dram_tensor("out_rows", rows, F32, kind="ExternalOutput").ap())
    build(nc, *args)
    r = _run(nc, [arrays], core_ids=[0])
    return r.results[0]["out_rows"][None]
```

```python
from contextlib import ExitStack

import numpy as np

import concourse.bass as bass
from concourse import mybir

F32 = mybir.dt.float32
F32R = mybir.dt.float32r
BF16 = mybir.dt.bfloat16
I32 = mybir.dt.int32
U32 = mybir.dt.uint32
ALU = mybir.AluOpType
ACT = mybir.ActivationFunctionType
AX = mybir.AxisListType



def alone(eng, sem):
    eng.sem_inc(sem, 1)


P = 128
NEG = -1.0e30
MAGIC = 1597463007.0


def bc(t, n):
    return t.rearrange("p (m o) -> p m o", o=1).broadcast_to([t.shape[0], t.shape[1], n])


def bm(t, m):
    return t.rearrange("p (o n) -> p o n", o=1).broadcast_to([t.shape[0], m, t.shape[1]])


def infini_attention(nc, x, wqT, wkT, wvT, woT, beta, router_w, router_b, out, wcol):
    T, D = x.shape
    H = beta.shape[1]
    DK = D // H
    SEG = 64
    G = D // P
    J = P // DK
    TILES = 2
    SEGS = 4
    BT = TILES * P
    NB = T // BT
    VW = DK + 1
    SCALE = float(DK) ** -0.5

    with ExitStack() as ctx:
        def sb(name, shape, dt=F32):
            return ctx.enter_context(nc.sbuf_tensor(name, shape, dt))

        def sem(name):
            return ctx.enter_context(nc.semaphore(name))

        wq, wk, wv, wo = [(sb(f"{n}_high", [P, G, D], F32R), sb(f"{n}_low", [P, G, D], F32R))
                          for n in ("wq", "wk", "wv", "wo")]
        rw = sb("rw", [P, D])
        rb = sb("rb", [P, 1])
        ident = sb("ident", [P, P])
        identb = sb("identb", [P, P], BF16)
        causal = sb("causal", [P, SEG], BF16)
        headmask = sb("headmask", [P, J])
        bt = sb("bt", [P, H])
        be = sb("be", [P, H])
        bs = sb("bs", [P, H])
        betas = sb("betas", [P, H])
        omb = sb("omb", [P, J, G])
        xin = sb("xin", [P, 2, TILES, D])
        xn = sb("xn", [P, 2, TILES, D])
        xu = sb("xu", [P, 2, TILES, D])
        junk = sb("junk", [P, D])
        stats = sb("stats", [P, TILES, 6])
        mv = sb("mv", [P, TILES, 2])
        var = sb("var", [P, TILES])
        rstd = sb("rstd", [P, TILES])
        nwt = sb("nwt", [P, TILES])
        rs1 = sb("rs1", [P, 2, TILES])
        nmr = sb("nmr", [P, 2, TILES])
        wt = sb("wt", [P, TILES])
        xnT = (sb("xnT_high", [P, G, BT], F32R), sb("xnT_low", [P, G, BT], F32R))
        QT = sb("QT", [P, 2, G, BT])
        KT = sb("KT", [P, 2, G, BT])
        SQT = sb("SQT", [P, 2, G, BT])
        SKT = sb("SKT", [P, G, BT])
        ET = sb("ET", [P, 2, 2, BT])
        RT = sb("RT", [P, 2, 2, BT])
        SK = sb("SK", [P, 2, TILES, D])
        DV = sb("DV", [P, 2, TILES, 2, H, VW])
        VS = sb("VS", [P, 2, TILES, H, VW])
        ksum = sb("ksum", [P, G, SEGS])
        Z = sb("Z", [P, 2, SEGS + 1, G])
        Zbd = sb("Zbd", [P, 2, SEGS, G, J])
        den = sb("den", [P, 2, 2 * TILES * H])
        rden = sb("rden", [P, 2, 2 * TILES * H])
        w2 = sb("w2", [P, 2, TILES, H])
        mx = sb("mx", [P, J, G])
        Pq = sb("Pq", [P, J, G, SEG])
        PT = sb("PT", [P, J, G, SEG])
        rl = sb("rl", [P, J, G])
        w1 = sb("w1", [P, J, G])
        T1 = sb("T1", [P, D])
        T2 = sb("T2", [P, D])
        As = sb("As", [P, D])
        AT = (sb("AT_high", [P, G, P], F32R), sb("AT_low", [P, G, P], F32R))
        outt = sb("outt", [P, 2, D])
        NA = sb("NA", [P, 2, G, DK])
        M = sb("M", [P, 2, G, DK])
        Mbd = sb("Mbd", [P, 2, G, P])

        proj = [ctx.enter_context(nc.psum_tensor(f"proj{i}", [P, 512], F32)) for i in range(2)]
        S = ctx.enter_context(nc.psum_tensor("S", [P, J, 512], F32))
        AB = ctx.enter_context(nc.psum_tensor("AB", [P, 2, G, 2, DK], F32))
        AM = ctx.enter_context(nc.psum_tensor("AM", [P, 512], F32))

        s_w = [sem(f"s_w{i}") for i in range(4)]
        s_wh = sem("s_wh")
        s_wl = sem("s_wl")
        s_xh = sem("s_xh")
        s_ah = sem("s_ah")
        s_xu = sem("s_xu")
        s_rows = sem("s_rows")
        s_x = [sem("s_x0"), sem("s_x1")]
        s_alone_pe = sem("s_alone_pe")
        s_alone_dve = sem("s_alone_dve")
        s_c0 = sem("s_c0")
        s_const = sem("s_const")
        s_beta = sem("s_beta")
        s_be = sem("s_be")
        s_dve = sem("s_dve")
        s_ln = sem("s_ln")
        s_full = [sem("s_full0"), sem("s_full1")]
        s_free = [sem("s_free0"), sem("s_free1")]
        s_sq = sem("s_sq")
        s_sk = sem("s_sk")
        s_zbd = sem("s_zbd")
        s_dsk = sem("s_dsk")
        s_vs = [sem("s_vs0"), sem("s_vs1")]
        s_S = sem("s_S")
        s_sub = sem("s_sub")
        s_exp = sem("s_exp")
        s_pt = sem("s_pt")
        s_pv = sem("s_pv")
        s_ab = sem("s_ab")
        s_na = sem("s_na")
        s_tm = sem("s_tm")
        s_m = sem("s_m")
        s_mbd = sem("s_mbd")
        s_am = sem("s_am")
        s_t2 = sem("s_t2")
        s_t1 = sem("s_t1")
        s_as = sem("s_as")
        s_od = sem("s_od")
        s_of = sem("s_of")

        ORDER = (["AST1", "OUT1", "KT0", "KT1", "OUT0", "SK0", "DEN", "XT1"],
                 ["QT0", "QT1", "AST0", "V0", "V1", "SK1", "XT0"])
        FIRST = (["XF0", "KT0", "KT1", "SK0", "DEN", "XT1"],
                 ["XF1", "QT0", "QT1", "V0", "V1", "SK1", "XT0"])

        def order(m, b):
            skip = ()
            if m == 0:
                skip = ("AST1", "OUT1")
            if m == NB - 2:
                skip = ("XT0", "XT1")
            if m >= NB - 1:
                return [u for u in ORDER[b] if u in (("AST1", "OUT1") if m == NB else STAGE2)]
            return [u for u in ORDER[b] if u not in skip]

        STAGE2 = ("AST0", "OUT0", "AST1", "OUT1")

        def use(name, m):
            if m is None:
                b = 0 if name in FIRST[0] else 1
                return b, FIRST[b].index(name)
            b = 0 if name in ORDER[0] else 1
            if isinstance(m, int):
                return b, len(FIRST[b]) + sum(len(order(k, b)) for k in range(m)) + order(m, b).index(name)
            before = len(FIRST[b]) + len(order(0, b)) - len(ORDER[b])
            return b, m * len(ORDER[b]) + (before + ORDER[b].index(name))

        def take(eng, name, m):
            b, k = use(name, m)
            if not (isinstance(k, int) and k == 0):
                eng.wait_ge(s_free[b], k)
            return proj[b], s_full[b]

        def got(eng, name, m):
            b, k = use(name, m)
            eng.wait_ge(s_full[b], k + 1)
            return proj[b], s_free[b]

        def moved(eng, name, m):
            b, k = use(name, m)
            eng.wait_ge(s_free[b], k + 1)

        x_t = x.rearrange("(n a p) d -> n p a d", a=TILES, p=P)
        out_t = out.rearrange("(n p) d -> n p d", p=P)
        halves = [(32 * 0, 32 * 1), (32 * 2, 32 * 3)]
        PAIRS = NB // 2 - 1
        assert NB == 2 * PAIRS + 2 and PAIRS > 1
        raw_weights = ((QT, wq), (KT, wk), (SQT, wv), (SK, wo))

        block = ctx.enter_context(nc.Block())

        @block.sync
        def _(sp):
            sp.sem_inc(s_of, 2)
            for n in range(2):
                sp.dma_start(xin[:, n, :, :], x_t[n]).then_inc(s_x[n], 16)
            for n, d in enumerate((wqT, wkT, wvT, woT)):
                sp.dma_start(raw_weights[n][0][:, :, :, :].rearrange("p a b n -> p (a b n)")
                             .rearrange("p (c n) -> p c n", c=G),
                             d.rearrange("(c p) n -> p c n", p=P)).then_inc(s_w[n], 16)

            def shift_v(m, p):
                moved(sp, "V1", m)
                for src, dst in halves:
                    sp.dma_start(VS[dst:dst + 32, p, :, :, :], DV[src:src + 32, p, :, 1, :, :]).then_inc(s_vs[p], 16)

            def store(h, n, a, name):
                moved(sp, name, h)
                sp.dma_start(out_t[n], outt[:, a, :]).then_inc(s_od, 16)
                sp.wait_ge(s_od, n * 16 + 16)
                sp.sem_inc(s_of, 1)

            def half(m, p, first=False, ln=True, stage1=True):
                if ln:
                    sp.wait_ge(s_xu, m + 1)
                    sp.dma_start(xin[:, p, :, :], x_t[m + 2]).then_inc(s_x[p], 16)
                if not first:
                    store(m, m * 2 - 1, 1, "OUT1")
                store(m, m * 2, 0, "OUT0")
                if stage1:
                    shift_v(m, 1 - p)

            shift_v(None, 0)
            half(0, 0, first=True)
            half(1, 1)
            with sp.Fori(1, PAIRS) as i:
                half(i * 2, 0)
                half(i * 2 + 1, 1)
            half(NB - 2, 0, ln=False)
            half(NB - 1, 1, ln=False, stage1=False)
            store(NB, 2 * NB - 1, 1, "OUT1")
            sp.wait_ge(s_od, 32 * NB)

        @block.gpsimd
        def _(pool):
            pool.dma_start(rw[:, :], router_w.rearrange("d a -> a d").broadcast_to([P, D])).then_inc(s_rows, 16)
            pool.dma_start(rb[:, :], router_b.broadcast_to([P, 1])).then_inc(s_rows, 16)
            pool.dma_start(bt[:, :], beta.broadcast_to([P, H])).then_inc(s_rows, 16)
            pool.sem_inc(s_as, 1)
            pool.sem_inc(s_mbd, 1)
            pool.memset(ident[:, :], 0.0)
            pool.memset(identb[:, :], 0.0)
            pool.memset(causal[:, :], 0.0)
            pool.memset(headmask[:, :], 0.0)
            pool.memset(Z[:, :, :, :], 0.0)
            pool.memset(M[:, :, :, :], 0.0)
            pool.memset(Mbd[:, :, :, :], 0.0)
            for p in range(2):
                for a in range(TILES):
                    pool.memset(DV[:, p, a, 1, :, DK:VW], 1.0)
            pool.memset(junk[:, :], 0.0).then_inc(s_c0, 1)
            pool.wait_ge(s_c0, 1)
            for t in (ident, identb):
                pool.affine_select(out=t[:, :], in_=t[:, :], compare_op=ALU.not_equal, fill=1.0,
                                   base=0, pattern=[[-1, P]], channel_multiplier=1)
            step = 1
            for q in (0, SEG):
                pool.memset(junk[:, 0:1], 0.0).then_inc(s_c0, 1)
                step += 1
                pool.wait_ge(s_c0, step)
                pool.affine_select(out=causal[q:q + SEG, :], in_=causal[q:q + SEG, :], compare_op=ALU.is_ge,
                                   fill=NEG, base=0, pattern=[[-1, SEG]], channel_multiplier=1).then_inc(s_c0, 1)
                step += 1
                pool.wait_ge(s_c0, step)
            for j in range(J):
                pool.memset(headmask[DK * j:DK * j + DK, j:j + 1], 1.0).then_inc(s_c0, 1)
                step += 1
                pool.wait_ge(s_c0, step)
            pool.memset(junk[:, :], 0.0).then_inc(s_const, 1)
            pool.wait_ge(s_const, 1)

            def diagonal(s_no, b):
                pool.wait_ge(s_m, s_no + 2)
                for g in range(G):
                    ins = pool.tensor_tensor(Mbd[:, 1 - b, g, :].rearrange("p (j d) -> p j d", j=J),
                                             bm(M[:, 1 - b, g, :], J), bc(headmask[:, :], DK), ALU.mult)
                ins.then_inc(s_mbd, 1)

            def rows(n2, m, a):
                pool.wait_ge(s_t2, n2 + 2)
                pool.wait_ge(s_t1, n2 + 2)
                pool.tensor_tensor(As[:, :], T1[:, :], T2[:, :], ALU.add).then_inc(s_as, 1)
                pool.wait_ge(s_as, n2 + 2)

            def half(m):
                for a in range(TILES):
                    for b in range(2):
                        diagonal(m * SEGS + (2 * a + b), b)
                    rows(m * 2 + a, m, a)

            half(0)
            half(1)
            with pool.Fori(1, PAIRS) as i:
                half(i * 2)
                half(i * 2 + 1)
            half(NB - 2)
            half(NB - 1)

        @block.scalar
        def _(act):
            act.wait_ge(s_rows, 16 * 3)
            act.activation(be[:, :], bt[:, :], ACT.Exp, scale=-1.0).then_inc(s_be, 1)

            def copy(dst, src):
                return act.activation(dst, src, ACT.Copy)

            for n, (raw, (high, _)) in enumerate(raw_weights):
                act.wait_ge(s_w[n], 16)
                copy(high[:, :, :].rearrange("p c n -> p (c n)"),
                     raw[:, :, :, :].rearrange("p a b n -> p (a b n)")).then_inc(s_wh, 1)

            def xT(m, name, k):
                bank, _ = got(act, f"{name}{k}", m)
                copy(xnT[0][:, 2 * k:2 * k + 2, :], bank[:, :].rearrange("p (c t) -> p c t", c=2)).then_inc(s_xh, 1)

            def feature(m, k, name, raw, pn, scale, s_used):
                bank, free = got(act, f"{name}{k}", m)
                v = bank[:, :].rearrange("p (c t) -> p c t", c=2)
                act.activation(raw[:, pn, 2 * k:2 * k + 2, :], v, ACT.Copy, scale=scale)
                if s_used is not None:
                    act.wait_ge(*s_used)
                act.activation(ET[:, k, :, :], v, ACT.Exp)
                act.activation(RT[:, k, :, :], v, ACT.Relu).then_inc(free, 1)

            def v_tile(m, pn, a):
                bank, free = got(act, f"V{a}", m)
                copy(DV[:, pn, a, 1, :, 0:DK], bank[:, :].rearrange("p (h d) -> p h d", h=H)).then_inc(free, 1)

            def sk_tile(m, pn, a):
                bank, free = got(act, f"SK{a}", m)
                copy(SK[:, pn, a, :], bank[:, :]).then_inc(free, 1)

            def prob(m, a):
                act.wait_ge(s_sub, m * 2 + (a + 1))
                act.activation(Pq[:, :, :, :], Pq[:, :, :, :], ACT.Exp).then_inc(s_exp, 1)

            def neg_a(m, sg):
                act.wait_ge(s_ab, m * SEGS + (sg + 1))
                copy(NA[:, sg % 2, :, :], AB[:, sg % 2, :, 0, :]).then_inc(s_na, 1)

            def a_t(h, a):
                bank, _ = got(act, f"AST{a}", h)
                copy(AT[0][:, :, :], bank[:, :].rearrange("p (g t) -> p g t", g=G)).then_inc(s_ah, 1)

            def half(m, p, first=False, ln=True, stage1=True):
                pn = 1 - p
                if not first:
                    a_t(m, 1)
                prob(m, 0)
                if stage1:
                    feature(m, 0, "QT", QT, pn, SCALE, (s_sk, m * 2 + 1))
                neg_a(m, 0)
                if stage1:
                    feature(m, 1, "QT", QT, pn, SCALE, (s_sk, m * 2 + 2))
                neg_a(m, 1)
                if stage1:
                    feature(m, 0, "KT", KT, pn, 1.0, (s_sq, m * 2 + 3))
                a_t(m, 0)
                prob(m, 1)
                if stage1:
                    feature(m, 1, "KT", KT, pn, 1.0, (s_sq, m * 2 + 4))
                neg_a(m, 2)
                if stage1:
                    v_tile(m, pn, 0)
                    v_tile(m, pn, 1)
                neg_a(m, 3)
                if stage1:
                    sk_tile(m, pn, 0)
                    sk_tile(m, pn, 1)
                if ln:
                    xT(m, "XT", 0)
                    xT(m, "XT", 1)

            xT(None, "XF", 0)
            xT(None, "XF", 1)
            for k in range(2):
                feature(None, k, "QT", QT, 0, SCALE, None)
            for k in range(2):
                feature(None, k, "KT", KT, 0, 1.0, (s_sq, k + 1))
            v_tile(None, 0, 0)
            v_tile(None, 0, 1)
            sk_tile(None, 0, 0)
            sk_tile(None, 0, 1)
            xT(None, "XT", 0)
            xT(None, "XT", 1)
            half(0, 0, first=True)
            half(1, 1)
            with act.Fori(1, PAIRS) as i:
                half(i * 2, 0)
                half(i * 2 + 1, 1)
            half(NB - 2, 0, ln=False)
            half(NB - 1, 1, ln=False, stage1=False)
            a_t(NB, 1)

        @block.vector
        def _(dve):
            done = [0]
            base = [0]

            def link(ins):
                done[0] += 1
                ins.then_inc(s_dve, 1)
                dve.wait_ge(s_dve, base[0] + done[0])

            def statistics(nh, p):
                dve.wait_ge(s_x[p], (nh + 1) * 16)
                for a in range(TILES):
                    ins = dve.bn_stats(stats[:, a, :], xin[:, p, a, :])
                    if a == TILES - 1:
                        link(ins)
                    else:
                        ins.then_inc(s_dve, 1)
                        done[0] += 1
                alone(dve, s_alone_dve)
                for a in range(TILES):
                    ins = dve.bn_aggr(mv[:, a, :], stats[:, a, :])
                    if a == TILES - 1:
                        link(ins)
                    else:
                        ins.then_inc(s_dve, 1)
                        done[0] += 1

            def deviation():
                link(dve.tensor_scalar(var[:, :], mv[:, :, 1], 1e-5, None, ALU.add))
                rsqrt(dve, link, rstd[:, :], var[:, :], nwt[:, :])

            def normalise(n, p):
                for a in range(TILES):
                    ins = dve.tensor_scalar(xn[:, p, a, :], xin[:, p, a, :], mv[:, a, 0:1], rstd[:, a:a + 1],
                                            ALU.subtract, ALU.mult)
                ins.then_inc(s_ln, 1)
                dve.scalar_tensor_tensor(out=nmr[:, p, :], in0=mv[:, :, 0], scalar=-1.0, in1=rstd[:, :],
                                         op0=ALU.mult, op1=ALU.mult)
                link(dve.tensor_scalar(rs1[:, p, :], rstd[:, :], 1.0, None, ALU.add))

            def residual(p):
                for a in range(TILES):
                    ins = dve.tensor_scalar(xu[:, p, a, :], xin[:, p, a, :], rs1[:, p, a:a + 1],
                                            nmr[:, p, a:a + 1], ALU.mult, ALU.add)
                ins.then_inc(s_xu, 1)

            def low_x(m, n2, name, k):
                bank, free = got(dve, f"{name}{k}", m)
                dve.wait_ge(s_xh, n2 + (k + 1))
                dve.tensor_tensor(xnT[1][:, 2 * k:2 * k + 2, :], bank[:, :].rearrange("p (c t) -> p c t", c=2),
                                  xnT[0][:, 2 * k:2 * k + 2, :].bitcast(F32), ALU.subtract).then_inc(free, 1)

            def low_a(h, n, a):
                bank, free = got(dve, f"AST{a}", h)
                dve.wait_ge(s_ah, n + 1)
                dve.tensor_tensor(AT[1][:, :, :], bank[:, :].rearrange("p (g t) -> p g t", g=G),
                                  AT[0][:, :, :].bitcast(F32), ALU.subtract).then_inc(free, 1)

            def sigma(m, name, k, dst, s_done):
                moved(dve, f"{name}{k}", m)
                dve.scalar_tensor_tensor(out=dst, in0=ET[:, k, :, :], scalar=1.0, in1=RT[:, k, :, :],
                                         op0=ALU.min, op1=ALU.add).then_inc(s_done, 1)

            def z_chain(n, n2, pn):
                dve.wait_ge(s_sk, n2 + 2)
                link(dve.tensor_reduce(ksum[:, :, :], SKT[:, :, :].rearrange("p g (s t) -> p g s t", s=SEGS),
                                       AX.X, ALU.add))
                link(dve.tensor_copy(Z[:, pn, 0, :], Z[:, 1 - pn, SEGS, :]))
                for s in range(SEGS):
                    link(dve.tensor_tensor(Z[:, pn, s + 1, :], Z[:, pn, s, :], ksum[:, :, s], ALU.add))
                sg = SEGS * G
                dve.tensor_tensor(Zbd[:, pn, :, :, :].rearrange("p s g j -> p (s g) j"),
                                  Z[:, pn, 0:SEGS, :].rearrange("p s (g o) -> p (s g) o", o=1).broadcast_to([P, sg, J]),
                                  headmask[:, :].rearrange("p (o j) -> p o j", o=1).broadcast_to([P, sg, J]),
                                  ALU.mult).then_inc(s_zbd, 1)

            def denominators(m, n2, pn):
                bank, free = got(dve, "DEN", m)
                N = 2 * TILES * H
                for b in range(2):
                    r = slice(b * SEG, b * SEG + SEG)
                    ins = dve.tensor_scalar(den[r, pn, :].rearrange("p (n j) -> p n j", j=J),
                                            bank[r, 0:2 * N].rearrange("p (n b j) -> p n b j", b=2, j=J)[:, :, b, :],
                                            1e-6, None, ALU.add)
                ins.then_inc(free, 1)
                moved(dve, "DEN", m)
                link(dve.reciprocal(rden[:, pn, :], den[:, pn, :]))
                link(dve.tensor_tensor(w2[:, pn, :, :], rden[:, pn, TILES * H:N].rearrange("p (a h) -> p a h", a=TILES),
                                  betas[:, :].rearrange("p (o h) -> p o h", o=1).broadcast_to([P, TILES, H]), ALU.mult))
                for a in range(TILES):
                    moved(dve, f"SK{a}", m)
                    dve.scalar_tensor_tensor(
                        out=DV[:, pn, a, 0, :, 0:DK], in0=SK[:, pn, a, :].rearrange("p (h d) -> p h d", h=H),
                        scalar=-1.0,
                        in1=rden[:, pn, a * H:a * H + H].rearrange("p (h o) -> p h o", o=1).broadcast_to([P, H, DK]),
                        op0=ALU.mult, op1=ALU.mult).then_inc(s_dsk, 1)

            def s_half(a):
                return S[:, :, a * 256:a * 256 + 256].rearrange("p j (g k) -> p j g k", g=G)

            def softmax_in(m, a):
                dve.wait_ge(s_S, m * 2 + (a + 1))
                link(dve.tensor_reduce(mx[:, :, :], s_half(a), AX.X, ALU.max))
                dve.tensor_tensor(Pq[:, :, :, :], s_half(a),
                                  mx[:, :, :].rearrange("p j (g o) -> p j g o", o=1).broadcast_to([P, J, G, SEG]),
                                  ALU.subtract).then_inc(s_sub, 1)

            def p_transpose(m, a):
                dve.wait_ge(s_exp, m * 2 + (a + 1))
                dve.transpose(PT[:, :, :, :].rearrange("p j g k -> p (j g k)"),
                              Pq[:, :, :, :].rearrange("p j g k -> p (j g k)")).then_inc(s_pt, 1)

            def m_next(m, sg):
                b = sg % 2
                dve.wait_ge(s_tm, m * SEGS + (sg + 1))
                dve.tensor_tensor(M[:, 1 - b, :, :], AB[:, b, :, 1, :], M[:, b, :, :], ALU.add).then_inc(s_m, 1)

            def softmax_part(m, a):
                dve.wait_ge(s_pv, m * 2 + (a + 1))
                dve.wait_ge(s_as, m * 2 + a + 1)
                O = S[:, :, a * 256:a * 256 + G * VW].rearrange("p j (g d) -> p j g d", g=G)
                link(dve.reciprocal(rl[:, :, :].rearrange("p j (g o) -> p j g o", o=1), O[:, :, :, DK:VW]))
                link(dve.tensor_tensor(w1[:, :, :], rl[:, :, :], omb[:, :, :], ALU.mult))
                dve.tensor_tensor(T1[:, :].rearrange("p (g j d) -> p j g d", g=G, j=J), O[:, :, :, 0:DK],
                                  w1[:, :, :].rearrange("p j (g o) -> p j g o", o=1).broadcast_to([P, J, G, DK]),
                                  ALU.mult).then_inc(s_t1, 1)

            def memory_part(m, p, a):
                dve.wait_ge(s_am, m * SEGS + (2 * a + 2))
                dve.tensor_tensor(T2[:, :].rearrange("p (h d) -> p h d", h=H),
                                  AM[:, :].rearrange("p (h d) -> p h d", h=H),
                                  w2[:, p, a, :].rearrange("p (h o) -> p h o", o=1).broadcast_to([P, H, DK]),
                                  ALU.mult).then_inc(s_t2, 1)

            def out_rows(h, n, p, a):
                bank, free = got(dve, f"OUT{a}", h)
                dve.wait_ge(s_of, n + 1)
                dve.tensor_tensor(outt[:, a, :], bank[:, :], xu[:, p, a, :], ALU.add).then_inc(free, 1)

            def router(p, col):
                for a in range(TILES):
                    link(dve.tensor_tensor_reduce(junk[:, :], xn[:, p, a, :], rw[:, :], 1.0, 0.0, ALU.mult, ALU.add,
                                                  wt[:, a:a + 1]))
                link(dve.tensor_copy(col, wt[:, :]))

            def half(m, i, p, first=False, ln=True, stage1=True):
                pn = 1 - p
                n2 = (m + 1) * 2 if stage1 else None
                softmax_in(m, 0)
                if not first:
                    low_a(m, m * 2 - 1, 1)
                p_transpose(m, 0)
                if stage1:
                    sigma(m, "QT", 0, SQT[:, pn, 0:2, :], s_sq)
                if not first:
                    out_rows(m, m * 2 - 1, pn, 1)
                    if stage1:
                        moved(dve, "OUT1", m)
                if stage1:
                    sigma(m, "QT", 1, SQT[:, pn, 2:4, :], s_sq)
                m_next(m, 0)
                if stage1:
                    residual(pn)
                if ln:
                    statistics(i + 1, p)
                softmax_part(m, 0)
                if stage1:
                    sigma(m, "KT", 0, SKT[:, 0:2, :], s_sk)
                m_next(m, 1)
                memory_part(m, p, 0)
                softmax_in(m, 1)
                low_a(m, m * 2, 0)
                p_transpose(m, 1)
                if stage1:
                    sigma(m, "KT", 1, SKT[:, 2:4, :], s_sk)
                if stage1:
                    z_chain(m + 1, n2, pn)
                m_next(m, 2)
                if ln:
                    deviation()
                dve.wait_ge(s_xu, m + 1)
                out_rows(m, m * 2, p, 0)
                softmax_part(m, 1)
                if ln:
                    normalise(m + 2, p)
                m_next(m, 3)
                if stage1:
                    denominators(m, n2, pn)
                if ln:
                    low_x(m, (m + 2) * 2, "XT", 0)
                memory_part(m, p, 1)
                if ln:
                    low_x(m, (m + 2) * 2, "XT", 1)
                if ln:
                    router(p, wcol[:, bass.ds((m + 2) * 2, 2)])

            def low_weights():
                for n, (raw, (high, low)) in enumerate(raw_weights):
                    dve.wait_ge(s_w[n], 16)
                    dve.wait_ge(s_wh, n + 1)
                    dve.tensor_tensor(low[:, :, :].rearrange("p c n -> p (c n)"),
                                      raw[:, :, :, :].rearrange("p a b n -> p (a b n)"),
                                      high[:, :, :].rearrange("p c n -> p (c n)").bitcast(F32),
                                      ALU.subtract).then_inc(s_wl, 1)

            LINKS = 72
            for s in (s_m, s_t1, s_t2):
                dve.sem_inc(s, 1)
            dve.wait_ge(s_const, 1)
            dve.wait_ge(s_rows, 16 * 3)
            dve.wait_ge(s_be, 1)
            link(dve.tensor_scalar(bs[:, :], be[:, :], 1.0, None, ALU.add))
            link(dve.reciprocal(betas[:, :], bs[:, :]))
            link(dve.tensor_scalar(omb[:, :, :].rearrange("p j g -> p g j"),
                                   betas[:, :].rearrange("p (g j) -> p g j", g=G), -1.0, 1.0, ALU.mult, ALU.add))
            for n in range(2):
                statistics(0, n)
                deviation()
                normalise(n, n)
                if n == 0:
                    low_weights()
                    residual(0)
                    low_x(None, 0, "XF", 0)
                    low_x(None, 0, "XF", 1)
                router(n, wcol[:, 2 * n:2 * n + 2])
            for k in range(2):
                sigma(None, "QT", k, SQT[:, 0, 2 * k:2 * k + 2, :], s_sq)
            for k in range(2):
                sigma(None, "KT", k, SKT[:, 2 * k:2 * k + 2, :], s_sk)
            z_chain(0, 0, 0)
            denominators(None, 0, 0)
            low_x(None, 2, "XT", 0)
            low_x(None, 2, "XT", 1)
            half(0, 0, 0, first=True)
            half(1, 0, 1)
            start = done[0]
            with dve.Fori(1, PAIRS) as i:
                done[0] = 0
                base[0] = i * LINKS + (start - LINKS)
                half(i * 2, i, 0)
                half(i * 2 + 1, i, 1)
                assert done[0] == LINKS, done[0]
            base[0] = start + (PAIRS - 1) * LINKS
            done[0] = 0
            half(NB - 2, PAIRS, 0, ln=False)
            half(NB - 1, PAIRS, 1, ln=False, stage1=False)
            low_a(NB, 2 * NB - 1, 1)
            out_rows(NB, 2 * NB - 1, 1, 1)
            dve.tensor_scalar(wcol[:, :], wcol[:, :], rb[:, 0:1], None, ALU.add)

        @block.tensor
        def _(pe):
            def x_transposes(m, n, pn, name, k):
                if k == 0:
                    pe.wait_ge(s_ln, n + 1)
                bank, full = take(pe, f"{name}{k}", m)
                for c in range(2):
                    for a in range(TILES):
                        o = c * BT + a * P
                        ch = 2 * k + c
                        ins = pe.transpose(bank[:, o:o + P], xn[:, pn, a, ch * P:ch * P + P], ident[:, :])
                ins.then_inc(full, 1)

            PARTS = ((0, 0), (0, 1), (1, 0))

            def feature(m, name, w, k, before=None):
                if before is not None:
                    for x in (0, 1):
                        moved(pe, f"{before[0]}{x}", before[1])
                bank, full = take(pe, f"{name}{k}", m)
                for g in range(2):
                    o = (2 * k + g) * P
                    for n, (hx, hw) in enumerate(PARTS):
                        for c in range(G):
                            ins = pe.matmul(bank[:, g * BT:g * BT + BT], w[hw][:, c, o:o + P], xnT[hx][:, c, :],
                                            start=n + c == 0, stop=n == 2 and c == G - 1)
                ins.then_inc(full, 1)

            def values(m, a):
                bank, full = take(pe, f"V{a}", m)
                for n, (hx, hw) in enumerate(PARTS):
                    for c in range(G):
                        ins = pe.matmul(bank[:, :], xnT[hx][:, c, a * P:a * P + P], wv[hw][:, c, :],
                                        start=n + c == 0, stop=n == 2 and c == G - 1)
                ins.then_inc(full, 1)

            def sk_rows(m, n2, a):
                if a == 0:
                    pe.wait_ge(s_sk, n2 + 2)
                bank, full = take(pe, f"SK{a}", m)
                for g in range(G):
                    ins = pe.transpose(bank[:, g * P:g * P + P], SKT[:, g, a * P:a * P + P], ident[:, :])
                ins.then_inc(full, 1)

            def denominators(m, n, pn):
                pe.wait_ge(s_zbd, n + 1)
                pe.wait_ge(s_sq, n * 2 + 2)
                bank, full = take(pe, "DEN", m)
                for q in range(2):
                    for a in range(TILES):
                        for g in range(G):
                            t = slice(a * P, a * P + P)
                            lhsT = SKT[:, g, t] if q == 0 else SQT[:, pn, g, t]
                            o = ((q * TILES + a) * G + g) * 2 * J
                            ins = pe.matmul(bank[:, o:o + 2 * J].rearrange("p (b j) -> p b j", b=2), lhsT,
                                            Zbd[:, pn, 2 * a:2 * a + 2, g, :], start=True, stop=True)
                ins.then_inc(full, 1)

            def scores(m, p, a):
                pe.wait_ge(s_t1, m * 2 + a + 1)
                for j in range(J):
                    pe.matmul(S[:, j, a * 256:a * 256 + 256].rearrange("p (g k) -> p g k", g=G), identb[:, :],
                              causal[:, :].rearrange("p (o k) -> p o k", o=1).broadcast_to([P, G, SEG]),
                              start=True, stop=False, skip_group_check=True)
                for b in range(2):
                    t = a * P + b * SEG
                    for g in range(G):
                        for j in range(J):
                            q = slice(DK * j, DK * j + DK)
                            o = a * 256 + g * SEG
                            ins = pe.matmul(S[b * SEG:b * SEG + SEG, j, o:o + SEG], QT[q, p, g, t:t + SEG],
                                            KT[q, p, g, t:t + SEG], start=False, stop=(g == G - 1),
                                            skip_group_check=True)
                ins.then_inc(s_S, 1)

            def a_and_b(m, p, sg):
                a, b = sg // 2, sg % 2
                if sg == 0:
                    pe.wait_ge(s_dsk, m * 2 + 2)
                pe.wait_ge(s_m, m * SEGS + sg + 1)
                alone(pe, s_alone_pe)
                t = slice(b * SEG, b * SEG + SEG)
                for g in range(G):
                    for j in range(J):
                        h = g * J + j
                        ins = pe.matmul(AB[DK * j:DK * j + DK, b, g, :, :], SK[t, p, a, h * DK:h * DK + DK],
                                        DV[t, p, a, :, h, 0:DK], start=g == 0, stop=g == G - 1,
                                        skip_group_check=True)
                ins.then_inc(s_ab, 1)

            def t_times_m(m, sg):
                b = sg % 2
                pe.wait_ge(s_na, m * SEGS + (sg + 1))
                alone(pe, s_alone_pe)
                for g in range(G):
                    for j in range(J):
                        q = slice(DK * j, DK * j + DK)
                        ins = pe.matmul(AB[q, b, g, 1, :], NA[q, b, g, :], M[q, b, g, :], start=False,
                                        stop=g == G - 1, skip_group_check=True)
                ins.then_inc(s_tm, 1)

            def memory(m, p, sg):
                a, b = sg // 2, sg % 2
                t = a * P + b * SEG
                pe.wait_ge(s_mbd, m * SEGS + sg + 1)
                if b == 0:
                    pe.wait_ge(s_t2, m * 2 + a + 1)
                for g in range(G):
                    ins = pe.matmul(AM[b * SEG:b * SEG + SEG, g * P:g * P + P], SQT[:, p, g, t:t + SEG],
                                    Mbd[:, b, g, :], start=True, stop=True)
                ins.then_inc(s_am, 1)

            def pv(m, mh, p, a):
                pe.wait_ge(s_pt, m * 2 + (a + 1))
                if a == 0:
                    pe.wait_ge(s_vs[p], (mh + 1) * 32)
                alone(pe, s_alone_pe)
                for g in range(G):
                    for j in range(J):
                        h = g * J + j
                        o = a * 256 + g * VW
                        for q in range(4):
                            r = slice(32 * q, 32 * q + 32)
                            dst = S[r, j, o:o + VW]
                            own = (q % 2) * 32
                            ins = pe.matmul(dst, PT[r, j, g, own:own + 32], DV[r, p, a, 1, h, :],
                                            start=True, stop=q % 2 == 0)
                            if q % 2:
                                ins = pe.matmul(dst, PT[r, j, g, 0:32], VS[r, p, a, h, :], start=False, stop=True)
                ins.then_inc(s_pv, 1)

            def as_transposes(h, n, a):
                pe.wait_ge(s_as, n + 2)
                bank, full = take(pe, f"AST{a}", h)
                for g in range(G):
                    ins = pe.transpose(bank[:, g * P:g * P + P], As[:, g * P:g * P + P], ident[:, :])
                ins.then_inc(full, 1)

            def out_proj(h, a):
                moved(pe, f"AST{a}", h)
                bank, full = take(pe, f"OUT{a}", h)
                for n, (ha, hw) in enumerate(PARTS):
                    for g in range(G):
                        ins = pe.matmul(bank[:, :], AT[ha][:, g, :], wo[hw][:, g, :], start=n + g == 0,
                                        stop=n == 2 and g == G - 1)
                ins.then_inc(full, 1)

            def half(m, mh, p, first=False, ln=True, stage1=True):
                pn = 1 - p
                n = m + 1 if stage1 else None
                n2 = (m + 1) * 2 if stage1 else None
                scores(m, p, 0)
                if not first:
                    as_transposes(m, m * 2 - 1, 1)
                if stage1:
                    if isinstance(m, int):
                        feature(m, "QT", wq, 0, ("XT", None if m == 0 else m - 1))
                    else:
                        feature(m, "QT", wq, 0, ("XT", m - 1))
                a_and_b(m, p, 0)
                if not first:
                    out_proj(m, 1)
                if stage1:
                    feature(m, "QT", wq, 1)
                t_times_m(m, 0)
                memory(m, p, 0)
                pv(m, mh, p, 0)
                a_and_b(m, p, 1)
                if stage1:
                    feature(m, "KT", wk, 0)
                t_times_m(m, 1)
                memory(m, p, 1)
                scores(m, p, 1)
                if stage1:
                    feature(m, "KT", wk, 1)
                as_transposes(m, m * 2, 0)
                a_and_b(m, p, 2)
                if stage1:
                    values(m, 0)
                out_proj(m, 0)
                t_times_m(m, 2)
                memory(m, p, 2)
                pv(m, mh, p, 1)
                if stage1:
                    values(m, 1)
                a_and_b(m, p, 3)
                if stage1:
                    sk_rows(m, n2, 0)
                    sk_rows(m, n2, 1)
                t_times_m(m, 3)
                if stage1:
                    denominators(m, n, pn)
                if ln:
                    x_transposes(m, m + 2, p, "XT", 0)
                memory(m, p, 3)
                if ln:
                    x_transposes(m, m + 2, p, "XT", 1)

            pe.wait_ge(s_const, 1)
            x_transposes(None, 0, 0, "XF", 0)
            x_transposes(None, 0, 0, "XF", 1)
            pe.wait_ge(s_wl, 4)
            feature(None, "QT", wq, 0, ("XF", None))
            feature(None, "QT", wq, 1)
            feature(None, "KT", wk, 0)
            feature(None, "KT", wk, 1)
            values(None, 0)
            values(None, 1)
            sk_rows(None, 0, 0)
            sk_rows(None, 0, 1)
            denominators(None, 0, 0)
            x_transposes(None, 1, 1, "XT", 0)
            x_transposes(None, 1, 1, "XT", 1)
            half(0, 0, 0, first=True)
            half(1, 0, 1)
            with pe.Fori(1, PAIRS) as i:
                half(i * 2, i, 0)
                half(i * 2 + 1, i, 1)
            half(NB - 2, PAIRS, 0, ln=False)
            half(NB - 1, PAIRS, 1, ln=False, stage1=False)
            as_transposes(NB, 2 * NB - 1, 1)
            out_proj(NB, 1)


def select_tokens(nc, w, thr, idx, K, list_dram):
    NT = w.shape[1]
    N = P * NT
    Q = K // P
    BIG = 65536.0
    KNEG = float(N - K + 1)

    with ExitStack() as ctx:
        def sb(name, shape, dt=F32):
            return ctx.enter_context(nc.sbuf_tensor(name, shape, dt))

        def sem(name):
            return ctx.enter_context(nc.semaphore(name))

        onesP = sb("onesP", [P, P])
        before = sb("before", [P, P])
        oneT = sb("oneT", [P, NT])
        hit = sb("hit", [P, NT])
        y = sb("y", [P, NT])
        cnt = sb("cnt", [P, 2])
        flag = sb("flag", [P, 1])
        sign = sb("sign", [P, 1])
        kk = sb("kk", [P, 1])
        bitf = sb("bitf", [P, 1])
        biti = sb("biti", [P, 1], I32)
        cur = sb("cur", [P, 1], I32)
        cand = sb("cand", [P, 1], I32)
        keep = sb("keep", [P, 1], I32)
        lim = sb("lim", [P, 1])
        gt = sb("gt", [P, NT])
        eq = sb("eq", [P, NT])
        chosen = sb("chosen", [P, NT])
        tot = sb("tot", [P, NT])
        run = sb("run", [P, NT])
        place = sb("place", [P, NT])
        away = sb("away", [P, NT])
        dest = sb("dest", [P, NT], U32)
        token = sb("token", [P, NT], U32)
        zero = sb("zero", [P, 1], U32)
        pc = ctx.enter_context(nc.psum_tensor("pc", [P, 512], F32))
        pp = ctx.enter_context(nc.psum_tensor("pp", [P, 512], F32))
        pt = ctx.enter_context(nc.psum_tensor("pt", [P, 512], F32))

        s_k0 = sem("s_k0")
        s_k = sem("s_k")
        s_cnt = sem("s_cnt")
        s_tot = sem("s_tot")
        s_step = sem("s_step")
        s_x = sem("s_mark")
        s_pre = sem("s_pre")
        s_dest = sem("s_dest")
        s_pad = sem("s_pad")
        s_sc = sem("s_scat")
        s_idx = sem("s_idx")

        block = ctx.enter_context(nc.Block())

        @block.gpsimd
        def _(pool):
            pool.memset(onesP[:, :], 1.0)
            pool.memset(oneT[:, :], 1.0)
            pool.memset(zero[:, :], 0)
            pool.iota(token[:, :], pattern=[[P, NT]], base=0, channel_multiplier=1)
            pool.memset(before[:, :], 1.0).then_inc(s_k0, 1)
            pool.wait_ge(s_k0, 1)
            pool.affine_select(out=before[:, :], in_=before[:, :], compare_op=ALU.is_gt, fill=0.0,
                               base=0, pattern=[[1, P]], channel_multiplier=-1).then_inc(s_k, 1)
            pool.wait_ge(s_k, 1)
            pool.dma_start(list_dram[K - 1:K, :], zero[0:1, :]).then_inc(s_pad, 16)
            pool.wait_ge(s_pad, 16)
            pool.wait_ge(s_dest, 1)
            for j in range(NT):
                pool.indirect_dma_start(list_dram, bass.IndirectOffsetOnAxis(ap=dest[:, j:j + 1], axis=0),
                                        token[:, j:j + 1], None, bounds_check=K - 2,
                                        oob_is_err=False).then_inc(s_sc, 16)
            pool.wait_ge(s_sc, 16 * NT)
            pool.dma_start(idx[:, :], list_dram.rearrange("(p q) a -> p (q a)", q=Q)).then_inc(s_idx, 16)
            pool.wait_ge(s_idx, 16)

        @block.tensor
        def _(pe):
            pe.wait_ge(s_k, 1)

            def total(n):
                pe.wait_ge(s_cnt, n + 1)
                pe.matmul(pc[:, 0:2], onesP[:, :], cnt[:, :], start=True, stop=True).then_inc(s_tot, 1)

            total(0)
            with pe.Fori(0, 31) as i:
                total(i + 1)
            total(32)
            for n, x in enumerate((eq, chosen)):
                pe.wait_ge(s_x, n + 1)
                pe.matmul(pp[:, 0:NT], before[:, :], x[:, :], start=True, stop=True)
                pe.matmul(pt[:, 0:NT], onesP[:, :], x[:, :], start=True, stop=True).then_inc(s_pre, 1)

        @block.vector
        def _(dve):
            done = [0]
            base = [0]

            def link(ins):
                done[0] += 1
                ins.then_inc(s_step, 1)
                dve.wait_ge(s_step, base[0] + done[0])

            def count(src, level, op, n, out):
                dve.scalar_tensor_tensor(out=out, in0=src, scalar=level, in1=oneT[:, :], op0=op, op1=ALU.mult,
                                         accum_out=cnt[:, 0:1]).then_inc(s_cnt, 1)
                dve.wait_ge(s_tot, n + 1)

            dve.wait_ge(s_k, 1)
            link(dve.memset(cnt[:, :], 0.0))
            link(dve.memset(cur[:, :], 0))
            link(dve.memset(bitf[:, :], float(2 ** 30)))
            link(dve.memset(biti[:, :], 2 ** 30))
            count(w[:, :], 0.0, ALU.is_ge, 0, hit[:, :])
            link(dve.tensor_scalar(flag[:, :], pc[:, 0:1], float(K), None, ALU.is_ge))
            link(dve.tensor_scalar(sign[:, :], flag[:, :], 2.0, -1.0, ALU.mult, ALU.add))
            link(dve.tensor_scalar(kk[:, :], flag[:, :], float(K) - KNEG, KNEG, ALU.mult, ALU.add))
            link(dve.tensor_scalar(y[:, :], w[:, :], sign[:, 0:1], None, ALU.mult))
            start = done[0]
            LINKS = 5
            with dve.Fori(0, 31) as i:
                done[0] = 0
                base[0] = i * LINKS + start
                link(dve.tensor_tensor(cand[:, :], cur[:, :], biti[:, :], ALU.bitwise_or))
                count(y[:, :], cand[:, 0:1].bitcast(F32), ALU.is_ge, i + 1, hit[:, :])
                link(dve.tensor_scalar(keep[:, :], pc[:, 0:1], kk[:, 0:1], bitf[:, 0:1], ALU.is_ge, ALU.mult))
                link(dve.tensor_tensor(cur[:, :], cur[:, :], keep[:, :], ALU.bitwise_or))
                link(dve.tensor_scalar(bitf[:, :], bitf[:, :], 0.5, None, ALU.mult))
                link(dve.tensor_copy(biti[:, :], bitf[:, :]))
                assert done[0] == LINKS, done[0]
            base[0] = start + 31 * LINKS
            done[0] = 0
            link(dve.tensor_tensor(thr[:, :], cur[:, :].bitcast(F32), sign[:, :], ALU.mult))
            count(w[:, :], thr[:, 0:1], ALU.is_gt, 32, gt[:, :])
            link(dve.tensor_scalar(lim[:, :], pc[:, 0:1], -1.0, float(K - 1), ALU.mult, ALU.add))
            dve.tensor_scalar(eq[:, :], w[:, :], thr[:, 0:1], None, ALU.is_equal).then_inc(s_x, 1)

            def before_each(n):
                dve.wait_ge(s_pre, n + 1)
                link(dve.tensor_copy(tot[:, :], pt[:, 0:NT]))
                link(dve.tensor_tensor_scan(run[:, :], oneT[:, :], tot[:, :], 0.0, ALU.mult, ALU.add))
                link(dve.tensor_tensor(run[:, :], run[:, :], tot[:, :], ALU.subtract))
                link(dve.tensor_tensor(place[:, :], pp[:, 0:NT], run[:, :], ALU.add))

            before_each(0)
            link(dve.scalar_tensor_tensor(out=hit[:, :], in0=place[:, :], scalar=lim[:, 0:1], in1=eq[:, :],
                                          op0=ALU.is_lt, op1=ALU.mult))
            dve.tensor_tensor(chosen[:, :], gt[:, :], hit[:, :], ALU.add).then_inc(s_x, 1)
            dve.wait_ge(s_x, 2)
            before_each(1)
            link(dve.tensor_scalar(away[:, :], chosen[:, :], -BIG, BIG, ALU.mult, ALU.add))
            link(dve.tensor_tensor(place[:, :], place[:, :], chosen[:, :], ALU.mult))
            dve.tensor_tensor(dest[:, :], place[:, :], away[:, :], ALU.add).then_inc(s_dest, 1)


def rsqrt(dve, link, y, v, t):
    link(dve.tensor_scalar(y.bitcast(I32), v.bitcast(I32), -0.5, MAGIC, ALU.mult, ALU.add))
    for _ in range(4):
        link(dve.scalar_tensor_tensor(out=t, in0=y, scalar=-0.5, in1=y, op0=ALU.mult, op1=ALU.mult))
        link(dve.tensor_tensor(t, t, v, ALU.mult))
        link(dve.scalar_tensor_tensor(out=y, in0=t, scalar=1.5, in1=y, op0=ALU.add, op1=ALU.mult))


def feed_forward(nc, x, maskT, positions, router_w, router_b, wq_d, wk_d, wv_d, wo_d, w1_d, w2_d, ln1, ln2,
                 thr, idx, out, cols_dram):
    D = x.shape[1]
    F = w1_d.shape[1]
    C = maskT.shape[0]
    H, DK = 16, 32
    Q = idx.shape[1]
    K = Q * P
    G = D // P
    J = P // DK
    CC = C // P
    FC = F // P
    HF = DK // 2
    INV = 1.0 / np.sqrt(np.float32(DK))
    freq = (np.float32(1.0) / np.float32(10000.0) ** (np.arange(0, DK, 2, dtype=np.float32) / np.float32(DK)))
    TWO_PI = 2.0 * np.pi
    C1 = 6.28125
    C2 = float(np.float32(np.floor((TWO_PI - C1) * 2 ** 20) / 2 ** 20))
    C3 = float(np.float32(TWO_PI - C1 - C2))
    ROUND = 12582912.0
    PI = float(np.nextafter(np.float32(np.pi), np.float32(0)))

    with ExitStack() as ctx:
        def sb(name, shape, dt=F32, c=ctx):
            return c.enter_context(nc.sbuf_tensor(name, shape, dt))

        def sem(name, c=ctx):
            return c.enter_context(nc.semaphore(name))

        ident = sb("ident2", [P, P])
        xs = sb("xs", [P, Q, D])
        wsel = sb("wsel", [P, Q])
        above = sb("above", [P, Q])
        cidx = sb("cidx", [P, Q], U32)
        l2 = sb("l2", [P, D])
        xs2 = sb("xs2", [P, Q, D])
        x1T = sb("x1T", [P, G, K])
        ms = sb("ms", [P, Q])
        rr = sb("rr", [P, Q])
        rt = sb("rt", [P, Q])

        mid = ctx.enter_context(ExitStack())
        qrow = xs2
        KS = sb("KS", [P, H, K], F32R, c=mid)
        V = sb("V2", [P, Q, D], c=mid)
        with ExitStack() as c1:
            wq = sb("wq2", [P, G, D], c=c1)
            wk = sb("wk2", [P, G, D], c=c1)
            wv = x1T[:, 0:2, :].rearrange("p g (a n) -> p (g a) n", n=D)
            mrow = x1T[:, 2:4, :]
            rw = sb("rw2", [P, D], c=c1)
            rb = sb("rb2", [P, 1], c=c1)
            pos = sb("pos", [P, Q], I32, c=c1)
            posf = sb("posf", [P, Q], c=c1)
            l1 = sb("l1", [P, D], c=c1)
            c2 = sb("c2", [P, 2, Q], U32, c=c1)
            inv = sb("inv", [P, HF], c=c1)
            ang = sb("ang", [P, Q * HF], c=c1)
            turn = sb("turn", [P, Q * HF], c=c1)
            angc = sb("angc", [P, Q * HF], c=c1)
            sin = sb("sin", [P, Q, HF], c=c1)
            cos = sb("cos", [P, Q, HF], c=c1)
            coss = sb("coss", [P, 2, Q, HF], c=c1)
            sins = sb("sins", [P, 2, Q, HF], c=c1)
            nsins = sb("nsins", [P, 2, Q, HF], c=c1)
            stats = sb("stats2", [P, Q, 6], c=c1)
            mv = sb("mv2", [P, Q, 2], c=c1)
            var = sb("var2", [P, Q], c=c1)
            rstd = sb("rstd2", [P, Q], c=c1)
            rt0 = sb("rt0", [P, Q], c=c1)
            hn = sb("hn", [P, D], c=c1)
            hnT = sb("hnT", [P, G, P], c=c1)
            qa = sb("qa", [P, D], c=c1)
            junk = qa
            qb = sb("qb", [P, D], c=c1)
            junk2 = sb("junk2", [P, 1], c=c1)
            krow = sb("krow", [P, D], c=c1)
            kst = sb("kst", [P, H, 4, DK], F32R, c=c1)
            mcol = sb("mcol", [P, 2, P * 8], c=c1)
            bank = [c1.enter_context(nc.psum_tensor(f"fb{i}", [P, 512], F32)) for i in range(6)]
            tb = [c1.enter_context(nc.psum_tensor(f"ft{i}", [P, 512], F32)) for i in range(2)]

            s_w = sem("s_w2", c1)
            s_xg = sem("s_xg", c1)
            s_rows = sem("s_rows2", c1)
            s_pos = sem("s_pos", c1)
            s_ci = sem("s_ci", c1)
            s_mr = [sem("s_mr0", c1), sem("s_mr1", c1)]
            s_mt = sem("s_mt", c1)
            s_mc = sem("s_mc", c1)
            s_mw = [sem("s_mw0", c1), sem("s_mw1", c1)]
            s_k0 = sem("s_l0", c1)
            s_k = sem("s_l", c1)
            s_st = sem("s_st", c1)
            s_pool = sem("s_pool", c1)
            s_ang = sem("s_ang", c1)
            s_sin = sem("s_sin", c1)
            s_hn = sem("s_hn", c1)
            s_ht = sem("s_ht", c1)
            s_hc = sem("s_hc", c1)
            s_q = sem("s_q2", c1)
            s_vc = sem("s_vc", c1)
            s_r = sem("s_r", c1)
            s_kh = sem("s_kh", c1)
            s_kl = sem("s_kl", c1)
            s_rt = sem("s_rt", c1)
            s_kt = sem("s_kt", c1)

            block = c1.enter_context(nc.Block())

            @block.sync
            def _(sp):
                for w_, d_ in ((wq, wq_d), (wk, wk_d), (wv, wv_d)):
                    sp.dma_start(w_[:, :, :], d_.rearrange("(c p) n -> p c n", p=P)).then_inc(s_w, 16)
                for r_, d_ in ((l1, ln1), (l2, ln2)):
                    sp.dma_start(r_[:, :], d_.broadcast_to([P, D])).then_inc(s_w, 16)
                sp.dma_start(rw[:, :], router_w.rearrange("d a -> a d").broadcast_to([P, D])).then_inc(s_w, 16)
                sp.dma_start(rb[:, :], router_b.broadcast_to([P, 1])).then_inc(s_w, 16)
                for t in range(Q):
                    for hh in range(2):
                        n = 2 * t + hh
                        sp.wait_ge(s_mc, 2 * n + 2)
                        dst = cols_dram.rearrange("(u c p) k -> u p c k", u=2, p=P)[hh, :, :, t * P:t * P + P]
                        sp.dma_start(dst, mcol[:, hh, :].rearrange("p (c k) -> p c k", k=P)).then_inc(s_mw[hh], 16)

            @block.gpsimd
            def _(pool):
                for q in range(Q):
                    pool.indirect_dma_start(xs[:, q, :], None, x,
                                            bass.IndirectOffsetOnAxis(ap=idx[:, q:q + 1], axis=0)).then_inc(s_xg, 16)
                pool.wait_ge(s_ci, 1)
                for q in range(Q):
                    pool.indirect_dma_start(pos[:, q:q + 1], None, positions,
                                            bass.IndirectOffsetOnAxis(ap=cidx[:, q:q + 1], axis=0)).then_inc(s_pos, 16)
                pool.memset(ident[:, :], 0.0)
                for c in range(HF):
                    pool.memset(inv[:, c:c + 1], float(freq[c]))
                pool.memset(junk2[:, :], 0.0).then_inc(s_k0, 1)
                pool.wait_ge(s_k0, 1)
                pool.affine_select(out=ident[:, :], in_=ident[:, :], compare_op=ALU.not_equal, fill=1.0,
                                   base=0, pattern=[[-1, P]], channel_multiplier=1).then_inc(s_k, 1)
                for t in range(Q):
                    for hh in range(2):
                        n = 2 * t + hh
                        if t > 0:
                            pool.wait_ge(s_mt, 2 * (n - 2) + 2)
                        pool.indirect_dma_start(mrow[:, hh, :], None, maskT.rearrange("c (u e) -> (c u) e", u=2),
                                                bass.IndirectOffsetOnAxis(ap=c2[:, hh, t:t + 1], axis=0)).then_inc(s_mr[hh], 16)
                for hh in range(2):
                    pool.wait_ge(s_mw[hh], 16 * Q)

            def stacked(row):
                return row.rearrange("p (h o d) -> p h o d", o=1, d=DK).broadcast_to([P, H, 2, DK])

            @block.scalar
            def _(act):
                def masks(t):
                    for hh in range(2):
                        for e in range(2):
                            n = 4 * t + 2 * hh + e
                            act.wait_ge(s_mt, n + 1)
                            if t > 0 and e == 0:
                                act.wait_ge(s_mw[hh], 16 * t)
                            act.activation(mcol[:, hh, e * 512:e * 512 + 512], tb[n % 2][:, :], ACT.Copy).then_inc(s_mc, 1)

                act.wait_ge(s_ang, 1)
                act.activation(sin[:, :, :].rearrange("p q f -> p (q f)"), ang[:, :], ACT.Sin)
                act.activation(cos[:, :, :].rearrange("p q f -> p (q f)"), angc[:, :], ACT.Sin).then_inc(s_sin, 1)
                for t in range(Q):
                    act.wait_ge(s_ht, t + 1)
                    act.activation(hnT[:, :, :], bank[0][:, :].rearrange("p (g k) -> p g k", g=G), ACT.Copy).then_inc(s_hc, 1)
                    act.wait_ge(s_q, 3 * t + 3)
                    act.activation(V[:, t, :], bank[3][:, :], ACT.Copy).then_inc(s_vc, 1)
                    masks(t)
                    cols = slice(t * P, t * P + P)
                    act.wait_ge(s_r, 2 * t + 2)
                    act.activation(kst[:, :, 0:4:2, :], stacked(krow[:, :]), ACT.Copy).then_inc(s_kh, 1)
                    for g in range(G):
                        act.wait_ge(s_rt, G * t + g + 1)
                        act.activation(KS[:, 4 * g:4 * g + 4, cols],
                                       bank[4 + g % 2][:, :].rearrange("p (h k) -> p h k", h=4), ACT.Copy)\
                           .then_inc(s_kt, 1)

            @block.vector
            def _(dve):
                done = [0]

                def link(ins):
                    done[0] += 1
                    ins.then_inc(s_st, 1)
                    dve.wait_ge(s_st, done[0])

                link(dve.tensor_scalar(cidx[:, :], idx[:, :], float(C - 1), None, ALU.min))
                link(dve.tensor_scalar(c2[:, 0, :], cidx[:, :], 2.0, None, ALU.mult))
                dve.tensor_scalar(c2[:, 1, :], cidx[:, :], 2.0, 1.0, ALU.mult, ALU.add).then_inc(s_ci, 1)
                dve.wait_ge(s_xg, 16 * Q)
                for q in range(Q):
                    link(dve.bn_stats(stats[:, q, :], xs[:, q, :]))
                    link(dve.bn_aggr(mv[:, q, :], stats[:, q, :]))
                link(dve.tensor_scalar(var[:, :], mv[:, :, 1], 1e-5, None, ALU.add))
                rsqrt(dve, link, rstd[:, :], var[:, :], rt0[:, :])
                dve.wait_ge(s_w, 16 * 7)
                for q in range(Q):
                    link(dve.tensor_scalar(xs[:, q, :], xs[:, q, :], mv[:, q, 0:1], rstd[:, q:q + 1],
                                           ALU.subtract, ALU.mult))
                    link(dve.tensor_tensor_reduce(junk[:, :], xs[:, q, :], rw[:, :], 1.0, 0.0, ALU.mult, ALU.add,
                                                  wsel[:, q:q + 1]))
                    link(dve.tensor_tensor_reduce(junk[:, :], xs[:, q, :], xs[:, q, :], 1.0, 0.0, ALU.mult, ALU.add,
                                                  ms[:, q:q + 1]))
                link(dve.tensor_scalar(wsel[:, :], wsel[:, :], rb[:, 0:1], None, ALU.add))
                link(dve.tensor_scalar(above[:, :], wsel[:, :], thr[:, 0:1], None, ALU.is_gt))
                link(dve.tensor_scalar(ms[:, :], ms[:, :], 1.0 / D, 1e-6, ALU.mult, ALU.add))
                rsqrt(dve, link, rr[:, :], ms[:, :], rt[:, :])
                dve.wait_ge(s_pos, 16 * Q)
                dve.wait_ge(s_k, 1)
                link(dve.tensor_copy(posf[:, :], pos[:, :]))
                a3 = ang[:, :].rearrange("p (q f) -> p q f", q=Q)
                link(dve.tensor_tensor(a3, bc(posf[:, :], HF), bm(inv[:, :], Q), ALU.mult))
                link(dve.tensor_scalar(turn[:, :], ang[:, :], 1.0 / TWO_PI, None, ALU.mult))
                link(dve.tensor_scalar(turn[:, :], turn[:, :], ROUND, -ROUND, ALU.add, ALU.add))
                for c in (C1, C2, C3):
                    link(dve.scalar_tensor_tensor(out=ang[:, :], in0=turn[:, :], scalar=-c, in1=ang[:, :],
                                                  op0=ALU.mult, op1=ALU.add))
                link(dve.tensor_scalar(ang[:, :], ang[:, :], PI, -PI, ALU.min, ALU.max))
                link(dve.tensor_scalar(angc[:, :], ang[:, :], TWO_PI / 4, None, ALU.add))
                link(dve.tensor_scalar(turn[:, :], angc[:, :], PI, -TWO_PI, ALU.is_gt, ALU.mult))
                link(dve.tensor_tensor(angc[:, :], angc[:, :], turn[:, :], ALU.add))
                dve.tensor_scalar(angc[:, :], angc[:, :], PI, -PI, ALU.min, ALU.max).then_inc(s_ang, 1)
                dve.wait_ge(s_sin, 1)
                for n, scale in ((0, float(INV)), (1, 1.0)):
                    dve.tensor_scalar(coss[:, n, :, :], cos[:, :, :], scale, None, ALU.mult)
                    dve.tensor_scalar(sins[:, n, :, :], sin[:, :, :], scale, None, ALU.mult)
                    link(dve.tensor_scalar(nsins[:, n, :, :], sin[:, :, :], -scale, None, ALU.mult))
                for t in range(Q):
                    if t > 0:
                        dve.wait_ge(s_ht, t)
                    dve.scalar_tensor_tensor(out=hn[:, :], in0=xs[:, t, :], scalar=rr[:, t:t + 1], in1=l1[:, :],
                                             op0=ALU.mult, op1=ALU.mult).then_inc(s_hn, 1)
                    for n in range(2):
                        dve.wait_ge(s_q, 3 * t + n + 1)
                        dve.wait_ge(s_r, 2 * t + n)
                        b3 = bank[1 + n][:, :].rearrange("p (h f) -> p h f", f=HF)
                        b4 = bank[1 + n][:, :].rearrange("p (h u f) -> p h u f", u=2, f=HF)
                        q4 = qb[:, :].rearrange("p (h u f) -> p h u f", u=2, f=HF)
                        link(dve.tensor_tensor(qa[:, :].rearrange("p (h f) -> p h f", f=HF), b3,
                                               bm(coss[:, n, t, :], 2 * H), ALU.mult))
                        link(dve.tensor_tensor(q4[:, :, 0, :], b4[:, :, 1, :], bm(nsins[:, n, t, :], H), ALU.mult))
                        link(dve.tensor_tensor(q4[:, :, 1, :], b4[:, :, 0, :], bm(sins[:, n, t, :], H), ALU.mult))
                        dve.tensor_tensor(qrow[:, t, :] if n == 0 else krow[:, :], qa[:, :], qb[:, :],
                                          ALU.add).then_inc(s_r, 1)
                    dve.wait_ge(s_kh, t + 1)
                    dve.wait_ge(s_r, 2 * t + 2)
                    dve.tensor_tensor(kst[:, :, 1:4:2, :], stacked(krow[:, :]), kst[:, :, 0:4:2, :].bitcast(F32),
                                      ALU.subtract).then_inc(s_kl, 1)

            @block.tensor
            def _(pe):
                pe.wait_ge(s_k, 1)
                pe.wait_ge(s_w, 16 * 7)

                def masks(t):
                    for hh in range(2):
                        pe.wait_ge(s_mr[hh], 16 * (t + 1))
                        for e in range(2):
                            n = 4 * t + 2 * hh + e
                            if n >= 2:
                                pe.wait_ge(s_mc, n - 1)
                            for c in range(4):
                                o = (4 * e + c) * P
                                ins = pe.transpose(tb[n % 2][:, c * P:c * P + P], mrow[:, hh, o:o + P], ident[:, :])
                            ins.then_inc(s_mt, 1)

                for t in range(Q):
                    pe.wait_ge(s_hn, t + 1)
                    if t > 0:
                        pe.wait_ge(s_hc, t)
                    for g in range(G):
                        ins = pe.transpose(bank[0][:, g * P:g * P + P], hn[:, g * P:g * P + P], ident[:, :])
                    ins.then_inc(s_ht, 1)
                    pe.wait_ge(s_hc, t + 1)
                    if t > 0:
                        pe.wait_ge(s_r, 2 * t)
                        pe.wait_ge(s_vc, t)
                    for n, w_ in enumerate((wq, wk, wv)):
                        for c in range(G):
                            ins = pe.matmul(bank[1 + n][:, :], hnT[:, c, :], w_[:, c, :], start=c == 0, stop=c == G - 1)
                        ins.then_inc(s_q, 1)
                    masks(t)
                    pe.wait_ge(s_kl, t + 1)
                    for g in range(G):
                        n = G * t + g
                        if n >= 2:
                            pe.wait_ge(s_kt, n - 1)
                        for j in range(4):
                            h = 4 * g + j
                            ins = pe.transpose(bank[4 + g % 2][:, j * P:j * P + P],
                                               kst[:, h, :, :].rearrange("p u d -> p (u d)").bitcast(F32), ident[:, :])
                        ins.then_inc(s_rt, 1)

        with ExitStack() as c2_:
            wo = sb("wo2", [P, G, D], c=c2_)
            QS = sb("QS", [P, H, P], F32R, c=c2_)
            qst = sb("qst", [P, H, 4, DK], F32R, c=c2_)
            mc = sb("mc", [P, 2, K], c=c2_)
            Sm = sb("Sm", [P, 2, K], c=c2_)
            mxs = sb("mxs", [P, 2, 2], c=c2_)
            rsum = sb("rsum", [P, 2, H], c=c2_)
            rinv = sb("rinv", [P, H], c=c2_)
            PTs = sb("PTs", [P, 4, Q, P], c=c2_)
            OTs = sb("OTs", [P, G, P], c=c2_)
            On = sb("On", [P, D], c=c2_)
            OnT = sb("OnT", [P, G, P], c=c2_)
            x1c = sb("x1c", [P, D], c=c2_)
            h2 = sb("h2", [P, D], c=c2_)
            m1 = sb("m1", [P, 1], c=c2_)
            v1 = sb("v1", [P, 1], c=c2_)
            r1 = sb("r1", [P, 1], c=c2_)
            t1 = sb("t1", [P, 1], c=c2_)
            Sp = [c2_.enter_context(nc.psum_tensor(f"Sp{i}", [P, 1024], F32)) for i in range(2)]
            Tp = [c2_.enter_context(nc.psum_tensor(f"Tp{i}", [P, 512], F32)) for i in range(2)]
            Op = c2_.enter_context(nc.psum_tensor("Op", [P, 512], F32))
            Wp = c2_.enter_context(nc.psum_tensor("Wp", [P, 512], F32))

            s_w = sem("s_w3", c2_)
            s_alone = sem("s_alone", c2_)
            s_mg = [sem("s_mg0", c2_), sem("s_mg1", c2_)]
            s_qh = sem("s_qh", c2_)
            s_ql = sem("s_ql", c2_)
            s_qp = sem("s_qp", c2_)
            s_qs = sem("s_qs", c2_)
            s_s = sem("s_s", c2_)
            s_sm = sem("s_sm", c2_)
            s_e = sem("s_e", c2_)
            s_t = sem("s_t", c2_)
            s_ta = sem("s_ta", c2_)
            s_td = sem("s_td", c2_)
            s_pv = sem("s_pv2", c2_)
            s_oc = sem("s_oc", c2_)
            s_on = sem("s_on", c2_)
            s_or = sem("s_or", c2_)
            s_ot = sem("s_ot", c2_)
            s_otc = sem("s_otc", c2_)
            s_wo = sem("s_wo", c2_)
            s_h2 = sem("s_h2", c2_)
            s_h2t = sem("s_h2t", c2_)
            s_x1 = sem("s_x1", c2_)
            s_dv = sem("s_dv", c2_)
            KC = K - 1
            PAIRS = Q // 2 - 1

            def tile(t):
                return slice(t, t + 1) if isinstance(t, int) else bass.ds(t, 1)

            def cols(t):
                return slice(t * P, t * P + P) if isinstance(t, int) else bass.ds(t * P, P)

            block = c2_.enter_context(nc.Block())

            @block.sync
            def _(sp):
                sp.dma_start(wo[:, :, :], wo_d.rearrange("(c p) n -> p c n", p=P)).then_inc(s_w, 16)

            @block.gpsimd
            def _(pool):
                for t in range(Q):
                    if t >= 2:
                        pool.wait_ge(s_sm, (t - 1) * H + 1)
                    pool.indirect_dma_start(mc[:, t % 2, :], None, cols_dram,
                                            bass.IndirectOffsetOnAxis(ap=cidx[:, t:t + 1], axis=0))\
                        .then_inc(s_mg[t % 2], 16)
                for b in range(2):
                    pool.wait_ge(s_mg[b], 16 * (Q // 2))

            def q_rows(t):
                return qrow[:, tile(t), :].rearrange("p o (h d) -> p h o d", d=DK).broadcast_to([P, H, 2, DK])

            @block.scalar
            def _(act):
                def take_t(t, h):
                    act.wait_ge(s_t, t * (2 * H) + (2 * h + 1))
                    act.wait_ge(s_pv, t * G + (h // 4 + 1))
                    act.activation(PTs[:, h % 4, 0:4, :], Tp[0][:, :].rearrange("p (k q) -> p k q", k=4),
                                   ACT.Copy).then_inc(s_ta, 1)

                def take_o(t, g):
                    act.wait_ge(s_pv, t * G + (g + 2))
                    act.activation(OTs[:, g, :], Op[:, 0:P], ACT.Copy).then_inc(s_oc, 1)

                def stack(t):
                    act.activation(qst[:, :, 0:2, :], q_rows(t), ACT.Copy).then_inc(s_qh, 1)

                def take_stack(t, g):
                    act.wait_ge(s_qp, t * G + (g + 1))
                    act.activation(QS[:, 4 * g:4 * g + 4, :], Wp[:, :].rearrange("p (h k) -> p h k", h=4),
                                   ACT.Copy).then_inc(s_qs, 1)

                def take_on(t):
                    act.wait_ge(s_ot, t + 1)
                    act.activation(OnT[:, :, :], Wp[:, :].rearrange("p (g k) -> p g k", g=G), ACT.Copy).then_inc(s_otc, 1)

                def take_x1(t):
                    act.wait_ge(s_h2t, t + 1)
                    act.activation(x1T[:, :, cols(t)], Wp[:, :].rearrange("p (g k) -> p g k", g=G),
                                   ACT.Copy).then_inc(s_x1, 1)

                def heads(t, b, before=True, after=True):
                    for h in range(H):
                        act.wait_ge(s_sm, t * H + (h + 2))
                        act.activation(Sm[:, h % 2, 0:KC], Sm[:, h % 2, 0:KC], ACT.Exp, bias=mxs[:, h % 2, 1:2],
                                       accum_out=rsum[:, b, h:h + 1]).then_inc(s_e, 1)
                        if h == 1 and before:
                            take_o(t - 1, G - 1)
                        if h > 4 and h % 4 == 1:
                            take_o(t, h // 4 - 1)
                        if h > 0:
                            take_t(t, h - 1)
                        elif before:
                            take_t(t - 1, H - 1)
                        if h == 4 and before:
                            take_on(t - 1)
                        if h == 6 and after:
                            stack(t + 1)
                        if h == 10 and before:
                            take_x1(t - 1)
                        if 11 <= h < 15 and after:
                            take_stack(t + 1, h - 11)

                act.sem_inc(s_ta, 1)
                act.sem_inc(s_oc, 1)
                stack(0)
                for g in range(G):
                    take_stack(0, g)
                heads(0, 0, before=False)
                with act.Fori(0, PAIRS) as i:
                    heads(i * 2 + 1, 1)
                    heads(i * 2 + 2, 0)
                heads(Q - 1, 1, after=False)
                take_t(Q - 1, H - 1)
                take_o(Q - 1, G - 1)
                take_on(Q - 1)
                take_x1(Q - 1)

            @block.vector
            def _(dve):
                done = [0]
                base = [0]

                def link(ins):
                    done[0] += 1
                    ins.then_inc(s_dv, 1)
                    dve.wait_ge(s_dv, base[0] + done[0])

                def take_t(t, h):
                    dve.wait_ge(s_t, t * (2 * H) + (2 * h + 2))
                    dve.wait_ge(s_pv, t * G + (h // 4 + 1))
                    dve.tensor_copy(PTs[:, h % 4, 4:8, :], Tp[1][:, :].rearrange("p (k q) -> p k q", k=4))\
                       .then_inc(s_td, 1)

                def stack(t):
                    dve.wait_ge(s_qh, t + 1)
                    alone(dve, s_alone)
                    dve.tensor_tensor(qst[:, :, 2:4, :], q_rows(t), qst[:, :, 0:2, :].bitcast(F32),
                                      ALU.subtract).then_inc(s_ql, 1)

                def weights(t, b):
                    dve.wait_ge(s_e, t * H + H)
                    link(dve.reciprocal(rinv[:, :], rsum[:, b, :]))

                def attention_rows(t):
                    dve.wait_ge(s_on, t + 1)
                    dve.tensor_tensor(On[:, :].rearrange("p (h d) -> p h d", h=H),
                                      Wp[:, :].rearrange("p (h d) -> p h d", h=H), bc(rinv[:, :], DK),
                                      ALU.mult).then_inc(s_or, 1)

                def second_norm(t):
                    dve.wait_ge(s_wo, t + 1)
                    link(dve.tensor_tensor(x1c[:, :], Wp[:, :], xs[:, tile(t), :].rearrange("p o d -> p (o d)"), ALU.add))
                    dve.tensor_copy(xs2[:, tile(t), :].rearrange("p o d -> p (o d)"), x1c[:, :])
                    link(dve.tensor_tensor_reduce(h2[:, :], x1c[:, :], x1c[:, :], 1.0, 0.0, ALU.mult, ALU.add,
                                                  m1[:, :]))
                    link(dve.tensor_scalar(v1[:, :], m1[:, :], 1.0 / D, 1e-6, ALU.mult, ALU.add))
                    rsqrt(dve, link, r1[:, :], v1[:, :], t1[:, :])
                    dve.scalar_tensor_tensor(out=h2[:, :], in0=x1c[:, :], scalar=r1[:, 0:1], in1=l2[:, :],
                                             op0=ALU.mult, op1=ALU.mult).then_inc(s_h2, 1)

                def heads(t, th, b, before=True, after=True):
                    dve.wait_ge(s_mg[b], th * 16 + 16)
                    for h in range(H):
                        dve.wait_ge(s_s, t * H + (h + 1))
                        if before or h >= 2:
                            dve.wait_ge(s_t, t * (2 * H) + 2 * (h - 1))
                        alone(dve, s_alone)
                        link(dve.tensor_tensor_reduce(Sm[:, h % 2, 0:KC], Sp[h % 2][:, 0:KC], mc[:, b, 0:KC], 1.0,
                                                      -3.0e38, ALU.add, ALU.max, mxs[:, h % 2, 0:1]))
                        dve.tensor_scalar(mxs[:, h % 2, 1:2], mxs[:, h % 2, 0:1], -1.0, None, ALU.mult)\
                           .then_inc(s_sm, 1)
                        if h > 0:
                            take_t(t, h - 1)
                        elif before:
                            take_t(t - 1, H - 1)
                            weights(t - 1, 1 - b)
                        if h == 2 and before:
                            attention_rows(t - 1)
                        if h == 6 and before:
                            second_norm(t - 1)
                        if h == 8 and after:
                            stack(t + 1)

                dve.sem_inc(s_sm, 1)
                dve.sem_inc(s_td, 1)
                dve.memset(Sm[:, :, KC:K], 0.0)
                stack(0)
                heads(0, 0, 0, before=False)
                start = done[0]
                LINKS = 66
                with dve.Fori(0, PAIRS) as i:
                    done[0] = 0
                    base[0] = i * LINKS + start
                    heads(i * 2 + 1, i, 1)
                    heads(i * 2 + 2, i + 1, 0)
                    assert done[0] == LINKS, done[0]
                done[0] = 0
                base[0] = start + PAIRS * LINKS
                heads(Q - 1, Q // 2 - 1, 1, after=False)
                take_t(Q - 1, H - 1)
                weights(Q - 1, 1)
                attention_rows(Q - 1)
                second_norm(Q - 1)

            @block.tensor
            def _(pe):
                def score(t, h):
                    pe.wait_ge(s_qs, t * G + (h // 4 + 1))
                    if not (isinstance(t, int) and t == 0 and h < 2):
                        pe.wait_ge(s_sm, t * H + h)
                    for u in range(2):
                        ins = pe.matmul(Sp[h % 2][:, u * 512:u * 512 + 512], QS[:, h, :],
                                        KS[:, h, u * 512:u * 512 + 512], start=True, stop=True)
                    ins.then_inc(s_s, 1)

                def turn_p(t, h):
                    pe.wait_ge(s_e, t * H + (h + 1))
                    pe.wait_ge(s_ta, t * H + (h + 1))
                    for k in range(4):
                        ins = pe.transpose(Tp[0][:, k * P:k * P + P], Sm[:, h % 2, k * P:k * P + P], ident[:, :])
                    ins.then_inc(s_t, 1)
                    pe.wait_ge(s_td, t * H + (h + 1))
                    for k in range(4, 8):
                        ins = pe.transpose(Tp[1][:, (k - 4) * P:(k - 4) * P + P],
                                           Sm[:, h % 2, k * P:k * P + P], ident[:, :])
                    ins.then_inc(s_t, 1)

                def values(t, g):
                    pe.wait_ge(s_ta, t * H + (4 * g + 5))
                    pe.wait_ge(s_td, t * H + (4 * g + 5))
                    pe.wait_ge(s_oc, t * G + (g + 1))
                    for k in range(Q):
                        n = P if k < Q - 1 else P - 1
                        for j in range(J):
                            r = slice(DK * j, DK * j + DK)
                            h = g * J + j
                            ins = pe.matmul(Op[r, 0:P], V[0:n, k, h * DK:h * DK + DK], PTs[0:n, j, k, :],
                                            start=k == 0, stop=k == Q - 1)
                    ins.then_inc(s_pv, 1)

                def back(t):
                    pe.wait_ge(s_oc, t * G + (G + 1))
                    for g in range(G):
                        ins = pe.transpose(Wp[:, g * P:g * P + P], OTs[:, g, :], ident[:, :])
                    ins.then_inc(s_on, 1)

                def again(t):
                    pe.wait_ge(s_or, t + 1)
                    for g in range(G):
                        ins = pe.transpose(Wp[:, g * P:g * P + P], On[:, g * P:g * P + P], ident[:, :])
                    ins.then_inc(s_ot, 1)

                def project(t):
                    pe.wait_ge(s_otc, t + 1)
                    for g in range(G):
                        ins = pe.matmul(Wp[:, :], OnT[:, g, :], wo[:, g, :], start=g == 0, stop=g == G - 1)
                    ins.then_inc(s_wo, 1)

                def norm_t(t):
                    pe.wait_ge(s_h2, t + 1)
                    for g in range(G):
                        ins = pe.transpose(Wp[:, g * P:g * P + P], h2[:, g * P:g * P + P], ident[:, :])
                    ins.then_inc(s_h2t, 1)

                def stack(t, g, first=False):
                    if g == 0:
                        pe.wait_ge(s_ql, t + 1)
                        if not first:
                            pe.wait_ge(s_x1, t - 1)
                    else:
                        pe.wait_ge(s_qs, t * G + g)
                    for j in range(4):
                        ins = pe.transpose(Wp[:, j * P:j * P + P],
                                           qst[:, 4 * g + j, :, :].rearrange("p u d -> p (u d)").bitcast(F32),
                                           ident[:, :])
                    ins.then_inc(s_qp, 1)

                def heads(t, before=True, after=True):
                    for h in range(H):
                        turn_p(t, h)
                        if h > 0 and h % 4 == 0:
                            values(t, h // 4 - 1)
                        if h == 0 and before:
                            values(t - 1, G - 1)
                        if h + 2 < H:
                            score(t, h + 2)
                        elif after:
                            score(t + 1, h + 2 - H)
                        if before and h == 1:
                            back(t - 1)
                        if before and h == 3:
                            again(t - 1)
                        if before and h == 5:
                            project(t - 1)
                        if before and h == 9:
                            norm_t(t - 1)
                        if after and 10 <= h < 14:
                            stack(t + 1, h - 10, first=not before)

                pe.sem_inc(s_pv, 1)
                for g in range(G):
                    stack(0, g, first=True)
                score(0, 0)
                score(0, 1)
                pe.wait_ge(s_w, 16)
                heads(0, before=False)
                with pe.Fori(0, PAIRS) as i:
                    heads(i * 2 + 1)
                    heads(i * 2 + 2)
                heads(Q - 1, after=False)
                values(Q - 1, G - 1)
                back(Q - 1)
                again(Q - 1)
                project(Q - 1)
                norm_t(Q - 1)
        mid.close()
        mlp(nc, xs, xs2, x1T, wsel, above, w1_d, w2_d, idx, out)


def mlp(nc, xs, x1, x1T, wsel, above, w1_d, w2_d, idx, out):
    Q = xs.shape[1]
    D = xs.shape[2]
    F = w1_d.shape[1]
    K = Q * P
    G = D // P
    FC = F // P
    HT = K // 2
    QH = Q // 2

    with ExitStack() as ctx:
        def sb(name, shape, dt=F32):
            return ctx.enter_context(nc.sbuf_tensor(name, shape, dt))

        def sem(name):
            return ctx.enter_context(nc.semaphore(name))

        w1 = sb("w1m", [P, G, F])
        w2 = sb("w2m", [P, FC, D])
        GT = sb("GT", [P, FC, HT])
        nab = sb("nab", [P, Q])
        fin = sb("fin", [P, Q, D])
        hb = [ctx.enter_context(nc.psum_tensor(f"hb{i}", [P, 512], F32)) for i in range(4)]
        yb = [ctx.enter_context(nc.psum_tensor(f"yb{i}", [P, 512], F32)) for i in range(2)]

        s_w1 = sem("s_w1m")
        s_w2 = sem("s_w2m")
        s_h = sem("s_hm")
        s_g = sem("s_gm")
        s_y = sem("s_ym")
        s_v = sem("s_vm")
        s_f = sem("s_fm")
        s_t = sem("s_tm2")
        s_o = sem("s_om")

        block = ctx.enter_context(nc.Block())

        @block.sync
        def _(sp):
            sp.dma_start(w1[:, :, :], w1_d.rearrange("(c p) n -> p c n", p=P)).then_inc(s_w1, 16)
            sp.dma_start(w2[:, :, :], w2_d.rearrange("(c p) n -> p c n", p=P)).then_inc(s_w2, 16)

        @block.tensor
        def _(pe):
            pe.wait_ge(s_w1, 16)
            for u in range(2):
                for f in range(FC):
                    n = u * FC + f
                    if n >= 4:
                        pe.wait_ge(s_g, n - 3)
                    for c in range(G):
                        ins = pe.matmul(hb[n % 4][:, :], w1[:, c, f * P:f * P + P], x1T[:, c, u * HT:u * HT + HT],
                                        start=c == 0, stop=c == G - 1)
                    ins.then_inc(s_h, 1)
                if u == 0:
                    pe.wait_ge(s_w2, 16)
                pe.wait_ge(s_g, (u + 1) * FC)
                for q in range(QH):
                    n = u * QH + q
                    if n >= 2:
                        pe.wait_ge(s_t, n - 1)
                    for f in range(FC):
                        ins = pe.matmul(yb[n % 2][:, :], GT[:, f, q * P:q * P + P], w2[:, f, :],
                                        start=f == 0, stop=f == FC - 1)
                    ins.then_inc(s_y, 1)

        @block.scalar
        def _(act):
            for n in range(2 * FC):
                act.wait_ge(s_h, n + 1)
                act.activation(GT[:, n % FC, :], hb[n % 4][:, :], ACT.Gelu_apprx_tanh).then_inc(s_g, 1)

        @block.vector
        def _(dve):
            done = [0]

            def link(ins):
                done[0] += 1
                ins.then_inc(s_v, 1)
                dve.wait_ge(s_v, done[0])

            link(dve.tensor_scalar(nab[:, :], above[:, :], -1.0, None, ALU.mult))
            for q in range(Q):
                dve.wait_ge(s_y, q + 1)
                dve.tensor_tensor(fin[:, q, :], yb[q % 2][:, :], x1[:, q, :], ALU.add).then_inc(s_t, 1)
                dve.wait_ge(s_t, q + 1)
                link(dve.tensor_scalar(fin[:, q, :], fin[:, q, :], wsel[:, q:q + 1], None, ALU.mult))
                dve.scalar_tensor_tensor(out=fin[:, q, :], in0=xs[:, q, :], scalar=nab[:, q:q + 1],
                                         in1=fin[:, q, :], op0=ALU.mult, op1=ALU.add).then_inc(s_f, 1)

        @block.gpsimd
        def _(pool):
            for q in range(Q):
                pool.wait_ge(s_f, q + 1)
                n = P if q < Q - 1 else P - 1
                pool.indirect_dma_start(out, bass.IndirectOffsetOnAxis(ap=idx[0:n, q:q + 1], axis=0),
                                        fin[0:n, q, :], None, compute_op=ALU.add).then_inc(s_o, 16)
            pool.wait_ge(s_o, 16 * Q)


def build(nc, x, wqT, wkT, wvT, woT, beta, maskT, positions, router_w, router_b, wq, wk, wv, wo, w1, w2, ln1, ln2,
          out):
    T = x.shape[0]
    K = T // 8
    list_dram = nc.dram_tensor("chosen_list", [K, 1], U32, kind="Internal").ap()
    cols_dram = nc.dram_tensor("mask_columns", [maskT.shape[0], K], F32, kind="Internal").ap()
    with ExitStack() as ctx:
        w = ctx.enter_context(nc.sbuf_tensor("w", [P, T // P], F32))
        thr = ctx.enter_context(nc.sbuf_tensor("thr", [P, 1], F32))
        idx = ctx.enter_context(nc.sbuf_tensor("idx", [P, K // P], U32))
        infini_attention(nc, x, wqT, wkT, wvT, woT, beta, router_w, router_b, out, w)
        select_tokens(nc, w, thr, idx, K, list_dram)
        feed_forward(nc, x, maskT, positions, router_w, router_b, wq, wk, wv, wo, w1, w2, ln1, ln2, thr, idx, out,
                     cols_dram)


def kernel(**inputs):
    import numpy as _np
    import concourse.bacc as _bacc
    from concourse import mybir as _mybir
    from concourse.bass_utils import run_bass_kernel_spmd as _run

    def attn(name):
        return _np.asarray(inputs["L0_attn_" + name])

    def ffn(name):
        return _np.asarray(inputs["L0_ffn_" + name])

    arrays = {
        "x": attn("x")[0],
        "wqT": attn("W_q").T, "wkT": attn("W_k").T, "wvT": attn("W_v").T, "woT": attn("W_o").T,
        "beta": attn("beta_param")[None],
        "maskT": ffn("attention_mask")[0, 0].T, "positions": ffn("position_ids")[0][:, None],
        "router_w": ffn("router_w"), "router_b": ffn("router_b")[None],
        "wq": ffn("wq"), "wk": ffn("wk"), "wv": ffn("wv"), "wo": ffn("wo"), "w1": ffn("w1"), "w2": ffn("w2"),
        "ln1": ffn("ln1")[None], "ln2": ffn("ln2")[None],
    }
    arrays = {"in_" + k: _np.ascontiguousarray(v) for k, v in arrays.items()}
    nc = _bacc.Bacc("TRN2", target_bir_lowering=False, num_devices=1)
    args = [nc.dram_tensor(k, v.shape, _mybir.dt.from_np(v.dtype), kind="ExternalInput").ap()
            for k, v in arrays.items()]
    rows = arrays["in_x"].shape
    args.append(nc.dram_tensor("out_rows", rows, F32, kind="ExternalOutput").ap())
    build(nc, *args)
    r = _run(nc, [arrays], core_ids=[0])
    return r.results[0]["out_rows"][None]
```

```python
from contextlib import ExitStack

import numpy as np

import concourse.bass as bass
from concourse import mybir

F32 = mybir.dt.float32
F32R = mybir.dt.float32r
BF16 = mybir.dt.bfloat16
I32 = mybir.dt.int32
U32 = mybir.dt.uint32
ALU = mybir.AluOpType
ACT = mybir.ActivationFunctionType
AX = mybir.AxisListType



def alone(eng, sem):
    eng.sem_inc(sem, 1)


P = 128
NEG = -1.0e30
MAGIC = 1597463007.0


def bc(t, n):
    return t.rearrange("p (m o) -> p m o", o=1).broadcast_to([t.shape[0], t.shape[1], n])


def bm(t, m):
    return t.rearrange("p (o n) -> p o n", o=1).broadcast_to([t.shape[0], m, t.shape[1]])


def infini_attention(nc, x, wqT, wkT, wvT, woT, beta, router_w, router_b, out, wcol):
    T, D = x.shape
    H = beta.shape[1]
    DK = D // H
    SEG = 64
    G = D // P
    J = P // DK
    TILES = 2
    SEGS = 4
    BT = TILES * P
    NB = T // BT
    VW = DK + 1
    SCALE = float(DK) ** -0.5

    with ExitStack() as ctx:
        def sb(name, shape, dt=F32):
            return ctx.enter_context(nc.sbuf_tensor(name, shape, dt))

        def sem(name):
            return ctx.enter_context(nc.semaphore(name))

        wq, wk, wv, wo = [(sb(f"{n}_high", [P, G, D], F32R), sb(f"{n}_low", [P, G, D], F32R))
                          for n in ("wq", "wk", "wv", "wo")]
        rw = sb("rw", [P, D])
        rb = sb("rb", [P, 1])
        ident = sb("ident", [P, P])
        identb = sb("identb", [P, P], BF16)
        causal = sb("causal", [P, SEG], BF16)
        headmask = sb("headmask", [P, J])
        bt = sb("bt", [P, H])
        be = sb("be", [P, H])
        bs = sb("bs", [P, H])
        betas = sb("betas", [P, H])
        omb = sb("omb", [P, J, G])
        xin = sb("xin", [P, 2, TILES, D])
        xn = sb("xn", [P, 2, TILES, D])
        xu = sb("xu", [P, 2, TILES, D])
        junk = sb("junk", [P, D])
        stats = sb("stats", [P, TILES, 6])
        mv = sb("mv", [P, TILES, 2])
        var = sb("var", [P, TILES])
        rstd = sb("rstd", [P, TILES])
        nwt = sb("nwt", [P, TILES])
        rs1 = sb("rs1", [P, 2, TILES])
        nmr = sb("nmr", [P, 2, TILES])
        wt = sb("wt", [P, TILES])
        xnT = (sb("xnT_high", [P, G, BT], F32R), sb("xnT_low", [P, G, BT], F32R))
        QT = sb("QT", [P, 2, G, BT])
        KT = sb("KT", [P, 2, G, BT])
        SQT = sb("SQT", [P, 2, G, BT])
        SKT = sb("SKT", [P, G, BT])
        ET = sb("ET", [P, 2, 2, BT])
        RT = sb("RT", [P, 2, 2, BT])
        SK = sb("SK", [P, 2, TILES, D])
        DV = sb("DV", [P, 2, TILES, 2, H, VW])
        VS = sb("VS", [P, 2, TILES, H, VW])
        ksum = sb("ksum", [P, G, SEGS])
        Z = sb("Z", [P, 2, SEGS + 1, G])
        Zbd = sb("Zbd", [P, 2, G, 32])
        DT = sb("DT", [P, 512])
        den = sb("den", [P, 2, 2 * TILES * H])
        rden = sb("rden", [P, 2, 2 * TILES * H])
        w2 = sb("w2", [P, 2, TILES, H])
        mx = sb("mx", [P, J, G])
        Pq = sb("Pq", [P, J, G, SEG])
        PT = sb("PT", [P, J, G, SEG])
        rl = sb("rl", [P, J, G])
        w1 = sb("w1", [P, J, G])
        T1 = sb("T1", [P, D])
        T2 = sb("T2", [P, D])
        As = sb("As", [P, D])
        AT = (sb("AT_high", [P, G, P], F32R), sb("AT_low", [P, G, P], F32R))
        outt = sb("outt", [P, 2, D])
        NA = sb("NA", [P, 2, G, DK])
        M = sb("M", [P, 2, G, DK])
        Mbd = sb("Mbd", [P, 2, G, P])

        proj = [ctx.enter_context(nc.psum_tensor(f"proj{i}", [P, 512], F32)) for i in range(2)]
        S = ctx.enter_context(nc.psum_tensor("S", [P, J, 512], F32))
        AB = ctx.enter_context(nc.psum_tensor("AB", [P, 2, G, 2, DK], F32))
        AM = ctx.enter_context(nc.psum_tensor("AM", [P, 512], F32))

        s_w = [sem(f"s_w{i}") for i in range(4)]
        s_wh = sem("s_wh")
        s_wl = sem("s_wl")
        s_xh = sem("s_xh")
        s_ah = sem("s_ah")
        s_xu = sem("s_xu")
        s_rows = sem("s_rows")
        s_x = [sem("s_x0"), sem("s_x1")]
        s_alone_pe = sem("s_alone_pe")
        s_alone_dve = sem("s_alone_dve")
        s_c0 = sem("s_c0")
        s_const = sem("s_const")
        s_beta = sem("s_beta")
        s_be = sem("s_be")
        s_dve = sem("s_dve")
        s_ln = sem("s_ln")
        s_full = [sem("s_full0"), sem("s_full1")]
        s_free = [sem("s_free0"), sem("s_free1")]
        s_sq = sem("s_sq")
        s_sk = sem("s_sk")
        s_zbd = sem("s_zbd")
        s_dsk = sem("s_dsk")
        s_vs = [sem("s_vs0"), sem("s_vs1")]
        s_S = sem("s_S")
        s_sub = sem("s_sub")
        s_exp = sem("s_exp")
        s_pt = sem("s_pt")
        s_pv = sem("s_pv")
        s_ab = sem("s_ab")
        s_na = sem("s_na")
        s_tm = sem("s_tm")
        s_m = sem("s_m")
        s_mbd = sem("s_mbd")
        s_am = sem("s_am")
        s_t2 = sem("s_t2")
        s_t1 = sem("s_t1")
        s_as = sem("s_as")
        s_od = sem("s_od")
        s_of = sem("s_of")

        ORDER = (["AST1", "OUT1", "KT0", "KT1", "SK0", "OUT0", "XT0"],
                 ["QT0", "QT1", "AST0", "V0", "V1", "SK1", "DEN", "DNT", "XT1"])
        FIRST = (["XF0", "KT0", "KT1", "SK0", "XT0"],
                 ["XF1", "QT0", "QT1", "V0", "V1", "SK1", "DEN", "DNT", "XT1"])

        def order(m, b):
            skip = ()
            if m == 0:
                skip = ("AST1", "OUT1")
            if m == NB - 2:
                skip = ("XT0", "XT1")
            if m >= NB - 1:
                return [u for u in ORDER[b] if u in (("AST1", "OUT1") if m == NB else STAGE2)]
            return [u for u in ORDER[b] if u not in skip]

        STAGE2 = ("AST0", "OUT0", "AST1", "OUT1")

        def use(name, m):
            if m is None:
                b = 0 if name in FIRST[0] else 1
                return b, FIRST[b].index(name)
            b = 0 if name in ORDER[0] else 1
            if isinstance(m, int):
                return b, len(FIRST[b]) + sum(len(order(k, b)) for k in range(m)) + order(m, b).index(name)
            before = len(FIRST[b]) + len(order(0, b)) - len(ORDER[b])
            return b, m * len(ORDER[b]) + (before + ORDER[b].index(name))

        def take(eng, name, m):
            b, k = use(name, m)
            if not (isinstance(k, int) and k == 0):
                eng.wait_ge(s_free[b], k)
            return proj[b], s_full[b]

        def got(eng, name, m):
            b, k = use(name, m)
            eng.wait_ge(s_full[b], k + 1)
            return proj[b], s_free[b]

        def moved(eng, name, m):
            b, k = use(name, m)
            eng.wait_ge(s_free[b], k + 1)

        x_t = x.rearrange("(n a p) d -> n p a d", a=TILES, p=P)
        out_t = out.rearrange("(n p) d -> n p d", p=P)
        halves = [(32 * 0, 32 * 1), (32 * 2, 32 * 3)]
        PAIRS = NB // 2 - 1
        assert NB == 2 * PAIRS + 2 and PAIRS > 1
        raw_weights = ((QT, wq), (KT, wk), (SQT, wv), (SK, wo))

        block = ctx.enter_context(nc.Block())

        @block.sync
        def _(sp):
            sp.sem_inc(s_of, 2)
            for n in range(2):
                sp.dma_start(xin[:, n, :, :], x_t[n]).then_inc(s_x[n], 16)
            for n, d in enumerate((wqT, wkT, wvT, woT)):
                sp.dma_start(raw_weights[n][0][:, :, :, :].rearrange("p a b n -> p (a b n)")
                             .rearrange("p (c n) -> p c n", c=G),
                             d.rearrange("(c p) n -> p c n", p=P)).then_inc(s_w[n], 16)

            def shift_v(m, p):
                moved(sp, "V1", m)
                for src, dst in halves:
                    sp.dma_start(VS[dst:dst + 32, p, :, :, :], DV[src:src + 32, p, :, 1, :, :]).then_inc(s_vs[p], 16)

            def store(h, n, a, name):
                moved(sp, name, h)
                sp.dma_start(out_t[n], outt[:, a, :]).then_inc(s_od, 16)
                sp.wait_ge(s_od, n * 16 + 16)
                sp.sem_inc(s_of, 1)

            def half(m, p, first=False, ln=True, stage1=True):
                if ln:
                    sp.wait_ge(s_xu, m + 1)
                    sp.dma_start(xin[:, p, :, :], x_t[m + 2]).then_inc(s_x[p], 16)
                if not first:
                    store(m, m * 2 - 1, 1, "OUT1")
                store(m, m * 2, 0, "OUT0")
                if stage1:
                    shift_v(m, 1 - p)

            shift_v(None, 0)
            half(0, 0, first=True)
            half(1, 1)
            with sp.Fori(1, PAIRS) as i:
                half(i * 2, 0)
                half(i * 2 + 1, 1)
            half(NB - 2, 0, ln=False)
            half(NB - 1, 1, ln=False, stage1=False)
            store(NB, 2 * NB - 1, 1, "OUT1")
            sp.wait_ge(s_od, 32 * NB)

        @block.gpsimd
        def _(pool):
            pool.dma_start(rw[:, :], router_w.rearrange("d a -> a d").broadcast_to([P, D])).then_inc(s_rows, 16)
            pool.dma_start(rb[:, :], router_b.broadcast_to([P, 1])).then_inc(s_rows, 16)
            pool.dma_start(bt[:, :], beta.broadcast_to([P, H])).then_inc(s_rows, 16)
            pool.sem_inc(s_as, 1)
            pool.sem_inc(s_mbd, 1)
            pool.memset(ident[:, :], 0.0)
            pool.memset(identb[:, :], 0.0)
            pool.memset(causal[:, :], 0.0)
            pool.memset(headmask[:, :], 0.0)
            pool.memset(Z[:, :, :, :], 0.0)
            pool.memset(M[:, :, :, :], 0.0)
            pool.memset(Mbd[:, :, :, :], 0.0)
            pool.memset(Zbd[:, :, :, :], 0.0)
            for p in range(2):
                for a in range(TILES):
                    pool.memset(DV[:, p, a, 1, :, DK:VW], 1.0)
            pool.memset(junk[:, :], 0.0).then_inc(s_c0, 1)
            pool.wait_ge(s_c0, 1)
            for t in (ident, identb):
                pool.affine_select(out=t[:, :], in_=t[:, :], compare_op=ALU.not_equal, fill=1.0,
                                   base=0, pattern=[[-1, P]], channel_multiplier=1)
            step = 1
            for q in (0, SEG):
                pool.memset(junk[:, 0:1], 0.0).then_inc(s_c0, 1)
                step += 1
                pool.wait_ge(s_c0, step)
                pool.affine_select(out=causal[q:q + SEG, :], in_=causal[q:q + SEG, :], compare_op=ALU.is_ge,
                                   fill=NEG, base=0, pattern=[[-1, SEG]], channel_multiplier=1).then_inc(s_c0, 1)
                step += 1
                pool.wait_ge(s_c0, step)
            for j in range(J):
                pool.memset(headmask[DK * j:DK * j + DK, j:j + 1], 1.0).then_inc(s_c0, 1)
                step += 1
                pool.wait_ge(s_c0, step)
            pool.memset(junk[:, :], 0.0).then_inc(s_const, 1)
            pool.wait_ge(s_const, 1)

            def diagonal(s_no, b):
                pool.wait_ge(s_m, s_no + 2)
                for g in range(G):
                    ins = pool.tensor_tensor(Mbd[:, 1 - b, g, :].rearrange("p (j d) -> p j d", j=J),
                                             bm(M[:, 1 - b, g, :], J), bc(headmask[:, :], DK), ALU.mult)
                ins.then_inc(s_mbd, 1)

            def rows(n2, m, a):
                pool.wait_ge(s_t2, n2 + 2)
                pool.wait_ge(s_t1, n2 + 2)
                pool.tensor_tensor(As[:, :], T1[:, :], T2[:, :], ALU.add).then_inc(s_as, 1)
                pool.wait_ge(s_as, n2 + 2)

            def half(m):
                for a in range(TILES):
                    for b in range(2):
                        diagonal(m * SEGS + (2 * a + b), b)
                    rows(m * 2 + a, m, a)

            half(0)
            half(1)
            with pool.Fori(1, PAIRS) as i:
                half(i * 2)
                half(i * 2 + 1)
            half(NB - 2)
            half(NB - 1)

        @block.scalar
        def _(act):
            def copy(dst, src):
                return act.activation(dst, src, ACT.Copy)

            for n, (raw, (high, _)) in enumerate(raw_weights):
                act.wait_ge(s_w[n], 16)
                copy(high[:, :, :].rearrange("p c n -> p (c n)"),
                     raw[:, :, :, :].rearrange("p a b n -> p (a b n)")).then_inc(s_wh, 1)

            def xT(m, name, k):
                bank, _ = got(act, f"{name}{k}", m)
                copy(xnT[0][:, 2 * k:2 * k + 2, :], bank[:, :].rearrange("p (c t) -> p c t", c=2)).then_inc(s_xh, 1)

            def feature(m, k, name, raw, pn, scale, s_used):
                bank, free = got(act, f"{name}{k}", m)
                v = bank[:, :].rearrange("p (c t) -> p c t", c=2)
                act.activation(raw[:, pn, 2 * k:2 * k + 2, :], v, ACT.Copy, scale=scale)
                if s_used is not None:
                    act.wait_ge(*s_used)
                act.activation(ET[:, k, :, :], v, ACT.Exp)
                act.activation(RT[:, k, :, :], v, ACT.Relu).then_inc(free, 1)

            def v_tile(m, pn, a):
                bank, free = got(act, f"V{a}", m)
                copy(DV[:, pn, a, 1, :, 0:DK], bank[:, :].rearrange("p (h d) -> p h d", h=H)).then_inc(free, 1)

            def sk_tile(m, pn, a):
                bank, free = got(act, f"SK{a}", m)
                copy(SK[:, pn, a, :], bank[:, :]).then_inc(free, 1)

            def den_rows(m):
                bank, free = got(act, "DEN", m)
                copy(DT[:, :], bank[:, :]).then_inc(free, 1)

            def prob(m, a):
                act.wait_ge(s_sub, m * 2 + (a + 1))
                act.activation(Pq[:, :, :, :], Pq[:, :, :, :], ACT.Exp).then_inc(s_exp, 1)

            def neg_a(m, sg):
                act.wait_ge(s_ab, m * SEGS + (sg + 1))
                copy(NA[:, sg % 2, :, :], AB[:, sg % 2, :, 0, :]).then_inc(s_na, 1)

            def a_t(h, a):
                bank, _ = got(act, f"AST{a}", h)
                copy(AT[0][:, :, :], bank[:, :].rearrange("p (g t) -> p g t", g=G)).then_inc(s_ah, 1)

            def half(m, p, first=False, ln=True, stage1=True):
                pn = 1 - p
                if not first:
                    a_t(m, 1)
                prob(m, 0)
                if stage1:
                    feature(m, 0, "QT", QT, pn, SCALE, (s_sk, m * 2 + 1))
                neg_a(m, 0)
                if stage1:
                    feature(m, 1, "QT", QT, pn, SCALE, (s_sk, m * 2 + 2))
                neg_a(m, 1)
                if stage1:
                    feature(m, 0, "KT", KT, pn, 1.0, (s_sq, m * 2 + 3))
                a_t(m, 0)
                if stage1:
                    feature(m, 1, "KT", KT, pn, 1.0, (s_sq, m * 2 + 4))
                prob(m, 1)
                neg_a(m, 2)
                if stage1:
                    v_tile(m, pn, 0)
                    v_tile(m, pn, 1)
                neg_a(m, 3)
                if stage1:
                    sk_tile(m, pn, 0)
                    sk_tile(m, pn, 1)
                    den_rows(m)
                if ln:
                    xT(m, "XT", 0)
                    xT(m, "XT", 1)

            xT(None, "XF", 0)
            xT(None, "XF", 1)
            act.wait_ge(s_rows, 16 * 3)
            act.activation(be[:, :], bt[:, :], ACT.Exp, scale=-1.0).then_inc(s_be, 1)
            for k in range(2):
                feature(None, k, "QT", QT, 0, SCALE, None)
            for k in range(2):
                feature(None, k, "KT", KT, 0, 1.0, (s_sq, k + 1))
            v_tile(None, 0, 0)
            v_tile(None, 0, 1)
            sk_tile(None, 0, 0)
            sk_tile(None, 0, 1)
            den_rows(None)
            xT(None, "XT", 0)
            xT(None, "XT", 1)
            half(0, 0, first=True)
            half(1, 1)
            with act.Fori(1, PAIRS) as i:
                half(i * 2, 0)
                half(i * 2 + 1, 1)
            half(NB - 2, 0, ln=False)
            half(NB - 1, 1, ln=False, stage1=False)
            a_t(NB, 1)

        @block.vector
        def _(dve):
            done = [0]
            base = [0]

            def link(ins):
                done[0] += 1
                ins.then_inc(s_dve, 1)
                dve.wait_ge(s_dve, base[0] + done[0])

            def statistics(nh, p):
                dve.wait_ge(s_x[p], (nh + 1) * 16)
                for a in range(TILES):
                    ins = dve.bn_stats(stats[:, a, :], xin[:, p, a, :])
                    if a == TILES - 1:
                        link(ins)
                    else:
                        ins.then_inc(s_dve, 1)
                        done[0] += 1
                alone(dve, s_alone_dve)
                for a in range(TILES):
                    ins = dve.bn_aggr(mv[:, a, :], stats[:, a, :])
                    if a == TILES - 1:
                        link(ins)
                    else:
                        ins.then_inc(s_dve, 1)
                        done[0] += 1

            def deviation():
                link(dve.tensor_scalar(var[:, :], mv[:, :, 1], 1e-5, None, ALU.add))
                rsqrt(dve, link, rstd[:, :], var[:, :], nwt[:, :])

            def normalise(n, p):
                for a in range(TILES):
                    ins = dve.tensor_scalar(xn[:, p, a, :], xin[:, p, a, :], mv[:, a, 0:1], rstd[:, a:a + 1],
                                            ALU.subtract, ALU.mult)
                ins.then_inc(s_ln, 1)
                dve.scalar_tensor_tensor(out=nmr[:, p, :], in0=mv[:, :, 0], scalar=-1.0, in1=rstd[:, :],
                                         op0=ALU.mult, op1=ALU.mult)
                link(dve.tensor_scalar(rs1[:, p, :], rstd[:, :], 1.0, None, ALU.add))

            def residual(p):
                for a in range(TILES):
                    ins = dve.tensor_scalar(xu[:, p, a, :], xin[:, p, a, :], rs1[:, p, a:a + 1],
                                            nmr[:, p, a:a + 1], ALU.mult, ALU.add)
                ins.then_inc(s_xu, 1)

            def low_x(m, n2, name, k):
                bank, free = got(dve, f"{name}{k}", m)
                dve.wait_ge(s_xh, n2 + (k + 1))
                dve.tensor_tensor(xnT[1][:, 2 * k:2 * k + 2, :], bank[:, :].rearrange("p (c t) -> p c t", c=2),
                                  xnT[0][:, 2 * k:2 * k + 2, :].bitcast(F32), ALU.subtract).then_inc(free, 1)

            def low_a(h, n, a):
                bank, free = got(dve, f"AST{a}", h)
                dve.wait_ge(s_ah, n + 1)
                dve.tensor_tensor(AT[1][:, :, :], bank[:, :].rearrange("p (g t) -> p g t", g=G),
                                  AT[0][:, :, :].bitcast(F32), ALU.subtract).then_inc(free, 1)

            def sigma(m, name, k, dst, s_done):
                moved(dve, f"{name}{k}", m)
                dve.scalar_tensor_tensor(out=dst, in0=ET[:, k, :, :], scalar=1.0, in1=RT[:, k, :, :],
                                         op0=ALU.min, op1=ALU.add).then_inc(s_done, 1)

            def z_chain(n, n2, pn):
                dve.wait_ge(s_sk, n2 + 2)
                link(dve.tensor_reduce(ksum[:, :, :], SKT[:, :, :].rearrange("p g (s t) -> p g s t", s=SEGS),
                                       AX.X, ALU.add))
                link(dve.tensor_copy(Z[:, pn, 0, :], Z[:, 1 - pn, SEGS, :]))
                for s in range(SEGS):
                    link(dve.tensor_tensor(Z[:, pn, s + 1, :], Z[:, pn, s, :], ksum[:, :, s], ALU.add))
                for g in range(G):
                    ins = dve.tensor_tensor(Zbd[:, pn, g, 0:SEGS * J].rearrange("p (s j) -> p s j", j=J),
                                            bc(Z[:, pn, 0:SEGS, g], J), bm(headmask[:, :], SEGS), ALU.mult)
                ins.then_inc(s_zbd, 1)

            def denominators(m, n2, pn):
                bank, free = got(dve, "DNT", m)
                rows = bank[:, :].rearrange("p (q a g c) -> p q a g c", q=2, a=TILES, g=G)
                dst = den[:, pn, :].rearrange("p (q a g j) -> p q a g j", q=2, a=TILES, g=G)
                for a in range(TILES):
                    for b in range(2):
                        r = slice(b * SEG, b * SEG + SEG)
                        o = (2 * a + b) * J
                        ins = dve.tensor_scalar(dst[r, :, a, :, :], rows[r, :, a, :, o:o + J], 1e-6, None, ALU.add)
                ins.then_inc(free, 1)
                moved(dve, "DNT", m)

            def previous_values(m, pn):
                N = 2 * TILES * H
                link(dve.reciprocal(rden[:, pn, :], den[:, pn, :]))
                link(dve.tensor_tensor(w2[:, pn, :, :], rden[:, pn, TILES * H:N].rearrange("p (a h) -> p a h", a=TILES),
                                  betas[:, :].rearrange("p (o h) -> p o h", o=1).broadcast_to([P, TILES, H]), ALU.mult))
                for a in range(TILES):
                    moved(dve, f"SK{a}", m)
                    dve.scalar_tensor_tensor(
                        out=DV[:, pn, a, 0, :, 0:DK], in0=SK[:, pn, a, :].rearrange("p (h d) -> p h d", h=H),
                        scalar=-1.0,
                        in1=rden[:, pn, a * H:a * H + H].rearrange("p (h o) -> p h o", o=1).broadcast_to([P, H, DK]),
                        op0=ALU.mult, op1=ALU.mult).then_inc(s_dsk, 1)

            def s_half(a):
                return S[:, :, a * 256:a * 256 + 256].rearrange("p j (g k) -> p j g k", g=G)

            def softmax_in(m, a):
                dve.wait_ge(s_S, m * 2 + (a + 1))
                link(dve.tensor_reduce(mx[:, :, :], s_half(a), AX.X, ALU.max))
                dve.tensor_tensor(Pq[:, :, :, :], s_half(a),
                                  mx[:, :, :].rearrange("p j (g o) -> p j g o", o=1).broadcast_to([P, J, G, SEG]),
                                  ALU.subtract).then_inc(s_sub, 1)

            def p_transpose(m, a):
                dve.wait_ge(s_exp, m * 2 + (a + 1))
                dve.transpose(PT[:, :, :, :].rearrange("p j g k -> p (j g k)"),
                              Pq[:, :, :, :].rearrange("p j g k -> p (j g k)")).then_inc(s_pt, 1)

            def m_next(m, sg):
                b = sg % 2
                dve.wait_ge(s_tm, m * SEGS + (sg + 1))
                dve.tensor_tensor(M[:, 1 - b, :, :], AB[:, b, :, 1, :], M[:, b, :, :], ALU.add).then_inc(s_m, 1)

            def softmax_part(m, a):
                dve.wait_ge(s_pv, m * 2 + (a + 1))
                dve.wait_ge(s_as, m * 2 + a + 1)
                O = S[:, :, a * 256:a * 256 + G * VW].rearrange("p j (g d) -> p j g d", g=G)
                link(dve.reciprocal(rl[:, :, :].rearrange("p j (g o) -> p j g o", o=1), O[:, :, :, DK:VW]))
                link(dve.tensor_tensor(w1[:, :, :], rl[:, :, :], omb[:, :, :], ALU.mult))
                dve.tensor_tensor(T1[:, :].rearrange("p (g j d) -> p j g d", g=G, j=J), O[:, :, :, 0:DK],
                                  w1[:, :, :].rearrange("p j (g o) -> p j g o", o=1).broadcast_to([P, J, G, DK]),
                                  ALU.mult).then_inc(s_t1, 1)

            def memory_part(m, p, a):
                dve.wait_ge(s_am, m * SEGS + (2 * a + 2))
                dve.tensor_tensor(T2[:, :].rearrange("p (h d) -> p h d", h=H),
                                  AM[:, :].rearrange("p (h d) -> p h d", h=H),
                                  w2[:, p, a, :].rearrange("p (h o) -> p h o", o=1).broadcast_to([P, H, DK]),
                                  ALU.mult).then_inc(s_t2, 1)

            def out_rows(h, n, p, a):
                bank, free = got(dve, f"OUT{a}", h)
                dve.wait_ge(s_of, n + 1)
                dve.tensor_tensor(outt[:, a, :], bank[:, :], xu[:, p, a, :], ALU.add).then_inc(free, 1)

            def router(p, col):
                for a in range(TILES):
                    link(dve.tensor_tensor_reduce(junk[:, :], xn[:, p, a, :], rw[:, :], 1.0, 0.0, ALU.mult, ALU.add,
                                                  wt[:, a:a + 1]))
                link(dve.tensor_copy(col, wt[:, :]))

            def half(m, i, p, first=False, ln=True, stage1=True):
                pn = 1 - p
                n2 = (m + 1) * 2 if stage1 else None
                softmax_in(m, 0)
                if not first:
                    low_a(m, m * 2 - 1, 1)
                p_transpose(m, 0)
                if stage1:
                    sigma(m, "QT", 0, SQT[:, pn, 0:2, :], s_sq)
                if not first:
                    out_rows(m, m * 2 - 1, pn, 1)
                    if stage1:
                        moved(dve, "OUT1", m)
                if stage1:
                    sigma(m, "QT", 1, SQT[:, pn, 2:4, :], s_sq)
                m_next(m, 0)
                if stage1:
                    residual(pn)
                if ln:
                    statistics(i + 1, p)
                softmax_part(m, 0)
                if stage1:
                    sigma(m, "KT", 0, SKT[:, 0:2, :], s_sk)
                m_next(m, 1)
                memory_part(m, p, 0)
                softmax_in(m, 1)
                low_a(m, m * 2, 0)
                p_transpose(m, 1)
                if stage1:
                    sigma(m, "KT", 1, SKT[:, 2:4, :], s_sk)
                if stage1:
                    z_chain(m + 1, n2, pn)
                m_next(m, 2)
                if ln:
                    deviation()
                softmax_part(m, 1)
                if ln:
                    normalise(m + 2, p)
                dve.wait_ge(s_xu, m + 1)
                out_rows(m, m * 2, p, 0)
                m_next(m, 3)
                if stage1:
                    denominators(m, n2, pn)
                if ln:
                    low_x(m, (m + 2) * 2, "XT", 0)
                    low_x(m, (m + 2) * 2, "XT", 1)
                memory_part(m, p, 1)
                if stage1:
                    previous_values(m, pn)
                if ln:
                    router(p, wcol[:, bass.ds((m + 2) * 2, 2)])

            def beta_factors():
                dve.wait_ge(s_const, 1)
                dve.wait_ge(s_rows, 16 * 3)
                dve.wait_ge(s_be, 1)
                link(dve.tensor_scalar(bs[:, :], be[:, :], 1.0, None, ALU.add))
                link(dve.reciprocal(betas[:, :], bs[:, :]))
                link(dve.tensor_scalar(omb[:, :, :].rearrange("p j g -> p g j"),
                                       betas[:, :].rearrange("p (g j) -> p g j", g=G), -1.0, 1.0, ALU.mult, ALU.add))

            def low_weights():
                for n, (raw, (high, low)) in enumerate(raw_weights):
                    dve.wait_ge(s_w[n], 16)
                    dve.wait_ge(s_wh, n + 1)
                    dve.tensor_tensor(low[:, :, :].rearrange("p c n -> p (c n)"),
                                      raw[:, :, :, :].rearrange("p a b n -> p (a b n)"),
                                      high[:, :, :].rearrange("p c n -> p (c n)").bitcast(F32),
                                      ALU.subtract).then_inc(s_wl, 1)

            LINKS = 72
            for s in (s_m, s_t1, s_t2):
                dve.sem_inc(s, 1)
            for n in range(2):
                statistics(0, n)
                deviation()
                normalise(n, n)
                if n == 0:
                    low_weights()
                    residual(0)
                    low_x(None, 0, "XF", 0)
                    low_x(None, 0, "XF", 1)
                    beta_factors()
                router(n, wcol[:, 2 * n:2 * n + 2])
            for k in range(2):
                sigma(None, "QT", k, SQT[:, 0, 2 * k:2 * k + 2, :], s_sq)
            for k in range(2):
                sigma(None, "KT", k, SKT[:, 2 * k:2 * k + 2, :], s_sk)
            z_chain(0, 0, 0)
            denominators(None, 0, 0)
            previous_values(None, 0)
            low_x(None, 2, "XT", 0)
            low_x(None, 2, "XT", 1)
            half(0, 0, 0, first=True)
            half(1, 0, 1)
            start = done[0]
            with dve.Fori(1, PAIRS) as i:
                done[0] = 0
                base[0] = i * LINKS + (start - LINKS)
                half(i * 2, i, 0)
                half(i * 2 + 1, i, 1)
                assert done[0] == LINKS, done[0]
            base[0] = start + (PAIRS - 1) * LINKS
            done[0] = 0
            half(NB - 2, PAIRS, 0, ln=False)
            half(NB - 1, PAIRS, 1, ln=False, stage1=False)
            low_a(NB, 2 * NB - 1, 1)
            out_rows(NB, 2 * NB - 1, 1, 1)
            dve.tensor_scalar(wcol[:, :], wcol[:, :], rb[:, 0:1], None, ALU.add)

        @block.tensor
        def _(pe):
            def x_transposes(m, n, pn, name, k):
                if k == 0:
                    pe.wait_ge(s_ln, n + 1)
                bank, full = take(pe, f"{name}{k}", m)
                for c in range(2):
                    for a in range(TILES):
                        o = c * BT + a * P
                        ch = 2 * k + c
                        ins = pe.transpose(bank[:, o:o + P], xn[:, pn, a, ch * P:ch * P + P], ident[:, :])
                ins.then_inc(full, 1)

            PARTS = ((0, 0), (0, 1), (1, 0))

            def feature(m, name, w, k, before=None, half=None):
                if before is not None:
                    for x in (0, 1):
                        moved(pe, f"{before[0]}{x}", before[1])
                bank, full = take(pe, f"{name}{k}", m)
                for g in range(2) if half is None else (half,):
                    o = (2 * k + g) * P
                    for n, (hx, hw) in enumerate(PARTS):
                        for c in range(G):
                            ins = pe.matmul(bank[:, g * BT:g * BT + BT], w[hw][:, c, o:o + P], xnT[hx][:, c, :],
                                            start=n + c == 0, stop=n == 2 and c == G - 1)
                if half != 0:
                    ins.then_inc(full, 1)

            def values(m, a, parts=range(3)):
                bank, full = take(pe, f"V{a}", m)
                for n in parts:
                    hx, hw = PARTS[n]
                    for c in range(G):
                        ins = pe.matmul(bank[:, :], xnT[hx][:, c, a * P:a * P + P], wv[hw][:, c, :],
                                        start=n + c == 0, stop=n == 2 and c == G - 1)
                if parts[-1] == 2:
                    ins.then_inc(full, 1)

            def sk_rows(m, n2, a):
                if a == 0:
                    pe.wait_ge(s_sk, n2 + 2)
                bank, full = take(pe, f"SK{a}", m)
                for g in range(G):
                    ins = pe.transpose(bank[:, g * P:g * P + P], SKT[:, g, a * P:a * P + P], ident[:, :])
                ins.then_inc(full, 1)

            def denominators(m, n, pn):
                pe.wait_ge(s_zbd, n + 1)
                pe.wait_ge(s_sq, n * 2 + 2)
                bank, full = take(pe, "DEN", m)
                for q in range(2):
                    for g in range(G):
                        rhs = SKT[:, g, :] if q == 0 else SQT[:, pn, g, :]
                        ins = pe.matmul(bank[32 * g:32 * g + 32, q * BT:q * BT + BT], Zbd[:, pn, g, :], rhs,
                                        start=True, stop=True)
                ins.then_inc(full, 1)

            def den_transposes(m):
                moved(pe, "DEN", m)
                bank, full = take(pe, "DNT", m)
                for c in range(4):
                    ins = pe.transpose(bank[:, c * P:c * P + P], DT[:, c * P:c * P + P], ident[:, :])
                ins.then_inc(full, 1)

            def mask(m, a):
                pe.wait_ge(s_t1, m * 2 + a + 1)
                for j in range(J):
                    pe.matmul(S[:, j, a * 256:a * 256 + 256].rearrange("p (g k) -> p g k", g=G), identb[:, :],
                              causal[:, :].rearrange("p (o k) -> p o k", o=1).broadcast_to([P, G, SEG]),
                              start=True, stop=False, skip_group_check=True)

            def scores(p, a, b):
                t = a * P + b * SEG
                for g in range(G):
                    for j in range(J):
                        q = slice(DK * j, DK * j + DK)
                        o = a * 256 + g * SEG
                        ins = pe.matmul(S[b * SEG:b * SEG + SEG, j, o:o + SEG], QT[q, p, g, t:t + SEG],
                                        KT[q, p, g, t:t + SEG], start=False, stop=(g == G - 1),
                                        skip_group_check=True)
                if b == 1:
                    ins.then_inc(s_S, 1)

            def a_and_b(m, p, sg):
                a, b = sg // 2, sg % 2
                if sg == 0:
                    pe.wait_ge(s_dsk, m * 2 + 2)
                pe.wait_ge(s_m, m * SEGS + sg + 1)
                alone(pe, s_alone_pe)
                t = slice(b * SEG, b * SEG + SEG)
                for g in range(G):
                    for j in range(J):
                        h = g * J + j
                        ins = pe.matmul(AB[DK * j:DK * j + DK, b, g, :, :], SK[t, p, a, h * DK:h * DK + DK],
                                        DV[t, p, a, :, h, 0:DK], start=g == 0, stop=g == G - 1,
                                        skip_group_check=True)
                ins.then_inc(s_ab, 1)

            def t_times_m(m, sg):
                b = sg % 2
                pe.wait_ge(s_na, m * SEGS + (sg + 1))
                alone(pe, s_alone_pe)
                for g in range(G):
                    for j in range(J):
                        q = slice(DK * j, DK * j + DK)
                        ins = pe.matmul(AB[q, b, g, 1, :], NA[q, b, g, :], M[q, b, g, :], start=False,
                                        stop=g == G - 1, skip_group_check=True)
                ins.then_inc(s_tm, 1)

            def memory(m, p, sg):
                a, b = sg // 2, sg % 2
                t = a * P + b * SEG
                pe.wait_ge(s_mbd, m * SEGS + sg + 1)
                if b == 0:
                    pe.wait_ge(s_t2, m * 2 + a + 1)
                for g in range(G):
                    ins = pe.matmul(AM[b * SEG:b * SEG + SEG, g * P:g * P + P], SQT[:, p, g, t:t + SEG],
                                    Mbd[:, b, g, :], start=True, stop=True)
                ins.then_inc(s_am, 1)

            def pv(m, mh, p, a, gs):
                if gs[0] == 0:
                    pe.wait_ge(s_pt, m * 2 + (a + 1))
                    if a == 0:
                        pe.wait_ge(s_vs[p], (mh + 1) * 32)
                    alone(pe, s_alone_pe)
                for g in gs:
                    for j in range(J):
                        h = g * J + j
                        o = a * 256 + g * VW
                        for q in range(4):
                            r = slice(32 * q, 32 * q + 32)
                            dst = S[r, j, o:o + VW]
                            own = (q % 2) * 32
                            ins = pe.matmul(dst, PT[r, j, g, own:own + 32], DV[r, p, a, 1, h, :],
                                            start=True, stop=q % 2 == 0)
                            if q % 2:
                                ins = pe.matmul(dst, PT[r, j, g, 0:32], VS[r, p, a, h, :], start=False, stop=True)
                if gs[-1] == G - 1:
                    ins.then_inc(s_pv, 1)

            def as_transposes(h, n, a):
                pe.wait_ge(s_as, n + 2)
                bank, full = take(pe, f"AST{a}", h)
                for g in range(G):
                    ins = pe.transpose(bank[:, g * P:g * P + P], As[:, g * P:g * P + P], ident[:, :])
                ins.then_inc(full, 1)

            def out_proj(h, a):
                moved(pe, f"AST{a}", h)
                bank, full = take(pe, f"OUT{a}", h)
                for n, (ha, hw) in enumerate(PARTS):
                    for g in range(G):
                        ins = pe.matmul(bank[:, :], AT[ha][:, g, :], wo[hw][:, g, :], start=n + g == 0,
                                        stop=n == 2 and g == G - 1)
                ins.then_inc(full, 1)

            def half(m, mh, p, first=False, ln=True, stage1=True):
                pn = 1 - p
                n = m + 1 if stage1 else None
                n2 = (m + 1) * 2 if stage1 else None
                mask(m, 0)
                scores(p, 0, 0)
                if stage1:
                    feature(m, "QT", wq, 0, ("XT", None if isinstance(m, int) and m == 0 else m - 1), half=0)
                scores(p, 0, 1)
                if not first:
                    as_transposes(m, m * 2 - 1, 1)
                if stage1:
                    feature(m, "QT", wq, 0, half=1)
                a_and_b(m, p, 0)
                if not first:
                    out_proj(m, 1)
                if stage1:
                    feature(m, "QT", wq, 1, half=0)
                t_times_m(m, 0)
                memory(m, p, 0)
                if stage1:
                    feature(m, "QT", wq, 1, half=1)
                pv(m, mh, p, 0, (0, 1))
                if stage1:
                    feature(m, "KT", wk, 0, half=0)
                pv(m, mh, p, 0, (2, 3))
                a_and_b(m, p, 1)
                if stage1:
                    feature(m, "KT", wk, 0, half=1)
                t_times_m(m, 1)
                memory(m, p, 1)
                mask(m, 1)
                scores(p, 1, 0)
                if stage1:
                    feature(m, "KT", wk, 1, half=0)
                scores(p, 1, 1)
                as_transposes(m, m * 2, 0)
                if stage1:
                    feature(m, "KT", wk, 1, half=1)
                a_and_b(m, p, 2)
                if stage1:
                    values(m, 0)
                t_times_m(m, 2)
                memory(m, p, 2)
                if stage1:
                    values(m, 1, (0,))
                pv(m, mh, p, 1, (0, 1))
                if stage1:
                    values(m, 1, (1,))
                pv(m, mh, p, 1, (2, 3))
                if stage1:
                    values(m, 1, (2,))
                a_and_b(m, p, 3)
                if stage1:
                    sk_rows(m, n2, 0)
                    sk_rows(m, n2, 1)
                out_proj(m, 0)
                if stage1:
                    denominators(m, n, pn)
                t_times_m(m, 3)
                if ln:
                    x_transposes(m, m + 2, p, "XT", 0)
                if stage1:
                    den_transposes(m)
                memory(m, p, 3)
                if ln:
                    x_transposes(m, m + 2, p, "XT", 1)

            pe.wait_ge(s_const, 1)
            x_transposes(None, 0, 0, "XF", 0)
            x_transposes(None, 0, 0, "XF", 1)
            pe.wait_ge(s_wl, 4)
            feature(None, "QT", wq, 0, ("XF", None))
            feature(None, "QT", wq, 1)
            feature(None, "KT", wk, 0)
            feature(None, "KT", wk, 1)
            values(None, 0)
            values(None, 1)
            sk_rows(None, 0, 0)
            sk_rows(None, 0, 1)
            denominators(None, 0, 0)
            den_transposes(None)
            x_transposes(None, 1, 1, "XT", 0)
            x_transposes(None, 1, 1, "XT", 1)
            half(0, 0, 0, first=True)
            half(1, 0, 1)
            with pe.Fori(1, PAIRS) as i:
                half(i * 2, i, 0)
                half(i * 2 + 1, i, 1)
            half(NB - 2, PAIRS, 0, ln=False)
            half(NB - 1, PAIRS, 1, ln=False, stage1=False)
            as_transposes(NB, 2 * NB - 1, 1)
            out_proj(NB, 1)


def select_tokens(nc, w, thr, idx, K, list_dram):
    NT = w.shape[1]
    N = P * NT
    Q = K // P
    BIG = 65536.0
    KNEG = float(N - K + 1)

    with ExitStack() as ctx:
        def sb(name, shape, dt=F32):
            return ctx.enter_context(nc.sbuf_tensor(name, shape, dt))

        def sem(name):
            return ctx.enter_context(nc.semaphore(name))

        onesP = sb("onesP", [P, P])
        before = sb("before", [P, P])
        oneT = sb("oneT", [P, NT])
        hit = sb("hit", [P, NT])
        y = sb("y", [P, NT])
        cnt = sb("cnt", [P, 2])
        flag = sb("flag", [P, 1])
        sign = sb("sign", [P, 1])
        kk = sb("kk", [P, 1])
        bitf = sb("bitf", [P, 1])
        biti = sb("biti", [P, 1], I32)
        cur = sb("cur", [P, 1], I32)
        cand = sb("cand", [P, 1], I32)
        keep = sb("keep", [P, 1], I32)
        lim = sb("lim", [P, 1])
        gt = sb("gt", [P, NT])
        eq = sb("eq", [P, NT])
        chosen = sb("chosen", [P, NT])
        tot = sb("tot", [P, NT])
        run = sb("run", [P, NT])
        place = sb("place", [P, NT])
        away = sb("away", [P, NT])
        dest = sb("dest", [P, NT], U32)
        token = sb("token", [P, NT], U32)
        zero = sb("zero", [P, 1], U32)
        pc = ctx.enter_context(nc.psum_tensor("pc", [P, 512], F32))
        pp = ctx.enter_context(nc.psum_tensor("pp", [P, 512], F32))
        pt = ctx.enter_context(nc.psum_tensor("pt", [P, 512], F32))

        s_k0 = sem("s_k0")
        s_k = sem("s_k")
        s_cnt = sem("s_cnt")
        s_tot = sem("s_tot")
        s_step = sem("s_step")
        s_x = sem("s_mark")
        s_pre = sem("s_pre")
        s_dest = sem("s_dest")
        s_pad = sem("s_pad")
        s_sc = sem("s_scat")
        s_idx = sem("s_idx")

        block = ctx.enter_context(nc.Block())

        @block.gpsimd
        def _(pool):
            pool.memset(onesP[:, :], 1.0)
            pool.memset(oneT[:, :], 1.0)
            pool.memset(zero[:, :], 0)
            pool.iota(token[:, :], pattern=[[P, NT]], base=0, channel_multiplier=1)
            pool.memset(before[:, :], 1.0).then_inc(s_k0, 1)
            pool.wait_ge(s_k0, 1)
            pool.affine_select(out=before[:, :], in_=before[:, :], compare_op=ALU.is_gt, fill=0.0,
                               base=0, pattern=[[1, P]], channel_multiplier=-1).then_inc(s_k, 1)
            pool.wait_ge(s_k, 1)
            pool.dma_start(list_dram[K - 1:K, :], zero[0:1, :]).then_inc(s_pad, 16)
            pool.wait_ge(s_pad, 16)
            pool.wait_ge(s_dest, 1)
            for j in range(NT):
                pool.indirect_dma_start(list_dram, bass.IndirectOffsetOnAxis(ap=dest[:, j:j + 1], axis=0),
                                        token[:, j:j + 1], None, bounds_check=K - 2,
                                        oob_is_err=False).then_inc(s_sc, 16)
            pool.wait_ge(s_sc, 16 * NT)
            pool.dma_start(idx[:, :], list_dram.rearrange("(p q) a -> p (q a)", q=Q)).then_inc(s_idx, 16)
            pool.wait_ge(s_idx, 16)

        @block.tensor
        def _(pe):
            pe.wait_ge(s_k, 1)

            def total(n):
                pe.wait_ge(s_cnt, n + 1)
                pe.matmul(pc[:, 0:2], onesP[:, :], cnt[:, :], start=True, stop=True).then_inc(s_tot, 1)

            total(0)
            with pe.Fori(0, 31) as i:
                total(i + 1)
            total(32)
            for n, x in enumerate((eq, chosen)):
                pe.wait_ge(s_x, n + 1)
                pe.matmul(pp[:, 0:NT], before[:, :], x[:, :], start=True, stop=True)
                pe.matmul(pt[:, 0:NT], onesP[:, :], x[:, :], start=True, stop=True).then_inc(s_pre, 1)

        @block.vector
        def _(dve):
            done = [0]
            base = [0]

            def link(ins):
                done[0] += 1
                ins.then_inc(s_step, 1)
                dve.wait_ge(s_step, base[0] + done[0])

            def count(src, level, op, n, out):
                dve.scalar_tensor_tensor(out=out, in0=src, scalar=level, in1=oneT[:, :], op0=op, op1=ALU.mult,
                                         accum_out=cnt[:, 0:1]).then_inc(s_cnt, 1)
                dve.wait_ge(s_tot, n + 1)

            dve.wait_ge(s_k, 1)
            link(dve.memset(cnt[:, :], 0.0))
            link(dve.memset(cur[:, :], 0))
            link(dve.memset(bitf[:, :], float(2 ** 30)))
            link(dve.memset(biti[:, :], 2 ** 30))
            count(w[:, :], 0.0, ALU.is_ge, 0, hit[:, :])
            link(dve.tensor_scalar(flag[:, :], pc[:, 0:1], float(K), None, ALU.is_ge))
            link(dve.tensor_scalar(sign[:, :], flag[:, :], 2.0, -1.0, ALU.mult, ALU.add))
            link(dve.tensor_scalar(kk[:, :], flag[:, :], float(K) - KNEG, KNEG, ALU.mult, ALU.add))
            link(dve.tensor_scalar(y[:, :], w[:, :], sign[:, 0:1], None, ALU.mult))
            start = done[0]
            LINKS = 5
            with dve.Fori(0, 31) as i:
                done[0] = 0
                base[0] = i * LINKS + start
                link(dve.tensor_tensor(cand[:, :], cur[:, :], biti[:, :], ALU.bitwise_or))
                count(y[:, :], cand[:, 0:1].bitcast(F32), ALU.is_ge, i + 1, hit[:, :])
                link(dve.tensor_scalar(keep[:, :], pc[:, 0:1], kk[:, 0:1], bitf[:, 0:1], ALU.is_ge, ALU.mult))
                link(dve.tensor_tensor(cur[:, :], cur[:, :], keep[:, :], ALU.bitwise_or))
                link(dve.tensor_scalar(bitf[:, :], bitf[:, :], 0.5, None, ALU.mult))
                link(dve.tensor_copy(biti[:, :], bitf[:, :]))
                assert done[0] == LINKS, done[0]
            base[0] = start + 31 * LINKS
            done[0] = 0
            link(dve.tensor_tensor(thr[:, :], cur[:, :].bitcast(F32), sign[:, :], ALU.mult))
            count(w[:, :], thr[:, 0:1], ALU.is_gt, 32, gt[:, :])
            link(dve.tensor_scalar(lim[:, :], pc[:, 0:1], -1.0, float(K - 1), ALU.mult, ALU.add))
            dve.tensor_scalar(eq[:, :], w[:, :], thr[:, 0:1], None, ALU.is_equal).then_inc(s_x, 1)

            def before_each(n):
                dve.wait_ge(s_pre, n + 1)
                link(dve.tensor_copy(tot[:, :], pt[:, 0:NT]))
                link(dve.tensor_tensor_scan(run[:, :], oneT[:, :], tot[:, :], 0.0, ALU.mult, ALU.add))
                link(dve.tensor_tensor(run[:, :], run[:, :], tot[:, :], ALU.subtract))
                link(dve.tensor_tensor(place[:, :], pp[:, 0:NT], run[:, :], ALU.add))

            before_each(0)
            link(dve.scalar_tensor_tensor(out=hit[:, :], in0=place[:, :], scalar=lim[:, 0:1], in1=eq[:, :],
                                          op0=ALU.is_lt, op1=ALU.mult))
            dve.tensor_tensor(chosen[:, :], gt[:, :], hit[:, :], ALU.add).then_inc(s_x, 1)
            dve.wait_ge(s_x, 2)
            before_each(1)
            link(dve.tensor_scalar(away[:, :], chosen[:, :], -BIG, BIG, ALU.mult, ALU.add))
            link(dve.tensor_tensor(place[:, :], place[:, :], chosen[:, :], ALU.mult))
            dve.tensor_tensor(dest[:, :], place[:, :], away[:, :], ALU.add).then_inc(s_dest, 1)


def rsqrt(dve, link, y, v, t, steps=4, guess=True):
    if guess:
        link(dve.tensor_scalar(y.bitcast(I32), v.bitcast(I32), -0.5, MAGIC, ALU.mult, ALU.add))
    for _ in range(steps):
        link(dve.scalar_tensor_tensor(out=t, in0=y, scalar=-0.5, in1=y, op0=ALU.mult, op1=ALU.mult))
        link(dve.tensor_tensor(t, t, v, ALU.mult))
        link(dve.scalar_tensor_tensor(out=y, in0=t, scalar=1.5, in1=y, op0=ALU.add, op1=ALU.mult))


def feed_forward(nc, x, maskT, positions, router_w, router_b, wq_d, wk_d, wv_d, wo_d, w1_d, w2_d, ln1, ln2,
                 thr, idx, out, cols_dram):
    D = x.shape[1]
    F = w1_d.shape[1]
    C = maskT.shape[0]
    H, DK = 16, 32
    Q = idx.shape[1]
    K = Q * P
    G = D // P
    J = P // DK
    CC = C // P
    FC = F // P
    HF = DK // 2
    INV = 1.0 / np.sqrt(np.float32(DK))
    freq = (np.float32(1.0) / np.float32(10000.0) ** (np.arange(0, DK, 2, dtype=np.float32) / np.float32(DK)))
    TWO_PI = 2.0 * np.pi
    C1 = 6.28125
    C2 = float(np.float32(np.floor((TWO_PI - C1) * 2 ** 20) / 2 ** 20))
    C3 = float(np.float32(TWO_PI - C1 - C2))
    ROUND = 12582912.0
    PI = float(np.nextafter(np.float32(np.pi), np.float32(0)))

    with ExitStack() as ctx:
        def sb(name, shape, dt=F32, c=ctx):
            return c.enter_context(nc.sbuf_tensor(name, shape, dt))

        def sem(name, c=ctx):
            return c.enter_context(nc.semaphore(name))

        ident = sb("ident2", [P, P])
        xs = sb("xs", [P, Q, D])
        nab = sb("nab", [P, Q])
        wsel = sb("wsel", [P, Q])
        above = sb("above", [P, Q])
        cidx = sb("cidx", [P, Q], U32)
        l2 = sb("l2", [P, D])
        xs2 = sb("xs2", [P, Q, D])
        x1T = sb("x1T", [P, G, K])
        ms = sb("ms", [P, Q])
        rr = sb("rr", [P, Q])
        rt = sb("rt", [P, Q])

        mid = ctx.enter_context(ExitStack())
        qrow = xs2
        KS = sb("KS", [P, H, K], F32R, c=mid)
        V = sb("V2", [P, Q, D], c=mid)
        with ExitStack() as c1:
            wq = sb("wq2", [P, G, D], c=c1)
            wk = sb("wk2", [P, G, D], c=c1)
            wv = x1T[:, 0:2, :].rearrange("p g (a n) -> p (g a) n", n=D)
            mrow = x1T[:, 2:4, :]
            rw = sb("rw2", [P, D], c=c1)
            rb = sb("rb2", [P, 1], c=c1)
            pos = sb("pos", [P, Q], I32, c=c1)
            posf = sb("posf", [P, Q], c=c1)
            l1 = sb("l1", [P, D], c=c1)
            c2 = sb("c2", [P, 2, Q], U32, c=c1)
            inv = sb("inv", [P, HF], c=c1)
            ang = sb("ang", [P, Q * HF], c=c1)
            turn = sb("turn", [P, Q * HF], c=c1)
            angc = sb("angc", [P, Q * HF], c=c1)
            sin = sb("sin", [P, Q, HF], c=c1)
            cos = sb("cos", [P, Q, HF], c=c1)
            coss = sb("coss", [P, 2, Q, HF], c=c1)
            sins = sb("sins", [P, 2, Q, HF], c=c1)
            nsins = sb("nsins", [P, 2, Q, HF], c=c1)
            stats = sb("stats2", [P, Q, 6], c=c1)
            mv = sb("mv2", [P, Q, 2], c=c1)
            var = sb("var2", [P, Q], c=c1)
            rstd = sb("rstd2", [P, Q], c=c1)
            rt0 = sb("rt0", [P, Q], c=c1)
            hn = sb("hn", [P, D], c=c1)
            hnT = sb("hnT", [P, G, P], c=c1)
            qa = sb("qa", [P, D], c=c1)
            junk = qa
            qb = sb("qb", [P, D], c=c1)
            junk2 = sb("junk2", [P, 1], c=c1)
            krow = sb("krow", [P, D], c=c1)
            kst = sb("kst", [P, H, 4, DK], F32R, c=c1)
            mcol = sb("mcol", [P, 2, P * 8], c=c1)
            bank = [c1.enter_context(nc.psum_tensor(f"fb{i}", [P, 512], F32)) for i in range(6)]
            tb = [c1.enter_context(nc.psum_tensor(f"ft{i}", [P, 512], F32)) for i in range(2)]

            s_w = sem("s_w2", c1)
            s_xg = sem("s_xg", c1)
            s_rows = sem("s_rows2", c1)
            s_pos = sem("s_pos", c1)
            s_ci = sem("s_ci", c1)
            s_mr = [sem("s_mr0", c1), sem("s_mr1", c1)]
            s_mt = sem("s_mt", c1)
            s_mc = sem("s_mc", c1)
            s_mw = [sem("s_mw0", c1), sem("s_mw1", c1)]
            s_k0 = sem("s_l0", c1)
            s_k = sem("s_l", c1)
            s_st = sem("s_st", c1)
            s_pool = sem("s_pool", c1)
            s_xn = sem("s_xn", c1)
            s_ms = sem("s_ms", c1)
            s_ang = sem("s_ang", c1)
            s_sin = sem("s_sin", c1)
            s_hn = sem("s_hn", c1)
            s_ht = sem("s_ht", c1)
            s_hc = sem("s_hc", c1)
            s_q = sem("s_q2", c1)
            s_vc = sem("s_vc", c1)
            s_r = sem("s_r", c1)
            s_kh = sem("s_kh", c1)
            s_kl = sem("s_kl", c1)
            s_rt = sem("s_rt", c1)
            s_kt = sem("s_kt", c1)

            block = c1.enter_context(nc.Block())

            @block.sync
            def _(sp):
                for w_, d_ in ((wq, wq_d), (wk, wk_d), (wv, wv_d)):
                    sp.dma_start(w_[:, :, :], d_.rearrange("(c p) n -> p c n", p=P)).then_inc(s_w, 16)
                for r_, d_ in ((l1, ln1), (l2, ln2)):
                    sp.dma_start(r_[:, :], d_.broadcast_to([P, D])).then_inc(s_w, 16)
                sp.dma_start(rw[:, :], router_w.rearrange("d a -> a d").broadcast_to([P, D])).then_inc(s_w, 16)
                sp.dma_start(rb[:, :], router_b.broadcast_to([P, 1])).then_inc(s_w, 16)
                for t in range(Q):
                    for hh in range(2):
                        n = 2 * t + hh
                        sp.wait_ge(s_mc, 2 * n + 2)
                        dst = cols_dram.rearrange("(u c p) k -> u p c k", u=2, p=P)[hh, :, :, t * P:t * P + P]
                        sp.dma_start(dst, mcol[:, hh, :].rearrange("p (c k) -> p c k", k=P)).then_inc(s_mw[hh], 16)

            @block.gpsimd
            def _(pool):
                for q in range(Q):
                    pool.indirect_dma_start(xs[:, q, :], None, x,
                                            bass.IndirectOffsetOnAxis(ap=idx[:, q:q + 1], axis=0)).then_inc(s_xg, 16)
                pool.wait_ge(s_ci, 1)
                for q in range(Q):
                    pool.indirect_dma_start(pos[:, q:q + 1], None, positions,
                                            bass.IndirectOffsetOnAxis(ap=cidx[:, q:q + 1], axis=0)).then_inc(s_pos, 16)
                pool.memset(ident[:, :], 0.0)
                for c in range(HF):
                    pool.memset(inv[:, c:c + 1], float(freq[c]))
                pool.memset(junk2[:, :], 0.0).then_inc(s_k0, 1)
                pool.wait_ge(s_k0, 1)
                pool.affine_select(out=ident[:, :], in_=ident[:, :], compare_op=ALU.not_equal, fill=1.0,
                                   base=0, pattern=[[-1, P]], channel_multiplier=1).then_inc(s_k, 1)
                for t in range(Q):
                    for hh in range(2):
                        n = 2 * t + hh
                        if t > 0:
                            pool.wait_ge(s_mt, 2 * (n - 2) + 2)
                        pool.indirect_dma_start(mrow[:, hh, :], None, maskT.rearrange("c (u e) -> (c u) e", u=2),
                                                bass.IndirectOffsetOnAxis(ap=c2[:, hh, t:t + 1], axis=0)).then_inc(s_mr[hh], 16)
                for hh in range(2):
                    pool.wait_ge(s_mw[hh], 16 * Q)

            def stacked(row):
                return row.rearrange("p (h o d) -> p h o d", o=1, d=DK).broadcast_to([P, H, 2, DK])

            @block.scalar
            def _(act):
                def masks(t):
                    for hh in range(2):
                        for e in range(2):
                            n = 4 * t + 2 * hh + e
                            act.wait_ge(s_mt, n + 1)
                            if t > 0 and e == 0:
                                act.wait_ge(s_mw[hh], 16 * t)
                            act.activation(mcol[:, hh, e * 512:e * 512 + 512], tb[n % 2][:, :], ACT.Copy).then_inc(s_mc, 1)

                for q in range(Q):
                    act.wait_ge(s_xn, q + 1)
                    if q > 0:
                        act.wait_ge(s_ms, q)
                    act.activation(junk[:, :], xs[:, q, :], ACT.Square, accum_out=ms[:, q:q + 1]).then_inc(s_ms, 1)
                act.wait_ge(s_ang, 1)
                act.activation(sin[:, :, :].rearrange("p q f -> p (q f)"), ang[:, :], ACT.Sin)
                act.activation(cos[:, :, :].rearrange("p q f -> p (q f)"), angc[:, :], ACT.Sin).then_inc(s_sin, 1)
                for t in range(Q):
                    act.wait_ge(s_ht, t + 1)
                    act.activation(hnT[:, :, :], bank[0][:, :].rearrange("p (g k) -> p g k", g=G), ACT.Copy).then_inc(s_hc, 1)
                    act.wait_ge(s_q, 3 * t + 3)
                    act.activation(V[:, t, :], bank[3][:, :], ACT.Copy).then_inc(s_vc, 1)
                    masks(t)
                    cols = slice(t * P, t * P + P)
                    act.wait_ge(s_r, 2 * t + 2)
                    act.activation(kst[:, :, 0:4:2, :], stacked(krow[:, :]), ACT.Copy).then_inc(s_kh, 1)
                    for g in range(G):
                        act.wait_ge(s_rt, G * t + g + 1)
                        act.activation(KS[:, 4 * g:4 * g + 4, cols],
                                       bank[4 + g % 2][:, :].rearrange("p (h k) -> p h k", h=4), ACT.Copy)\
                           .then_inc(s_kt, 1)

            @block.vector
            def _(dve):
                done = [0]

                def link(ins):
                    done[0] += 1
                    ins.then_inc(s_st, 1)
                    dve.wait_ge(s_st, done[0])

                def angles():
                    dve.wait_ge(s_pos, 16 * Q)
                    dve.wait_ge(s_k, 1)
                    link(dve.tensor_copy(posf[:, :], pos[:, :]))
                    a3 = ang[:, :].rearrange("p (q f) -> p q f", q=Q)
                    link(dve.tensor_tensor(a3, bc(posf[:, :], HF), bm(inv[:, :], Q), ALU.mult))
                    link(dve.tensor_scalar(turn[:, :], ang[:, :], 1.0 / TWO_PI, None, ALU.mult))
                    link(dve.tensor_scalar(turn[:, :], turn[:, :], ROUND, -ROUND, ALU.add, ALU.add))
                    for c in (C1, C2, C3):
                        link(dve.scalar_tensor_tensor(out=ang[:, :], in0=turn[:, :], scalar=-c, in1=ang[:, :],
                                                      op0=ALU.mult, op1=ALU.add))
                    link(dve.tensor_scalar(ang[:, :], ang[:, :], PI, -PI, ALU.min, ALU.max))
                    link(dve.tensor_scalar(angc[:, :], ang[:, :], TWO_PI / 4, None, ALU.add))
                    link(dve.tensor_scalar(turn[:, :], angc[:, :], PI, -TWO_PI, ALU.is_gt, ALU.mult))
                    link(dve.tensor_tensor(angc[:, :], angc[:, :], turn[:, :], ALU.add))
                    dve.tensor_scalar(angc[:, :], angc[:, :], PI, -PI, ALU.min, ALU.max).then_inc(s_ang, 1)

                link(dve.tensor_scalar(cidx[:, :], idx[:, :], float(C - 1), None, ALU.min))
                link(dve.tensor_scalar(c2[:, 0, :], cidx[:, :], 2.0, None, ALU.mult))
                dve.tensor_scalar(c2[:, 1, :], cidx[:, :], 2.0, 1.0, ALU.mult, ALU.add).then_inc(s_ci, 1)
                dve.wait_ge(s_xg, 16 * Q)
                for q in range(Q):
                    link(dve.bn_stats(stats[:, q, :], xs[:, q, :]))
                    link(dve.bn_aggr(mv[:, q, :], stats[:, q, :]))
                link(dve.tensor_scalar(var[:, :], mv[:, :, 1], 1e-5, None, ALU.add))
                rsqrt(dve, link, rstd[:, :], var[:, :], rt0[:, :])
                dve.wait_ge(s_w, 16 * 7)
                for q in range(Q):
                    dve.tensor_scalar(xs[:, q, :], xs[:, q, :], mv[:, q, 0:1], rstd[:, q:q + 1],
                                      ALU.subtract, ALU.mult).then_inc(s_xn, 1)
                angles()
                dve.wait_ge(s_xn, Q)
                dve.wait_ge(s_ms, Q)
                link(dve.tensor_scalar(ms[:, :], ms[:, :], 1.0 / D, 1e-6, ALU.mult, ALU.add))
                rsqrt(dve, link, rr[:, :], ms[:, :], rt[:, :])
                dve.wait_ge(s_sin, 1)
                for n, scale in ((0, float(INV)), (1, 1.0)):
                    dve.tensor_scalar(coss[:, n, :, :], cos[:, :, :], scale, None, ALU.mult)
                    dve.tensor_scalar(sins[:, n, :, :], sin[:, :, :], scale, None, ALU.mult)
                    link(dve.tensor_scalar(nsins[:, n, :, :], sin[:, :, :], -scale, None, ALU.mult))
                for t in range(Q):
                    if t > 0:
                        dve.wait_ge(s_ht, t)
                    dve.scalar_tensor_tensor(out=hn[:, :], in0=xs[:, t, :], scalar=rr[:, t:t + 1], in1=l1[:, :],
                                             op0=ALU.mult, op1=ALU.mult).then_inc(s_hn, 1)
                    for n in range(2):
                        dve.wait_ge(s_q, 3 * t + n + 1)
                        dve.wait_ge(s_r, 2 * t + n)
                        b3 = bank[1 + n][:, :].rearrange("p (h f) -> p h f", f=HF)
                        b4 = bank[1 + n][:, :].rearrange("p (h u f) -> p h u f", u=2, f=HF)
                        q4 = qb[:, :].rearrange("p (h u f) -> p h u f", u=2, f=HF)
                        link(dve.tensor_tensor(qa[:, :].rearrange("p (h f) -> p h f", f=HF), b3,
                                               bm(coss[:, n, t, :], 2 * H), ALU.mult))
                        link(dve.tensor_tensor(q4[:, :, 0, :], b4[:, :, 1, :], bm(nsins[:, n, t, :], H), ALU.mult))
                        link(dve.tensor_tensor(q4[:, :, 1, :], b4[:, :, 0, :], bm(sins[:, n, t, :], H), ALU.mult))
                        dve.tensor_tensor(qrow[:, t, :] if n == 0 else krow[:, :], qa[:, :], qb[:, :],
                                          ALU.add).then_inc(s_r, 1)
                    dve.wait_ge(s_kh, t + 1)
                    dve.wait_ge(s_r, 2 * t + 2)
                    dve.tensor_tensor(kst[:, :, 1:4:2, :], stacked(krow[:, :]), kst[:, :, 0:4:2, :].bitcast(F32),
                                      ALU.subtract).then_inc(s_kl, 1)
                    link(dve.tensor_tensor_reduce(junk[:, :], xs[:, t, :], rw[:, :], 1.0, 0.0, ALU.mult, ALU.add,
                                                  wsel[:, t:t + 1]))
                link(dve.tensor_scalar(wsel[:, :], wsel[:, :], rb[:, 0:1], None, ALU.add))
                link(dve.tensor_scalar(above[:, :], wsel[:, :], thr[:, 0:1], None, ALU.is_gt))
                link(dve.tensor_scalar(nab[:, :], above[:, :], -1.0, None, ALU.mult))

            @block.tensor
            def _(pe):
                pe.wait_ge(s_k, 1)
                pe.wait_ge(s_w, 16 * 7)

                def masks(t):
                    for hh in range(2):
                        pe.wait_ge(s_mr[hh], 16 * (t + 1))
                        for e in range(2):
                            n = 4 * t + 2 * hh + e
                            if n >= 2:
                                pe.wait_ge(s_mc, n - 1)
                            for c in range(4):
                                o = (4 * e + c) * P
                                ins = pe.transpose(tb[n % 2][:, c * P:c * P + P], mrow[:, hh, o:o + P], ident[:, :])
                            ins.then_inc(s_mt, 1)

                for t in range(Q):
                    pe.wait_ge(s_hn, t + 1)
                    if t > 0:
                        pe.wait_ge(s_hc, t)
                    for g in range(G):
                        ins = pe.transpose(bank[0][:, g * P:g * P + P], hn[:, g * P:g * P + P], ident[:, :])
                    ins.then_inc(s_ht, 1)
                    pe.wait_ge(s_hc, t + 1)
                    if t > 0:
                        pe.wait_ge(s_r, 2 * t)
                        pe.wait_ge(s_vc, t)
                    for n, w_ in enumerate((wq, wk, wv)):
                        for c in range(G):
                            ins = pe.matmul(bank[1 + n][:, :], hnT[:, c, :], w_[:, c, :], start=c == 0, stop=c == G - 1)
                        ins.then_inc(s_q, 1)
                    masks(t)
                    pe.wait_ge(s_kl, t + 1)
                    for g in range(G):
                        n = G * t + g
                        if n >= 2:
                            pe.wait_ge(s_kt, n - 1)
                        for j in range(4):
                            h = 4 * g + j
                            ins = pe.transpose(bank[4 + g % 2][:, j * P:j * P + P],
                                               kst[:, h, :, :].rearrange("p u d -> p (u d)").bitcast(F32), ident[:, :])
                        ins.then_inc(s_rt, 1)

        with ExitStack() as c2_:
            wo = sb("wo2", [P, G, D], c=c2_)
            QS = sb("QS", [P, H, P], F32R, c=c2_)
            qst = sb("qst", [P, H, 4, DK], F32R, c=c2_)
            mc = sb("mc", [P, 2, K], c=c2_)
            Sm = sb("Sm", [P, 4, K], c=c2_)
            mxs = sb("mxs", [P, 4, 2], c=c2_)
            rsum = sb("rsum", [P, 2, H], c=c2_)
            rinv = sb("rinv", [P, H], c=c2_)
            PTs = sb("PTs", [P, 4, Q, P], c=c2_)
            OTs = sb("OTs", [P, G, P], c=c2_)
            On = sb("On", [P, D], c=c2_)
            OnT = sb("OnT", [P, G, P], c=c2_)
            x1c = sb("x1c", [P, D], c=c2_)
            h2 = sb("h2", [P, D], c=c2_)
            m1 = sb("m1", [P, 1], c=c2_)
            v1 = sb("v1", [P, 1], c=c2_)
            r1 = sb("r1", [P, 1], c=c2_)
            t1 = sb("t1", [P, 1], c=c2_)
            Sp = [c2_.enter_context(nc.psum_tensor(f"Sp{i}", [P, 1024], F32)) for i in range(2)]
            Tp = [c2_.enter_context(nc.psum_tensor(f"Tp{i}", [P, 512], F32)) for i in range(2)]
            Op = c2_.enter_context(nc.psum_tensor("Op", [P, 512], F32))
            Wp = c2_.enter_context(nc.psum_tensor("Wp", [P, 512], F32))

            s_w = sem("s_w3", c2_)
            s_alone = sem("s_alone", c2_)
            s_mg = [sem("s_mg0", c2_), sem("s_mg1", c2_)]
            s_qh = sem("s_qh", c2_)
            s_ql = sem("s_ql", c2_)
            s_qp = sem("s_qp", c2_)
            s_qs = sem("s_qs", c2_)
            s_s = sem("s_s", c2_)
            s_sm = sem("s_sm", c2_)
            s_e = sem("s_e", c2_)
            s_t = sem("s_t", c2_)
            s_ta = sem("s_ta", c2_)
            s_td = sem("s_td", c2_)
            s_pv = sem("s_pv2", c2_)
            s_oc = sem("s_oc", c2_)
            s_on = sem("s_on", c2_)
            s_or = sem("s_or", c2_)
            s_ot = sem("s_ot", c2_)
            s_otc = sem("s_otc", c2_)
            s_wo = sem("s_wo", c2_)
            s_xc = sem("s_xc", c2_)
            s_h2 = sem("s_h2", c2_)
            s_h2t = sem("s_h2t", c2_)
            s_x1 = sem("s_x1", c2_)
            s_dv = sem("s_dv", c2_)
            KC = K - 1
            PAIRS = Q // 2 - 1

            def tile(t):
                return slice(t, t + 1) if isinstance(t, int) else bass.ds(t, 1)

            def cols(t):
                return slice(t * P, t * P + P) if isinstance(t, int) else bass.ds(t * P, P)

            block = c2_.enter_context(nc.Block())

            @block.sync
            def _(sp):
                sp.dma_start(wo[:, :, :], wo_d.rearrange("(c p) n -> p c n", p=P)).then_inc(s_w, 16)

            @block.gpsimd
            def _(pool):
                for t in range(Q):
                    if t >= 2:
                        pool.wait_ge(s_sm, (t - 1) * H + 1)
                    pool.indirect_dma_start(mc[:, t % 2, :], None, cols_dram,
                                            bass.IndirectOffsetOnAxis(ap=cidx[:, t:t + 1], axis=0))\
                        .then_inc(s_mg[t % 2], 16)
                for b in range(2):
                    pool.wait_ge(s_mg[b], 16 * (Q // 2))

            def q_rows(t):
                return qrow[:, tile(t), :].rearrange("p o (h d) -> p h o d", d=DK).broadcast_to([P, H, 2, DK])

            @block.scalar
            def _(act):
                def take_t(t, h):
                    act.wait_ge(s_t, t * (2 * H) + (2 * h + 1))
                    act.wait_ge(s_pv, t * G + (h // 4 + 1))
                    act.activation(PTs[:, h % 4, 0:4, :], Tp[0][:, :].rearrange("p (k q) -> p k q", k=4),
                                   ACT.Copy).then_inc(s_ta, 1)

                def take_o(t, g):
                    act.wait_ge(s_pv, t * G + (g + 2))
                    act.activation(OTs[:, g, :], Op[:, 0:P], ACT.Copy).then_inc(s_oc, 1)

                def stack(t):
                    act.activation(qst[:, :, 0:2, :], q_rows(t), ACT.Copy).then_inc(s_qh, 1)

                def take_stack(t, g):
                    act.wait_ge(s_qp, t * G + (g + 1))
                    act.activation(QS[:, 4 * g:4 * g + 4, :], Wp[:, :].rearrange("p (h k) -> p h k", h=4),
                                   ACT.Copy).then_inc(s_qs, 1)

                def take_on(t):
                    act.wait_ge(s_ot, t + 1)
                    act.activation(OnT[:, :, :], Wp[:, :].rearrange("p (g k) -> p g k", g=G), ACT.Copy).then_inc(s_otc, 1)

                def take_x1(t):
                    act.wait_ge(s_h2t, t + 1)
                    act.activation(x1T[:, :, cols(t)], Wp[:, :].rearrange("p (g k) -> p g k", g=G),
                                   ACT.Copy).then_inc(s_x1, 1)

                def heads(t, b, before=True, after=True):
                    for h in range(H):
                        act.wait_ge(s_sm, t * H + (h + 2))
                        act.activation(Sm[:, h % 4, 0:KC], Sm[:, h % 4, 0:KC], ACT.Exp, bias=mxs[:, h % 4, 1:2],
                                       accum_out=rsum[:, b, h:h + 1]).then_inc(s_e, 1)
                        if h == 1 and before:
                            take_o(t - 1, G - 1)
                        if h > 4 and h % 4 == 1:
                            take_o(t, h // 4 - 1)
                        if h > 0:
                            take_t(t, h - 1)
                        elif before:
                            take_t(t - 1, H - 1)
                        if h == 4 and before:
                            take_on(t - 1)
                        if h == 3 and after:
                            stack(t + 1)
                        if h in (9, 10, 11) and after:
                            take_stack(t + 1, h - 9)
                        if h == 13 and before:
                            take_x1(t - 1)
                        if h == 14 and after:
                            take_stack(t + 1, 3)

                act.sem_inc(s_ta, 1)
                act.sem_inc(s_oc, 1)
                stack(0)
                for g in range(G):
                    take_stack(0, g)
                heads(0, 0, before=False)
                with act.Fori(0, PAIRS) as i:
                    heads(i * 2 + 1, 1)
                    heads(i * 2 + 2, 0)
                heads(Q - 1, 1, after=False)
                take_t(Q - 1, H - 1)
                take_o(Q - 1, G - 1)
                take_on(Q - 1)
                take_x1(Q - 1)

            @block.vector
            def _(dve):
                done = [0]
                base = [0]

                def link(ins):
                    done[0] += 1
                    ins.then_inc(s_dv, 1)
                    dve.wait_ge(s_dv, base[0] + done[0])

                def take_t(t, h):
                    dve.wait_ge(s_t, t * (2 * H) + (2 * h + 2))
                    dve.wait_ge(s_pv, t * G + (h // 4 + 1))
                    dve.tensor_copy(PTs[:, h % 4, 4:8, :], Tp[1][:, :].rearrange("p (k q) -> p k q", k=4))\
                       .then_inc(s_td, 1)

                def stack(t):
                    dve.wait_ge(s_qh, t + 1)
                    alone(dve, s_alone)
                    dve.tensor_tensor(qst[:, :, 2:4, :], q_rows(t), qst[:, :, 0:2, :].bitcast(F32),
                                      ALU.subtract).then_inc(s_ql, 1)

                def weights(t, b):
                    dve.wait_ge(s_e, t * H + H)
                    link(dve.reciprocal(rinv[:, :], rsum[:, b, :]))

                def attention_rows(t):
                    dve.wait_ge(s_on, t + 1)
                    dve.tensor_tensor(On[:, :].rearrange("p (h d) -> p h d", h=H),
                                      Wp[:, :].rearrange("p (h d) -> p h d", h=H), bc(rinv[:, :], DK),
                                      ALU.mult).then_inc(s_or, 1)

                def second_norm(t, step):
                    if step == 0:
                        dve.wait_ge(s_wo, t + 1)
                        link(dve.tensor_tensor(x1c[:, :], Wp[:, :], xs[:, tile(t), :].rearrange("p o d -> p (o d)"),
                                               ALU.add))
                        dve.tensor_copy(xs2[:, tile(t), :].rearrange("p o d -> p (o d)"), x1c[:, :]).then_inc(s_xc, 1)
                    elif step == 1:
                        link(dve.tensor_tensor_reduce(h2[:, :], x1c[:, :], x1c[:, :], 1.0, 0.0, ALU.mult, ALU.add,
                                                      m1[:, :]))
                        link(dve.tensor_scalar(v1[:, :], m1[:, :], 1.0 / D, 1e-6, ALU.mult, ALU.add))
                        rsqrt(dve, link, r1[:, :], v1[:, :], t1[:, :], 0)
                    elif step < 4:
                        rsqrt(dve, link, r1[:, :], v1[:, :], t1[:, :], 2, False)
                    else:
                        dve.scalar_tensor_tensor(out=h2[:, :], in0=x1c[:, :], scalar=r1[:, 0:1], in1=l2[:, :],
                                                 op0=ALU.mult, op1=ALU.mult).then_inc(s_h2, 1)

                def keep(q):
                    link(dve.tensor_scalar(xs[:, q, :], xs[:, q, :], nab[:, q:q + 1], None, ALU.mult))
                    link(dve.scalar_tensor_tensor(out=xs[:, q, :], in0=xs2[:, q, :], scalar=wsel[:, q:q + 1],
                                                  in1=xs[:, q, :], op0=ALU.mult, op1=ALU.add))

                def heads(t, th, b, before=True, after=True):
                    dve.wait_ge(s_mg[b], th * 16 + 16)
                    for h in range(H):
                        dve.wait_ge(s_s, t * H + (h + 1))
                        if before or h >= 4:
                            dve.wait_ge(s_t, t * (2 * H) + 2 * (h - 3))
                        alone(dve, s_alone)
                        link(dve.tensor_tensor_reduce(Sm[:, h % 4, 0:KC], Sp[h % 2][:, 0:KC], mc[:, b, 0:KC], 1.0,
                                                      -3.0e38, ALU.add, ALU.max, mxs[:, h % 4, 0:1]))
                        dve.tensor_scalar(mxs[:, h % 4, 1:2], mxs[:, h % 4, 0:1], -1.0, None, ALU.mult)\
                           .then_inc(s_sm, 1)
                        if h > 0:
                            take_t(t, h - 1)
                        elif before:
                            take_t(t - 1, H - 1)
                            weights(t - 1, 1 - b)
                        if h == 2 and before:
                            attention_rows(t - 1)
                        if 6 <= h < 11 and before:
                            second_norm(t - 1, h - 6)
                        if h == 5 and after:
                            stack(t + 1)
                        if not after and (h < Q - 2 or h == 12):
                            keep(min(h, Q - 2))

                dve.sem_inc(s_sm, 1)
                dve.sem_inc(s_td, 1)
                dve.memset(Sm[:, :, KC:K], 0.0)
                stack(0)
                heads(0, 0, 0, before=False)
                start = done[0]
                LINKS = 66
                with dve.Fori(0, PAIRS) as i:
                    done[0] = 0
                    base[0] = i * LINKS + start
                    heads(i * 2 + 1, i, 1)
                    heads(i * 2 + 2, i + 1, 0)
                    assert done[0] == LINKS, done[0]
                done[0] = 0
                base[0] = start + PAIRS * LINKS
                heads(Q - 1, Q // 2 - 1, 1, after=False)
                take_t(Q - 1, H - 1)
                weights(Q - 1, 1)
                attention_rows(Q - 1)
                for step in range(5):
                    second_norm(Q - 1, step)
                keep(Q - 1)

            @block.tensor
            def _(pe):
                def score(t, h):
                    pe.wait_ge(s_qs, t * G + (h // 4 + 1))
                    if not (isinstance(t, int) and t == 0 and h < 2):
                        pe.wait_ge(s_sm, t * H + h)
                    for u in range(2):
                        ins = pe.matmul(Sp[h % 2][:, u * 512:u * 512 + 512], QS[:, h, :],
                                        KS[:, h, u * 512:u * 512 + 512], start=True, stop=True)
                    ins.then_inc(s_s, 1)

                def turn_p(t, h):
                    pe.wait_ge(s_e, t * H + (h + 1))
                    pe.wait_ge(s_ta, t * H + (h + 1))
                    for k in range(4):
                        ins = pe.transpose(Tp[0][:, k * P:k * P + P], Sm[:, h % 4, k * P:k * P + P], ident[:, :])
                    ins.then_inc(s_t, 1)
                    pe.wait_ge(s_td, t * H + (h + 1))
                    for k in range(4, 8):
                        ins = pe.transpose(Tp[1][:, (k - 4) * P:(k - 4) * P + P],
                                           Sm[:, h % 4, k * P:k * P + P], ident[:, :])
                    ins.then_inc(s_t, 1)

                def values(t, g):
                    pe.wait_ge(s_ta, t * H + (4 * g + 5))
                    pe.wait_ge(s_td, t * H + (4 * g + 5))
                    pe.wait_ge(s_oc, t * G + (g + 1))
                    for k in range(Q):
                        n = P if k < Q - 1 else P - 1
                        for j in range(J):
                            r = slice(DK * j, DK * j + DK)
                            h = g * J + j
                            ins = pe.matmul(Op[r, 0:P], V[0:n, k, h * DK:h * DK + DK], PTs[0:n, j, k, :],
                                            start=k == 0, stop=k == Q - 1)
                    ins.then_inc(s_pv, 1)

                def back(t):
                    pe.wait_ge(s_oc, t * G + (G + 1))
                    for g in range(G):
                        ins = pe.transpose(Wp[:, g * P:g * P + P], OTs[:, g, :], ident[:, :])
                    ins.then_inc(s_on, 1)

                def again(t):
                    pe.wait_ge(s_or, t + 1)
                    for g in range(G):
                        ins = pe.transpose(Wp[:, g * P:g * P + P], On[:, g * P:g * P + P], ident[:, :])
                    ins.then_inc(s_ot, 1)

                def project(t):
                    pe.wait_ge(s_otc, t + 1)
                    for g in range(G):
                        ins = pe.matmul(Wp[:, :], OnT[:, g, :], wo[:, g, :], start=g == 0, stop=g == G - 1)
                    ins.then_inc(s_wo, 1)

                def norm_t(t, stacks=False):
                    pe.wait_ge(s_h2, t + 1)
                    if stacks:
                        pe.wait_ge(s_qs, t * G + (2 * G + 3))
                    for g in range(G):
                        ins = pe.transpose(Wp[:, g * P:g * P + P], h2[:, g * P:g * P + P], ident[:, :])
                    ins.then_inc(s_h2t, 1)

                def stack(t, g, first=False):
                    if g == 0:
                        pe.wait_ge(s_ql, t + 1)
                        if not first:
                            pe.wait_ge(s_xc, t - 1)
                    else:
                        pe.wait_ge(s_qs, t * G + g)
                        if g == 3 and not first:
                            pe.wait_ge(s_x1, t - 1)
                    for j in range(4):
                        ins = pe.transpose(Wp[:, j * P:j * P + P],
                                           qst[:, 4 * g + j, :, :].rearrange("p u d -> p (u d)").bitcast(F32),
                                           ident[:, :])
                    ins.then_inc(s_qp, 1)

                def heads(t, before=True, after=True):
                    for h in range(H):
                        if h + 2 < H:
                            score(t, h + 2)
                        elif after:
                            score(t + 1, h + 2 - H)
                        if h > 0 and h % 4 == 0:
                            values(t, h // 4 - 1)
                        if h == 0 and before:
                            values(t - 1, G - 1)
                        turn_p(t, h)
                        if before and h == 1:
                            back(t - 1)
                        if before and h == 3:
                            again(t - 1)
                        if before and h == 5:
                            project(t - 1)
                        if after and h in (8, 9, 10):
                            stack(t + 1, h - 8, first=not before)
                        if before and h == 12:
                            norm_t(t - 1, after)
                        if after and h == 13:
                            stack(t + 1, 3, first=not before)

                pe.sem_inc(s_pv, 1)
                for g in range(G):
                    stack(0, g, first=True)
                score(0, 0)
                score(0, 1)
                pe.wait_ge(s_w, 16)
                heads(0, before=False)
                with pe.Fori(0, PAIRS) as i:
                    heads(i * 2 + 1)
                    heads(i * 2 + 2)
                heads(Q - 1, after=False)
                values(Q - 1, G - 1)
                back(Q - 1)
                again(Q - 1)
                project(Q - 1)
                norm_t(Q - 1)
        mid.close()
        mlp(nc, xs, xs2, x1T, wsel, w1_d, w2_d, idx, out)


def mlp(nc, rest, fin, x1T, wsel, w1_d, w2_d, idx, out):
    Q = rest.shape[1]
    D = rest.shape[2]
    F = w1_d.shape[1]
    K = Q * P
    G = D // P
    FC = F // P
    NT = 2 * P
    U = K // NT
    QU = NT // P
    PAIRS = FC // 2
    PARTS = ((0, 0), (0, 1), (1, 0))

    with ExitStack() as ctx:
        def sb(name, shape, dt=F32):
            return ctx.enter_context(nc.sbuf_tensor(name, shape, dt))

        def sem(name):
            return ctx.enter_context(nc.semaphore(name))

        w1 = [sb(f"w1m{i}", [P, G, F], F32R) for i in range(2)]
        w2 = [sb(f"w2m{i}", [P, FC, D], F32R) for i in range(2)]
        xT = [sb(f"xT{i}", [P, G, NT], F32R) for i in range(2)]
        gT = [sb(f"gT{i}", [P, 4, 2, NT], F32R) for i in range(2)]
        gelu = sb("gelu", [P, 2, 2 * NT])
        hb = [ctx.enter_context(nc.psum_tensor(f"hb{i}", [P, 2 * NT], F32)) for i in range(4)]
        yb = [ctx.enter_context(nc.psum_tensor(f"yb{i}", [P, D], F32)) for i in range(4)]

        SLOTS = 4
        s_wd = [sem(f"s_wd{i}") for i in range(SLOTS)]
        s_wh = sem("s_whm")
        s_wl = sem("s_wlm")
        s_xh = sem("s_xhm")
        s_xl = sem("s_xlm")
        s_h = sem("s_hm")
        s_g = sem("s_gm")
        s_gh = sem("s_ghm")
        s_gl = sem("s_glm")
        s_y = sem("s_ym")
        s_f = sem("s_fm")
        s_o = sem("s_om")

        def first(k):
            return max(0, 2 * k - 1)

        def second(k):
            return min(2 * k + 2, 2 * PAIRS - 1)

        sources = {}
        for k in range(PAIRS):
            sources[first(k)] = ([w[:, :, k * NT:k * NT + NT] for w in w1],
                                 w1_d[:, k * NT:k * NT + NT].rearrange("(c p) n -> p c n", p=P))
            sources[second(k)] = ([w[:, 2 * k:2 * k + 2, :] for w in w2],
                                  w2_d[2 * k * P:2 * k * P + 2 * P, :].rearrange("(c p) n -> p c n", p=P))
        assert len(sources) == 2 * PAIRS

        def place(n):
            o = (n % SLOTS) * 2
            raw = fin[:, o:o + 2, :]
            c = sources[n][0][0].shape[1]
            return raw if c == 2 else raw.rearrange("p a n -> p (a n)").rearrange("p (c n) -> p c n", c=c)

        block = ctx.enter_context(nc.Block())

        @block.sync
        def _(sp):
            for n in range(2 * PAIRS):
                if n >= SLOTS:
                    sp.wait_ge(s_wl, n - SLOTS + 1)
                sp.dma_start(place(n), sources[n][1]).then_inc(s_wd[n % SLOTS], 16)

        @block.tensor
        def _(pe):
            def hidden(n):
                u, k = n // PAIRS, n % PAIRS
                if k == 0:
                    pe.wait_ge(s_xl, u + 1)
                if u == 0:
                    pe.wait_ge(s_wl, first(k) + 1)
                if n >= 4:
                    pe.wait_ge(s_g, n - 3)
                for e in range(2):
                    f = 2 * k + e
                    for m, (hx, hw) in enumerate(PARTS):
                        for c in range(G):
                            ins = pe.matmul(hb[n % 4][:, e * NT:e * NT + NT], w1[hw][:, c, f * P:f * P + P],
                                            xT[hx][:, c, :], start=m + c == 0, stop=m == 2 and c == G - 1)
                ins.then_inc(s_h, 1)

            def rows(n):
                u, k = n // PAIRS, n % PAIRS
                if u == 0:
                    pe.wait_ge(s_wl, second(k) + 1)
                pe.wait_ge(s_gl, n + 1)
                if k == 0 and u >= 2:
                    pe.wait_ge(s_f, (u - 1) * QU)
                for q in range(QU):
                    for e in range(2):
                        f = 2 * k + e
                        for m, (hg, hw) in enumerate(PARTS):
                            ins = pe.matmul(yb[(u % 2) * QU + q][:, :], gT[hg][:, n % 4, e, q * P:q * P + P],
                                            w2[hw][:, f, :], start=f + m == 0, stop=f == FC - 1 and m == 2)
                ins.then_inc(s_y, 1)

            hidden(0)
            hidden(1)
            for n in range(U * PAIRS):
                if n + 2 < U * PAIRS:
                    hidden(n + 2)
                rows(n)

        @block.scalar
        def _(act):
            def high(n):
                act.wait_ge(s_wd[n % SLOTS], 16 * (n // SLOTS + 1))
                act.activation(sources[n][0][0], place(n), ACT.Copy).then_inc(s_wh, 1)

            def high_x(u):
                if u > 0:
                    act.wait_ge(s_h, u * PAIRS)
                act.activation(xT[0][:, :, :], x1T[:, :, u * NT:u * NT + NT], ACT.Copy).then_inc(s_xh, 1)

            high_x(0)
            high(0)
            high(1)
            for n in range(U * PAIRS):
                for e in (2, 3):
                    if 2 * n + e < 2 * PAIRS:
                        high(2 * n + e)
                if n % PAIRS == PAIRS - 1 and n + 1 < U * PAIRS:
                    high_x(n // PAIRS + 1)
                act.wait_ge(s_h, n + 1)
                if n >= 2:
                    act.wait_ge(s_gl, n - 1)
                act.activation(gelu[:, n % 2, :], hb[n % 4][:, :], ACT.Gelu_apprx_tanh).then_inc(s_g, 1)

        @block.vector
        def _(dve):
            def low(n):
                dve.wait_ge(s_wh, n + 1)
                h, l = sources[n][0]
                dve.tensor_tensor(l, place(n), h.bitcast(F32), ALU.subtract).then_inc(s_wl, 1)

            def low_x(u):
                dve.wait_ge(s_xh, u + 1)
                dve.tensor_tensor(xT[1][:, :, :], x1T[:, :, u * NT:u * NT + NT], xT[0][:, :, :].bitcast(F32),
                                  ALU.subtract).then_inc(s_xl, 1)

            def final(u):
                dve.wait_ge(s_y, (u + 1) * PAIRS)
                dve.wait_ge(s_wl, 2 * PAIRS)
                for q in range(u * QU, u * QU + QU):
                    dve.scalar_tensor_tensor(out=fin[:, q, :], in0=yb[q % 4][:, :], scalar=wsel[:, q:q + 1],
                                             in1=rest[:, q, :], op0=ALU.mult, op1=ALU.add).then_inc(s_f, 1)

            low_x(0)
            low(0)
            low(1)
            for n in range(U * PAIRS):
                for e in (2, 3):
                    if 2 * n + e < 2 * PAIRS:
                        low(2 * n + e)
                if n % PAIRS == PAIRS - 1 and n + 1 < U * PAIRS:
                    low_x(n // PAIRS + 1)
                dve.wait_ge(s_g, n + 1)
                if n >= 4:
                    dve.wait_ge(s_y, n - 3)
                g = gelu[:, n % 2, :].rearrange("p (e t) -> p e t", e=2)
                dve.tensor_copy(gT[0][:, n % 4, :, :], g).then_inc(s_gh, 1)
                dve.wait_ge(s_gh, n + 1)
                dve.tensor_tensor(gT[1][:, n % 4, :, :], g, gT[0][:, n % 4, :, :].bitcast(F32),
                                  ALU.subtract).then_inc(s_gl, 1)
                if n % PAIRS == 1 and n > PAIRS:
                    final(n // PAIRS - 1)
            final(U - 1)

        @block.gpsimd
        def _(pool):
            for q in range(Q):
                pool.wait_ge(s_f, q + 1)
                n = P if q < Q - 1 else P - 1
                pool.indirect_dma_start(out, bass.IndirectOffsetOnAxis(ap=idx[0:n, q:q + 1], axis=0),
                                        fin[0:n, q, :], None, compute_op=ALU.add).then_inc(s_o, 16)
            pool.wait_ge(s_o, 16 * Q)


def build(nc, x, wqT, wkT, wvT, woT, beta, maskT, positions, router_w, router_b, wq, wk, wv, wo, w1, w2, ln1, ln2,
          out):
    T = x.shape[0]
    K = T // 8
    list_dram = nc.dram_tensor("chosen_list", [K, 1], U32, kind="Internal").ap()
    cols_dram = nc.dram_tensor("mask_columns", [maskT.shape[0], K], F32, kind="Internal").ap()
    with ExitStack() as ctx:
        w = ctx.enter_context(nc.sbuf_tensor("w", [P, T // P], F32))
        thr = ctx.enter_context(nc.sbuf_tensor("thr", [P, 1], F32))
        idx = ctx.enter_context(nc.sbuf_tensor("idx", [P, K // P], U32))
        infini_attention(nc, x, wqT, wkT, wvT, woT, beta, router_w, router_b, out, w)
        select_tokens(nc, w, thr, idx, K, list_dram)
        feed_forward(nc, x, maskT, positions, router_w, router_b, wq, wk, wv, wo, w1, w2, ln1, ln2, thr, idx, out,
                     cols_dram)


def kernel(**inputs):
    import numpy as _np
    import concourse.bacc as _bacc
    from concourse import mybir as _mybir
    from concourse.bass_utils import run_bass_kernel_spmd as _run

    def attn(name):
        return _np.asarray(inputs["L0_attn_" + name])

    def ffn(name):
        return _np.asarray(inputs["L0_ffn_" + name])

    arrays = {
        "x": attn("x")[0],
        "wqT": attn("W_q").T, "wkT": attn("W_k").T, "wvT": attn("W_v").T, "woT": attn("W_o").T,
        "beta": attn("beta_param")[None],
        "maskT": ffn("attention_mask")[0, 0].T, "positions": ffn("position_ids")[0][:, None],
        "router_w": ffn("router_w"), "router_b": ffn("router_b")[None],
        "wq": ffn("wq"), "wk": ffn("wk"), "wv": ffn("wv"), "wo": ffn("wo"), "w1": ffn("w1"), "w2": ffn("w2"),
        "ln1": ffn("ln1")[None], "ln2": ffn("ln2")[None],
    }
    arrays = {"in_" + k: _np.ascontiguousarray(v) for k, v in arrays.items()}
    nc = _bacc.Bacc("TRN2", target_bir_lowering=False, num_devices=1)
    args = [nc.dram_tensor(k, v.shape, _mybir.dt.from_np(v.dtype), kind="ExternalInput").ap()
            for k, v in arrays.items()]
    rows = arrays["in_x"].shape
    args.append(nc.dram_tensor("out_rows", rows, F32, kind="ExternalOutput").ap())
    build(nc, *args)
    r = _run(nc, [arrays], core_ids=[0])
    return r.results[0]["out_rows"][None]
```
